# Optimizing a Trainium2 kernel written in Bass

```python
import numpy as np
import jax
import jax.numpy as jnp

def _softmax(x, axis=-1):
    return jax.nn.softmax(x, axis=axis)

def _gelu(x):
    return jax.nn.gelu(x, approximate=True)

def _silu(x):
    return jax.nn.silu(x)

def _sigmoid(x):
    return jax.nn.sigmoid(x)

def _layernorm(x, axis=-1, eps=1e-05):
    m = jnp.mean(x, axis=axis, keepdims=True)
    v = jnp.var(x, axis=axis, keepdims=True)
    return (x - m) / jnp.sqrt(v + eps)

def _scatter_add(tgt, idx, src, axis=0):
    return tgt.at[idx].add(src)

def _segment_sum(src, seg, n):
    return jax.ops.segment_sum(src, seg, n)
kernel_name = 'mk_recurrent_d2_jaxref_r8_622134'

def setup_inputs(seed: int=0):
    np.random.seed(seed)
    _w = jnp.asarray

    def _L0_attn_setup():
        import jax, jax.numpy as jnp
        import numpy as np
        import math
        D_MODEL = 256
        D_STATE = 32
        R_MIN = 0.0
        R_MAX = 0.9
        MAX_PHASE = 6.283185307179586
        B_SZ = 4
        T_LEN = 256
        key = jax.random.key(seed)
        k_x, k_bre, k_bim, k_cre, k_cim = jax.random.split(key, 5)
        x = jax.random.normal(k_x, (B_SZ, T_LEN, D_MODEL), dtype=jnp.float32)
        u = np.linspace(0.0, 1.0, D_STATE, dtype=np.float64)
        mag_init = np.clip(R_MIN + (R_MAX - R_MIN) * u, 1e-06, 1.0 - 1e-06)
        nu_init = -np.log(mag_init)
        nu_log = jnp.asarray(np.log(np.clip(np.expm1(nu_init), 1e-06, None)), dtype=jnp.float32)
        theta_log = jnp.asarray(np.linspace(math.log(0.0001), math.log(MAX_PHASE), D_STATE), dtype=jnp.float32)
        B_re = jax.random.normal(k_bre, (D_STATE, D_MODEL), dtype=jnp.float32) / math.sqrt(D_MODEL)
        B_im = jax.random.normal(k_bim, (D_STATE, D_MODEL), dtype=jnp.float32) / math.sqrt(D_MODEL)
        C_re = jax.random.normal(k_cre, (D_MODEL, D_STATE), dtype=jnp.float32) / math.sqrt(D_STATE)
        C_im = jax.random.normal(k_cim, (D_MODEL, D_STATE), dtype=jnp.float32) / math.sqrt(D_STATE)
        D = jnp.ones((D_MODEL,), dtype=jnp.float32)
        return {'x': x, 'nu_log': nu_log, 'theta_log': theta_log, 'B_re': B_re, 'B_im': B_im, 'C_re': C_re, 'C_im': C_im, 'D': D}
    _L0_attn_in = _L0_attn_setup()

    def _L0_ffn_setup():
        import jax, jax.numpy as jnp
        import numpy as np
        L, N, E, H, K = (256, 8, 256, 1024, 8)
        key = jax.random.key(seed)
        ks = jax.random.split(key, 6)
        return {'x': jax.random.normal(ks[0], (L, N, E), dtype=jnp.float32), 'proj1': jax.random.normal(ks[1], (H, E), dtype=jnp.float32) * 0.02, 'proj1_bias': jax.random.normal(ks[2], (H,), dtype=jnp.float32) * 0.02, 'proj2': jax.random.normal(ks[3], (E, H), dtype=jnp.float32) * 0.02, 'proj2_bias': jax.random.normal(ks[4], (E,), dtype=jnp.float32) * 0.02, 'gate_w': jax.random.normal(ks[5], (E, K), dtype=jnp.float32)}
    _L0_ffn_in = _L0_ffn_setup()

    def _L1_attn_setup():
        import jax, jax.numpy as jnp
        import numpy as np
        D_MODEL = 256
        N_HEADS = 16
        QK_ROPE = 64
        QK_NOPE = 128
        KV_LORA = 64
        V_DIM = 128
        QK_DIM = QK_ROPE + QK_NOPE
        RMS_EPS = 1.1920928955078125e-07

        def apply_rope(x, base=10000.0):
            B, S, H, D = x.shape
            freqs = 1.0 / base ** (jnp.arange(0, D, 2, dtype=jnp.float32) / D)
            t = jnp.arange(S, dtype=jnp.float32)[:, None] * freqs[None, :]
            cos = jnp.cos(t)[None, :, None, :]
            sin = jnp.sin(t)[None, :, None, :]
            x1 = x[..., 0::2]
            x2 = x[..., 1::2]
            out = jnp.stack([x1 * cos - x2 * sin, x2 * cos + x1 * sin], axis=-1)
            return out.reshape(B, S, H, D).astype(x.dtype)
        key = jax.random.key(seed)
        ks = jax.random.split(key, 6)
        s = lambda fan_in: 1.0 / np.sqrt(fan_in)
        x = jax.random.normal(ks[0], (2, 256, D_MODEL), dtype=jnp.float32)
        Wq = jax.random.normal(ks[1], (D_MODEL, N_HEADS * QK_DIM), dtype=jnp.float32) * s(D_MODEL)
        Wkv_a = jax.random.normal(ks[2], (D_MODEL, KV_LORA + QK_ROPE), dtype=jnp.float32) * s(D_MODEL)
        kv_norm_w = jnp.ones((KV_LORA,), dtype=jnp.float32)
        Wkv_b = jax.random.normal(ks[3], (KV_LORA, N_HEADS * (QK_NOPE + V_DIM)), dtype=jnp.float32) * s(KV_LORA)
        Wo = jax.random.normal(ks[4], (N_HEADS * V_DIM, D_MODEL), dtype=jnp.float32) * s(N_HEADS * V_DIM)
        return {'x': x, 'Wq': Wq, 'Wkv_a': Wkv_a, 'kv_norm_w': kv_norm_w, 'Wkv_b': Wkv_b, 'Wo': Wo}
    _L1_attn_in = _L1_attn_setup()

    def _L1_ffn_setup():
        import jax, jax.numpy as jnp
        import numpy as np
        B, S, D_IN, D_OUT, E, R = (4, 256, 256, 256, 8, 16)
        SCALING = 32.0 / 16.0
        key = jax.random.key(seed)
        ks = jax.random.split(key, 7)
        return {'x': jax.random.normal(ks[0], (B, S, D_IN), jnp.float32), 'base_w': jax.random.normal(ks[1], (D_OUT, D_IN), jnp.float32) * 0.02, 'base_b': jax.random.normal(ks[2], (D_OUT,), jnp.float32) * 0.02, 'router_w': jax.random.normal(ks[3], (E, D_IN), jnp.float32) * 0.02, 'router_b': jax.random.normal(ks[4], (E,), jnp.float32) * 0.02, 'lora_A': jax.random.normal(ks[5], (E, D_IN, R), jnp.float32) * 0.02, 'lora_B': jax.random.normal(ks[6], (E, R, D_OUT), jnp.float32) * 0.02}
    _L1_ffn_in = _L1_ffn_setup()
    _d = {'L0_attn_x': _L0_attn_in['x'], 'L0_attn_nu_log': _L0_attn_in['nu_log'], 'L0_attn_theta_log': _L0_attn_in['theta_log'], 'L0_attn_B_re': _L0_attn_in['B_re'], 'L0_attn_B_im': _L0_attn_in['B_im'], 'L0_attn_C_re': _L0_attn_in['C_re'], 'L0_attn_C_im': _L0_attn_in['C_im'], 'L0_attn_D': _L0_attn_in['D'], 'L0_ffn_proj1': _L0_ffn_in['proj1'], 'L0_ffn_proj1_bias': _L0_ffn_in['proj1_bias'], 'L0_ffn_proj2': _L0_ffn_in['proj2'], 'L0_ffn_proj2_bias': _L0_ffn_in['proj2_bias'], 'L0_ffn_gate_w': _L0_ffn_in['gate_w'], 'L1_attn_Wq': _L1_attn_in['Wq'], 'L1_attn_Wkv_a': _L1_attn_in['Wkv_a'], 'L1_attn_kv_norm_w': _L1_attn_in['kv_norm_w'], 'L1_attn_Wkv_b': _L1_attn_in['Wkv_b'], 'L1_attn_Wo': _L1_attn_in['Wo'], 'L1_ffn_base_w': _L1_ffn_in['base_w'], 'L1_ffn_base_b': _L1_ffn_in['base_b'], 'L1_ffn_router_w': _L1_ffn_in['router_w'], 'L1_ffn_router_b': _L1_ffn_in['router_b'], 'L1_ffn_lora_A': _L1_ffn_in['lora_A'], 'L1_ffn_lora_B': _L1_ffn_in['lora_B']}
    _x0 = _d['L0_attn_x']
    _d['L0_attn_x'] = jax.random.normal(jax.random.fold_in(jax.random.key(seed), 1), (16, 256, 256), dtype=_x0.dtype)
    del _x0
    return _d

def reference(L0_attn_x, L0_attn_nu_log, L0_attn_theta_log, L0_attn_B_re, L0_attn_B_im, L0_attn_C_re, L0_attn_C_im, L0_attn_D, L0_ffn_proj1, L0_ffn_proj1_bias, L0_ffn_proj2, L0_ffn_proj2_bias, L0_ffn_gate_w, L1_attn_Wq, L1_attn_Wkv_a, L1_attn_kv_norm_w, L1_attn_Wkv_b, L1_attn_Wo, L1_ffn_base_w, L1_ffn_base_b, L1_ffn_router_w, L1_ffn_router_b, L1_ffn_lora_A, L1_ffn_lora_B):

    def _L0_attn_ref(x, nu_log, theta_log, B_re, B_im, C_re, C_im, D):
        import jax, jax.numpy as jnp
        import numpy as np
        import math
        D_MODEL = 256
        D_STATE = 32
        R_MIN = 0.0
        R_MAX = 0.9
        MAX_PHASE = 6.283185307179586
        B_SZ = 4
        T_LEN = 256
        nu = jax.nn.softplus(nu_log)
        mag = jnp.exp(-jnp.exp(nu))
        theta = jnp.exp(theta_log)
        A_re = mag * jnp.cos(theta)
        A_im = mag * jnp.sin(theta)
        gamma = jnp.sqrt(jnp.clip(1.0 - mag * mag, 0.0))
        gB_re = gamma[:, None] * B_re
        gB_im = gamma[:, None] * B_im
        Bu_re = jnp.einsum('btd,nd->btn', x, gB_re)
        Bu_im = jnp.einsum('btd,nd->btn', x, gB_im)

        def step(h, bu):
            h_re, h_im = h
            bu_re, bu_im = bu
            new_re = A_re * h_re - A_im * h_im + bu_re
            new_im = A_re * h_im + A_im * h_re + bu_im
            return ((new_re, new_im), (new_re, new_im))
        Bsz = x.shape[0]
        h0 = jnp.zeros((Bsz, A_re.shape[0]), dtype=x.dtype)
        _, (H_re, H_im) = jax.lax.scan(step, (h0, h0), (jnp.swapaxes(Bu_re, 0, 1), jnp.swapaxes(Bu_im, 0, 1)))
        H_re = jnp.swapaxes(H_re, 0, 1)
        H_im = jnp.swapaxes(H_im, 0, 1)
        y = jnp.einsum('btn,dn->btd', H_re, C_re) - jnp.einsum('btn,dn->btd', H_im, C_im) + D * x
        return y

    def _L0_ffn_ref(x, proj1, proj1_bias, proj2, proj2_bias, gate_w):
        import jax, jax.numpy as jnp
        import numpy as np
        L, N, E, H, K = (256, 8, 256, 1024, 8)
        dst = jnp.argmax(jnp.einsum('lne,ek->lnk', x, gate_w), axis=-1)
        h = jax.nn.gelu(jnp.einsum('lne,he->lnh', x, proj1) + proj1_bias, approximate=False)
        out = jnp.einsum('lnh,eh->lne', h, proj2) + proj2_bias
        del dst
        return out

    def _L1_attn_ref(x, Wq, Wkv_a, kv_norm_w, Wkv_b, Wo):
        import jax, jax.numpy as jnp
        import numpy as np
        D_MODEL = 256
        N_HEADS = 16
        QK_ROPE = 64
        QK_NOPE = 128
        KV_LORA = 64
        V_DIM = 128
        QK_DIM = QK_ROPE + QK_NOPE
        RMS_EPS = 1.1920928955078125e-07

        def apply_rope(x, base=10000.0):
            B, S, H, D = x.shape
            freqs = 1.0 / base ** (jnp.arange(0, D, 2, dtype=jnp.float32) / D)
            t = jnp.arange(S, dtype=jnp.float32)[:, None] * freqs[None, :]
            cos = jnp.cos(t)[None, :, None, :]
            sin = jnp.sin(t)[None, :, None, :]
            x1 = x[..., 0::2]
            x2 = x[..., 1::2]
            out = jnp.stack([x1 * cos - x2 * sin, x2 * cos + x1 * sin], axis=-1)
            return out.reshape(B, S, H, D).astype(x.dtype)
        B, S, _ = x.shape
        q = (x @ Wq).reshape(B, S, N_HEADS, QK_DIM)
        q_nope, q_rope = (q[..., :QK_NOPE], q[..., QK_NOPE:])
        q = jnp.concatenate([q_nope, apply_rope(q_rope)], axis=-1)
        kv = x @ Wkv_a
        c_kv, k_rope = (kv[..., :KV_LORA], kv[..., KV_LORA:])
        k_rope = apply_rope(k_rope.reshape(B, S, 1, QK_ROPE))
        c_kv = c_kv * jax.lax.rsqrt(jnp.mean(c_kv * c_kv, axis=-1, keepdims=True) + RMS_EPS) * kv_norm_w
        kv = (c_kv @ Wkv_b).reshape(B, S, N_HEADS, QK_NOPE + V_DIM)
        k_nope, v = (kv[..., :QK_NOPE], kv[..., QK_NOPE:])
        k = jnp.concatenate([k_nope, jnp.broadcast_to(k_rope, (B, S, N_HEADS, QK_ROPE))], axis=-1)
        scale = 1.0 / np.sqrt(QK_DIM)
        scores = jnp.einsum('bqhd,bkhd->bhqk', q, k) * scale
        mask = jnp.tril(jnp.ones((S, S), dtype=bool))
        scores = jnp.where(mask, scores, jnp.finfo(scores.dtype).min)
        attn = jax.nn.softmax(scores, axis=-1)
        out = jnp.einsum('bhqk,bkhd->bqhd', attn, v).reshape(B, S, N_HEADS * V_DIM)
        return out @ Wo

    def _L1_ffn_ref(x, base_w, base_b, router_w, router_b, lora_A, lora_B):
        import jax, jax.numpy as jnp
        import numpy as np
        B, S, D_IN, D_OUT, E, R = (4, 256, 256, 256, 8, 16)
        SCALING = 32.0 / 16.0
        b, s, d_in = x.shape
        n = b * s
        e = lora_A.shape[0]
        d_out = lora_B.shape[-1]
        result = jnp.einsum('bsd,od->bso', x, base_w) + base_b
        logits = jnp.einsum('bsd,ed->bse', x, router_w) + router_b
        probs = jax.nn.softmax(logits.astype(jnp.float32), axis=-1)
        top_vals, top_idx = jax.lax.top_k(probs, 2)
        top_vals = top_vals / jnp.sum(top_vals, axis=-1, keepdims=True)
        top_vals = top_vals.astype(x.dtype)
        flat_idx = top_idx.reshape(n, 2)
        flat_val = top_vals.reshape(n, 2)
        gate = jnp.zeros((n, e), x.dtype).at[jnp.arange(n)[:, None], flat_idx].set(flat_val)
        xf = x.reshape(n, d_in)
        mid = jnp.einsum('nd,edr->ner', xf, lora_A)
        mid = mid * gate[:, :, None]
        lora_out = jnp.einsum('ner,erd->nd', mid, lora_B)
        return result + SCALING * lora_out.reshape(b, s, d_out)
    x = L0_attn_x
    xn = _layernorm(x, axis=-1)
    s = _L0_attn_ref(xn, L0_attn_nu_log, L0_attn_theta_log, L0_attn_B_re, L0_attn_B_im, L0_attn_C_re, L0_attn_C_im, L0_attn_D)
    g = _silu(_L0_ffn_ref(xn, L0_ffn_proj1, L0_ffn_proj1_bias, L0_ffn_proj2, L0_ffn_proj2_bias, L0_ffn_gate_w))
    x = x + s * g
    xn = _layernorm(x, axis=-1)
    s = _L1_attn_ref(xn, L1_attn_Wq, L1_attn_Wkv_a, L1_attn_kv_norm_w, L1_attn_Wkv_b, L1_attn_Wo)
    g = _silu(_L1_ffn_ref(xn, L1_ffn_base_w, L1_ffn_base_b, L1_ffn_router_w, L1_ffn_router_b, L1_ffn_lora_A, L1_ffn_lora_B))
    x = x + s * g
    return x

_drawn_inputs = setup_inputs


def setup_inputs(seed=0):
    import zlib

    import numpy as np

    out = dict(_drawn_inputs(seed))
    spreads = {'L0_attn_D': (1.0, 0.6), 'L1_attn_kv_norm_w': (1.0, 0.6)}
    factors = {'L0_attn_nu_log': 4.553,
     'L0_attn_theta_log': 4.698,
     'L0_ffn_proj1_bias': 8.0,
     'L0_ffn_proj2_bias': 3.25,
     'L1_ffn_base_b': 8.0,
     'L1_ffn_router_w': 8.0,
     'L1_ffn_router_b': 8.0,
     'L1_ffn_lora_A': 8.0,
     'L1_ffn_lora_B': 8.0}
    for name, (base, spread) in spreads.items():
        noise = np.random.default_rng([zlib.crc32(name.encode()), seed]).standard_normal(out[name].shape)
        drawn = base * np.exp(spread * noise) if base else spread * noise
        out[name] = jnp.asarray(drawn.astype(out[name].dtype))
    for name, factor in factors.items():
        out[name] = (out[name] * factor).astype(out[name].dtype)
    return out
```

```python
from contextlib import ExitStack

import numpy as np

import concourse.bass as bass
from concourse import mybir

F32 = mybir.dt.float32
F32R = mybir.dt.float32r
I32 = mybir.dt.int32
ALU = mybir.AluOpType
ACT = mybir.ActivationFunctionType
AX = mybir.AxisListType

NB = 16
T = 256
D = 256
NH = 16
NT = NB * T // 128
NC = NB // 2
LN_EPS = 1e-5
RMS_EPS = 1.1920928955078125e-07
SCALE = 1.0 / float(np.sqrt(192))
BIG = 1e30
OFF_D, OFF_B2, OFF_BB, OFF_RB, OFF_KW, OFF_END = 0, 256, 512, 768, 776, 840


class Program:

    def __init__(self, nc, ctx):
        self.nc = nc
        self.ctx = ctx
        self.queue = {k: [] for k in "TVSGD"}
        self.count = {}
        self.sems = {}

    def put(self, engine, name, waits, *instructions):
        step = 16 if engine == "D" else 1
        key = f"{name}_{engine}"
        if key not in self.sems:
            self.sems[key] = self.ctx.enter_context(self.nc.semaphore(key))
            self.count[key] = 0
        self.count[key] += step
        self.queue[engine].append((list(waits), instructions, key, step))
        return key, self.count[key]

    def run(self, engine, e):
        seen = {}
        for waits, instructions, key, step in self.queue[engine]:
            for k, v in waits:
                if seen.get(k, 0) < v:
                    e.wait_ge(self.sems[k], v)
                    seen[k] = v
            for make in instructions:
                last = make(e)
            last.then_inc(self.sems[key], step)


class Ring:

    def __init__(self, buffers):
        self.buffers = buffers
        self.readers = [[] for _ in buffers]
        self.n = 0

    def take(self):
        i = self.n % len(self.buffers)
        self.n += 1
        assert self.readers[i] is not None, "taken again before its readers were named"
        r, self.readers[i] = self.readers[i], None
        return i, self.buffers[i], r

    def free(self, i, *readers):
        self.readers[i] = list(readers)


class Turns:

    def __init__(self, count, first):
        self.count = count
        self.first = first
        self.named = {}

    def readers(self, n):
        return self.first if n < self.count else self.named[n - self.count]

    def free(self, n, *readers):
        self.named[n] = list(readers)


def build(nc, x, consts, vecs, w1t, w2t, b1c, bt, ct, nuth, wqn, wkbt, wqr, wkva, wvbt, wo,
          baset, lorab, loraa, routert, out):
    ctx = ExitStack()
    with ctx:
        p = Program(nc, ctx)
        put = p.put

        def sb(name, shape, dt=F32, where=ctx):
            return where.enter_context(nc.sbuf_tensor(name, shape, dt))

        X = sb("X", [128, NT, D])
        CONST = sb("CONST", [128, 128 + 256 + 128 + 2])
        ident = CONST[:, 0:128]
        mask0 = CONST[:, 256:384]
        mask1 = CONST[:, 128:384]
        cosT = [CONST[:, 384 + 32 * q:384 + 32 * q + 32] for q in range(2)]
        sinT = [CONST[:, 448 + 32 * q:448 + 32 * q + 32] for q in range(2)]
        sgn = CONST[:, 512:513]
        sgnc = CONST[:, 513:514]
        VEC = sb("VEC", [128, OFF_END])
        rope_c = sb("rope_c", [128, 2, 2, 32])
        rope_s = sb("rope_s", [128, 2, 2, 32])
        wq_hi = sb("wq_hi", [128, 2, NH, 128], F32R)
        wq_lo = sb("wq_lo", [128, 2, NH, 128], F32R)
        wm_hi = sb("wm_hi", [128, 2, 520], F32R)
        wm_lo = sb("wm_lo", [128, 2, 520], F32R)
        woe = sb("woe", [128, 8, D])
        LB = sb("LB", [128, D])

        l0 = ExitStack()
        stage = [sb(f"stage{i}", [128, 2048], F32, l0) for i in range(3)]
        stk = sb("stk", [128, 2, 512], F32, l0)
        w1h = sb("w1h", [128, 2, 1024], F32R, l0)
        w1l = sb("w1l", [128, 2, 1024], F32R, l0)
        w2h = sb("w2h", [128, 8, D], F32R, l0)
        w2l = sb("w2l", [128, 8, D], F32R, l0)
        bh = sb("bh", [128, 2, 128], F32R, l0)
        bl = sb("bl", [128, 2, 128], F32R, l0)
        B1 = sb("B1", [128, 8], F32, l0)
        RR = sb("RR", [128, D], F32, l0)
        xn = [sb(f"xn{i}", [128, 4, D], F32, l0) for i in range(2)]
        xh = [sb(f"xh{i}", [128, 2, 512], F32R, l0) for i in range(2)]
        xl = [sb(f"xl{i}", [128, 2, 512], F32R, l0) for i in range(2)]
        hs = [sb(f"hs{i}", [128, 512], F32, l0) for i in range(2)]
        hh = [sb(f"hh{i}", [128, 512], F32R, l0) for i in range(3)]
        hl = [sb(f"hl{i}", [128, 512], F32R, l0) for i in range(3)]
        tc = sb("tc", [128, T], F32, l0)
        tsn = sb("tsn", [128, T], F32, l0)
        tci = sb("tci", [128, T], F32, l0)
        tsi = sb("tsi", [128, T], F32, l0)
        g1 = sb("g1", [128, T], F32, l0)
        g2 = sb("g2", [128, T], F32, l0)
        gs = sb("gs", [128, T], F32, l0)
        Z = [sb(f"Z{i}", [128, T], F32, l0) for i in range(2)]
        z0 = sb("z0", [128, 4, D], F32, l0)
        th0 = sb("th0", [128, 2, D], F32, l0)
        par = sb("par", [128, 64], F32, l0)
        pari = sb("pari", [128, 4], I32, l0)
        st0 = sb("st0", [128, 4, 6], F32, l0)
        mv0 = sb("mv0", [128, 4, 2], F32, l0)
        rs0 = sb("rs0", [128, 5, 4], F32, l0)
        ri0 = sb("ri0", [128, 4], I32, l0)
        l0.close()

        l1 = ExitStack()
        QT = [sb(f"QT{i}", [128, 2, NH, 128], F32, l1) for i in range(2)]
        QK = [sb(f"QK{i}", [128, 4, 128], F32, l1) for i in range(3)]
        q1b = [sb(f"q1b{i}", [128, 4, 2, 32], F32, l1) for i in range(3)]
        q2b = [sb(f"q2b{i}", [128, 4, 2, 32], F32, l1) for i in range(3)]
        SM = [sb(f"SM{i}", [128, 512], F32, l1) for i in range(3)]
        PP = [sb(f"PP{i}", [128, 512], F32, l1) for i in range(4)]
        PT = [sb(f"PT{i}", [128, 512], F32, l1) for i in range(4)]
        st_b = [sb(f"stb{i}", [128, 3, 4], F32, l1) for i in range(4)]
        oT = [sb(f"oT{i}", [128, 2, 512], F32, l1) for i in range(2)]
        yn = [sb(f"yn{i}", [128, 2, D], F32, l1) for i in range(2)]
        yh = [sb(f"yh{i}", [128, 2, T], F32R, l1) for i in range(2)]
        yl = [sb(f"yl{i}", [128, 2, T], F32R, l1) for i in range(2)]
        KV = [sb(f"KV{i}", [128, 2, 128], F32, l1) for i in range(3)]
        KT = [sb(f"KT{i}", [128, T], F32, l1) for i in range(2)]
        ML = sb("ML", [128, 2, 264], F32, l1)
        MT = sb("MT", [128, 2, 128], F32, l1)
        kr = sb("kr", [128, 4, 2, 2, 32], F32, l1)
        sq = sb("sq", [128, 2, 64], F32, l1)
        lg = sb("lg", [128, 12, 2, 8], F32, l1)
        lv = sb("lv", [128, 10, 2], F32, l1)
        st1 = sb("st1", [128, 2, 6], F32, l1)
        mv1 = sb("mv1", [128, 2, 2], F32, l1)
        rs1 = sb("rs1", [128, 5, 2], F32, l1)
        rs2 = sb("rs2", [128, 5, 2], F32, l1)
        ri1 = sb("ri1", [128, 2], I32, l1)
        ri2 = sb("ri2", [128, 2], I32, l1)
        z1 = [sb(f"z1{i}", [128, 2, D], F32, l1) for i in range(2)]
        th1 = [sb(f"th1{i}", [128, 2, D], F32, l1) for i in range(2)]
        w1b = [sb(f"w1b{i}", [128, 2, D], F32, l1) for i in range(2)]
        fo = [sb(f"fo{i}", [128, D], F32, l1) for i in range(2)]
        pr = [sb(f"pr{i}", [128, D], F32, l1) for i in range(2)]
        l1.close()

        bank = [ctx.enter_context(nc.psum_tensor(f"bank{i}", [128, 512], F32)) for i in range(8)]

        def load(name, dst, src, waits=()):
            return put("D", name, waits, lambda e: e.dma_start(dst, src))

        d_x = [None] * NC

        def load_x(c):
            d_x[c] = load(f"x{c}", X[:, 4 * c:4 * c + 4, :].rearrange("p a b -> p (a b)"),
                          x[:, 4 * c * D:(4 * c + 4) * D])

        load_x(0)
        d_const = load("const", CONST[:, :], consts)
        d_nuth = load("nuth", par[:, 0:2], nuth)
        d_w1 = load("w1", stage[0][:, :], w1t)
        d_bt = load("bt", stk[:, 0, 0:256], bt)
        d_b1 = load("b1", B1[:, :], b1c)
        d_vec = load("vec", VEC[:, :], vecs)
        d_ct = load("ct", RR[:, :], ct)
        d_w2 = load("w2", stage[1][:, :], w2t)
        load_x(1)
        d_wqr = load("wqr", stage[2][:, :], wqr)
        for c in range(2, NC):
            load_x(c)

        def split(waits, src, hi, lo, name):
            a = put("S", name + "h", waits, lambda e: e.activation(hi, src, ACT.Copy))
            b = put("V", name + "l", [*waits, a],
                    lambda e: e.tensor_tensor(lo, src, hi.bitcast(F32), ALU.subtract))
            return a, b

        def rsqrt(waits, v, eps, k, name, t, ti):
            half, y, a = t[:, 0, :], t[:, 4, :], t[:, 1, :]
            c = put("V", name, waits, lambda e: e.tensor_scalar(half, v, eps, None, ALU.add))
            c = put("V", name, [c], lambda e: e.tensor_scalar(
                ti, half.bitcast(I32), -0.5, 1597463007.0, ALU.mult, ALU.add))
            src = ti.bitcast(F32)
            for n in range(4):
                dst = y if n == 3 else t[:, 2 + n % 2, :]
                c = put("V", name, [c], lambda e, s=src: e.tensor_tensor(a, s, s, ALU.mult))
                c = put("V", name, [c], lambda e: e.tensor_tensor(a, a, half, ALU.mult))
                c = put("V", name, [c], lambda e: e.tensor_scalar(a, a, -0.5, 1.5, ALU.mult, ALU.add))
                c = put("V", name, [c], lambda e, s=src, d=dst: e.tensor_tensor(d, s, a, ALU.mult))
                src = dst
            return c

        def col(i, n=1):
            return par[:, i:i + n]

        def vp(c, f):
            return put("V", "par", c, f)

        def ts(dst, src, a, b, o1, o2=ALU.bypass):
            return lambda e: e.tensor_scalar(dst, src, a, b, o1, o2)

        def tt(dst, a, b, o):
            return lambda e: e.tensor_tensor(dst, a, b, o)

        MAGIC = 12582912.0
        LN2_HI, LN2_LO = 0.693145751953125, 1.42860682030941723212e-6
        INV_LN2 = 1.4426950408889634

        def exact_exp(c, src, dst, n, base):
            k, r, q, w = (col(base + n * i, n) for i in range(4))
            c = vp([*c], ts(r, src, -87.0, 88.0, ALU.max, ALU.min))
            c = vp([c], ts(k, r, INV_LN2, MAGIC, ALU.mult, ALU.add))
            c = vp([c], ts(k, k, MAGIC, None, ALU.subtract))
            c = vp([c], ts(w, k, LN2_HI, None, ALU.mult))
            c = vp([c], tt(r, r, w, ALU.subtract))
            c = vp([c], ts(w, k, LN2_LO, None, ALU.mult))
            c = vp([c], tt(r, r, w, ALU.subtract))
            c = vp([c], ts(q, r, 1.0 / 5040, 1.0 / 720, ALU.mult, ALU.add))
            for f in (1.0 / 120, 1.0 / 24, 1.0 / 6, 0.5, 1.0, 1.0):
                c = vp([c], tt(q, q, r, ALU.mult))
                c = vp([c], ts(q, q, f, None, ALU.add))
            c = vp([c], ts(pari[:, 0:n], k, 8388608.0, 1065353216.0, ALU.mult, ALU.add))
            return vp([c], tt(dst, q, pari[:, 0:n].bitcast(F32), ALU.mult))

        nu, en, theta = col(0), col(2), col(3)
        c = exact_exp([d_nuth], col(0, 2), col(2, 2), 2, 8)
        c = vp([c], ts(col(4), en, 1.0, -1.0, ALU.add, ALU.mult))
        c = exact_exp([c], col(4), col(5), 1, 8)
        mag = col(5)
        c = vp([c], ts(col(7), col(4), -87.0, None, ALU.is_gt))
        c = vp([c], tt(mag, mag, col(7), ALU.mult))
        c = vp([c], tt(col(6), mag, mag, ALU.mult))
        c = vp([c], ts(col(6), col(6), -1.0, 1.0, ALU.mult, ALU.add))
        gt = par[:, 16:21].unsqueeze(2)
        c = rsqrt([c], col(6), 0.0, 1, "par", gt, pari[:, 0:1])
        c = vp([c], tt(col(6), col(6), par[:, 20:21], ALU.mult))
        gamma = col(6)
        c = vp([c], ts(col(24), theta, 0.15915494309189535, MAGIC, ALU.mult, ALU.add))
        c = vp([c], ts(col(24), col(24), MAGIC, None, ALU.subtract))
        c = vp([c], ts(col(25), theta, 0.0, None, ALU.add))
        for part in (6.28125, 0.0019340515136718750, 1.2556659146932927e-06):
            c = vp([c], ts(col(26), col(24), part, None, ALU.mult))
            c = vp([c], tt(col(25), col(25), col(26), ALU.subtract))
        PI = 3.1415925
        c = vp([c], ts(col(25), col(25), PI, -PI, ALU.min, ALU.max))
        c = vp([c], ts(col(26), col(25), -1.0, None, ALU.mult))
        c = vp([c], tt(col(26), col(25), col(26), ALU.max))
        c = vp([c], ts(col(26), col(26), -1.0, 1.5707963267948966, ALU.mult, ALU.add))
        c = put("S", "sin", [c], lambda e: e.activation(col(27, 2), col(25, 2), ACT.Sin))
        ps, pc = col(27), col(28)

        def unit(c, s, co):
            c = vp([c], tt(col(30), s, s, ALU.mult))
            c = vp([c], tt(col(31), co, co, ALU.mult))
            c = vp([c], tt(col(30), col(30), col(31), ALU.add))
            c = vp([c], ts(col(30), col(30), -0.5, 1.5, ALU.mult, ALU.add))
            c = vp([c], tt(s, s, col(30), ALU.mult))
            return vp([c], tt(co, co, col(30), ALU.mult))

        c = unit(c, ps, pc)
        c = vp([c], lambda e: e.memset(tc[:, 0:1], 1.0))
        c = vp([c], lambda e: e.memset(tsn[:, 0:1], 0.0))
        n = 1
        while n < T:
            def cmul(c, dst, a, sa, b, sb_, sub):
                c = vp([c], lambda e: e.tensor_scalar(g1[:, 0:n], b, sb_, None, ALU.mult))
                return vp([c], lambda e: e.scalar_tensor_tensor(
                    dst, a, sa, g1[:, 0:n], ALU.mult, ALU.subtract if sub else ALU.add))
            def grow(c, n=n, ps=ps, pc=pc):
                c = vp([c], lambda e: e.tensor_scalar(g1[:, 0:n], tsn[:, 0:n], ps, None, ALU.mult))
                c = vp([c], lambda e: e.scalar_tensor_tensor(tc[:, n:2 * n], tc[:, 0:n], pc, g1[:, 0:n],
                                                             ALU.mult, ALU.subtract))
                c = vp([c], lambda e: e.tensor_scalar(g1[:, 0:n], tc[:, 0:n], ps, None, ALU.mult))
                return vp([c], lambda e: e.scalar_tensor_tensor(tsn[:, n:2 * n], tsn[:, 0:n], pc,
                                                                g1[:, 0:n], ALU.mult, ALU.add))
            c = grow(c)
            n *= 2
            if n < T:
                i = 32 + 2 * (n.bit_length() % 8)
                ns, nc_ = col(i), col(i + 1)
                c = vp([c], tt(ns, ps, pc, ALU.mult))
                c = vp([c], ts(ns, ns, 2.0, None, ALU.mult))
                c = vp([c], tt(nc_, ps, ps, ALU.mult))
                c = vp([c], ts(nc_, nc_, -2.0, 1.0, ALU.mult, ALU.add))
                c = unit(c, ns, nc_)
                ps, pc = ns, nc_
        c = vp([c], lambda e: e.tensor_scalar(tci[:, :], tc[:, :], gamma, None, ALU.mult))
        c = vp([c, d_const], lambda e: e.tensor_scalar(tsi[:, :], tsn[:, :], gamma, sgn, ALU.mult, ALU.mult))
        c = vp([c, d_ct], lambda e: e.tensor_scalar(RR[:, :], RR[:, :], sgnc, None, ALU.mult))
        k_tab = c

        st3 = stage[0][:, :].rearrange("p (k n) -> p k n", k=2)
        k_w1 = split([d_w1], st3, w1h[:, :, :], w1l[:, :, :], "w1s")
        k_b = split([d_bt], stk[:, 0, 0:256].rearrange("p (k n) -> p k n", k=2), bh[:, :, :], bl[:, :, :], "bs")
        st8 = stage[1][:, :].rearrange("p (k n) -> p k n", k=8)
        k_w2 = split([d_w2], st8, w2h[:, :, :], w2l[:, :, :], "w2s")

        tbank = Ring([bank[0]])
        fbank = Ring([bank[1], bank[2]])
        obank = [bank[3], bank[4]]
        ubank = Ring([bank[5]])
        ybank = Ring([bank[6]])
        wbank = Ring([bank[7]])
        xn_r = [[], []]
        xt_r = [[], []]
        k_xn = [None] * NC
        k_xt = [None] * NC
        turned = [None] * NC

        def l0_norm(c):
            q = c % 2
            w = [d_x[c]]
            a = put("V", "bn", w + ([k_xn[c - 1]] if c else []),
                    *[lambda e, i=i: e.bn_stats(st0[:, i, :], X[:, 4 * c + i, :]) for i in range(4)])
            a = put("V", "bn", [a], *[lambda e, i=i: e.bn_aggr(mv0[:, i, :], st0[:, i, :]) for i in range(4)])
            a = rsqrt([a], mv0[:, :, 1], LN_EPS, 4, "ln0", rs0, ri0[:, :])
            k_xn[c] = put("V", "xn", [a, *xn_r[q]], *[
                lambda e, i=i: e.tensor_scalar(xn[q][:, i, :], X[:, 4 * c + i, :], mv0[:, i, 0:1],
                                               rs0[:, 4, i:i + 1], ALU.subtract, ALU.mult)
                for i in range(4)])

        def l0_turn(c, k):
            q = c % 2
            i, bk, free = tbank.take()
            t = put("T", "tx", [k_xn[c], d_const, *free], *[
                lambda e, j=j: e.transpose(bk[:, 128 * j:128 * j + 128],
                                           xn[q][:, j, 128 * k:128 * k + 128], ident) for j in range(4)])
            h, l = split([t, *xt_r[q]], bk[:, :], xh[q][:, k, :], xl[q][:, k, :], "xt")
            tbank.free(i, h, l)
            k_xt[c] = [h, l]
            turned[c] = [t]

        def three(dst, wh, wl, mh, ml, first, last, skip=False):
            out_ = []
            for j, (a, b) in enumerate(((wl, mh), (wh, ml), (wh, mh))):
                out_.append(lambda e, a=a, b=b, j=j: e.matmul(
                    dst, a, b, start=(first and j == 0), stop=(last and j == 2), skip_group_check=skip))
            return out_

        z_k = [None] * NC
        z_r = [[], []]
        g_prev = []

        def l0_scan(c):
            nonlocal g_prev
            q = c % 2
            i, bk, free = ubank.take()
            m = []
            for k in range(2):
                m += three(bk[:, :], bh[:, k, :], bl[:, k, :], xh[q][:, k, :], xl[q][:, k, :], k == 0, k == 1)
            u = put("T", "bu", [*k_b, *k_xt[c], *free], *m)
            ks = []
            for b in range(2):
                r = slice(64 * b, 64 * b + 64)
                s = slice(256 * b, 256 * b + 256)
                ks.append(put("V", "rot", [u, k_tab, *g_prev], lambda e, r=r, s=s: e.tensor_tensor(
                    g1[r, :], bk[0:64, s], tci[r, :], ALU.mult)))
                ks.append(put("V", "rot", [], lambda e, r=r, s=s: e.tensor_tensor(
                    g2[r, :], bk[64:128, s], tsi[r, :], ALU.mult)))
            ubank.free(i, ks[-1])
            a = put("V", "rot", [ks[-1]], lambda e: e.tensor_tensor(g1[:, :], g1[:, :], g2[:, :], ALU.add))
            a = put("V", "rot", [a], lambda e: e.tensor_tensor_scan(gs[:, :], mag.broadcast_to([128, T]), g1[:, :], 0.0,
                                                                    ALU.mult, ALU.add))
            zs = []
            for b in range(2):
                r = slice(64 * b, 64 * b + 64)
                w = [a, *z_r[b]]
                put("V", "rot", w, lambda e, r=r, b=b: e.tensor_tensor(
                    Z[b][0:64, :], gs[r, :], tc[r, :], ALU.mult))
                zs.append(put("V", "rot", [], lambda e, r=r, b=b: e.tensor_tensor(
                    Z[b][64:128, :], gs[r, :], tsn[r, :], ALU.mult)))
            g_prev = [zs[-1]]
            z_k[c] = zs

        z_prev = [[], []]
        th_prev = []
        s_tok = {}

        def l0_y(c, b):
            q = c % 2
            i, bk, free = ybank.take()
            y = put("T", "y", [z_k[c][b], *free], *[
                lambda e, j=j: e.matmul(bk[:, 256 * j:256 * j + 256], Z[b][:, 128 * j:128 * j + 128],
                                        RR[:, :], start=True, stop=True) for j in range(2)])
            z_r[b] = [y]
            db = VEC[:, OFF_D:OFF_D + D].unsqueeze(1).broadcast_to([128, 2, D])
            s0 = xn[q]
            g = put("G", "dx", [k_xn[c], d_vec, *turned[c]], lambda e: e.tensor_tensor(
                s0[:, 2 * b:2 * b + 2, :], s0[:, 2 * b:2 * b + 2, :], db, ALU.mult))
            v = put("V", "sy", [y, g], lambda e: e.tensor_tensor(
                s0[:, 2 * b:2 * b + 2, :], bk[:, :].rearrange("p (a d) -> p a d", a=2),
                s0[:, 2 * b:2 * b + 2, :], ALU.add))
            ybank.free(i, v)
            s_tok[b] = v
            return g

        h_r = [[], [], []]
        hs_r = [[], []]
        k_h = {}
        hn = [0]

        def l0_up(c, hb):
            q = c % 2
            i, bk, free = fbank.take()
            m = []
            sl = slice(128 * hb, 128 * hb + 128)
            for k in range(2):
                m += three(bk[:, :], w1h[:, k, sl], w1l[:, k, sl], xh[q][:, k, :], xl[q][:, k, :],
                           k == 0, k == 1)
            t = put("T", "f1", [*k_w1, *k_xt[c], *free], *m)
            r, v = hn[0] % 3, hn[0] % 2
            hn[0] += 1
            g = put("S", "gelu", [t, d_b1, *hs_r[v]], lambda e: e.activation(
                hs[v][:, :], bk[:, :], ACT.Gelu, bias=B1[:, hb:hb + 1]))
            fbank.free(i, g)
            a, b = split([g, *h_r[r]], hs[v][:, :], hh[r][:, :], hl[r][:, :], "hs")
            hs_r[v] = [a, b]
            k_h[(c, hb)] = (r, a, b)
            return t

        z_free = []

        def l0_down(c, hb):
            nonlocal z_free
            r, a, b = k_h[(c, hb)]
            m = []
            for t in range(4):
                dst = obank[t // 2][:, 256 * (t % 2):256 * (t % 2) + 256]
                sl = slice(128 * t, 128 * t + 128)
                first = hb == 0 and t % 2 == 0
                m += three(dst, hh[r][:, sl], hl[r][:, sl], w2h[:, hb, :], w2l[:, hb, :],
                           first, hb == 7, skip=True)
            t = put("T", "f2", [a, b, *k_w2, *(z_free if hb == 0 else [])], *m)
            h_r[r] = [t]
            return t

        x1_k = [None] * NC

        def l0_out(c, t):
            nonlocal z_free, th_prev
            z_free = []
            s0 = xn[c % 2]
            for b in range(2):
                sl = slice(2 * b, 2 * b + 2)
                bb = VEC[:, OFF_B2:OFF_B2 + D].unsqueeze(1).broadcast_to([128, 2, D])
                z = put("V", "z0", [t, d_vec, *z_prev[b]], lambda e, b=b, sl=sl: e.tensor_tensor(
                    z0[:, sl, :], obank[b][:, :].rearrange("p (a d) -> p a d", a=2), bb, ALU.add))
                z_free.append(z)
            for b in range(2):
                sl = slice(2 * b, 2 * b + 2)
                xs = slice(4 * c + 2 * b, 4 * c + 2 * b + 2)
                th = put("S", "th0", [z_free[b], *th_prev], lambda e, sl=sl: e.activation(
                    th0[:, :, :], z0[:, sl, :], ACT.Tanh, scale=0.5))
                a = put("V", "x1", [th], lambda e, sl=sl: e.scalar_tensor_tensor(
                    z0[:, sl, :], th0[:, :, :], 1.0, z0[:, sl, :], ALU.add, ALU.mult))
                th_prev = [a]
                a = put("V", "x1", [a, s_tok[b]], lambda e, sl=sl: e.tensor_tensor(
                    s0[:, sl, :], s0[:, sl, :], z0[:, sl, :], ALU.mult))
                a = put("V", "x1", [a], lambda e, sl=sl, xs=xs: e.scalar_tensor_tensor(
                    X[:, xs, :], s0[:, sl, :], 0.5, X[:, xs, :], ALU.mult, ALU.add))
                z_prev[b] = [a]
            x1_k[c] = a
            xn_r[c % 2] = [a]

        free2 = {i: [] for i in range(3)}
        free2[0] = list(k_w1)
        free2[1] = list(k_w2)
        free_stk = {0: list(k_b), 1: []}
        k_w = {}

        def w_rope():
            src = stage[2][:, :].rearrange("p (k h n) -> p k h n", k=2, h=NH)
            a = put("S", "wr", [d_wqr], lambda e: e.activation(
                wq_hi[:, :, :, 64:128], src, ACT.Copy, scale=-SCALE))
            b = put("V", "wr", [a], lambda e: e.scalar_tensor_tensor(
                wq_lo[:, :, :, 64:128], src, -SCALE, wq_hi[:, :, :, 64:128].bitcast(F32),
                ALU.mult, ALU.subtract))
            free2[2] = [a, b]
            k_w["r"] = [a, b]

        d_wn = {}

        def load_nope(g):
            s = g
            d_wn[g] = [load(f"wn{g}", stage[s][:, :], wqn[:, g * 2048:(g + 1) * 2048], free2[s]),
                       load(f"wk{g}", stk[:, g, :], wkbt[:, g * 512:(g + 1) * 512], free_stk[g])]

        def w_nope(g, k):
            i, bk, free = wbank.take()
            wn = stage[g][:, :].rearrange("p (h d) -> p h d", h=8)
            t = put("T", "wn", [*d_wn[g], *free], *[
                lambda e, j=j: e.matmul(bk[:, 64 * j:64 * j + 64], wn[:, j, 128 * k:128 * k + 128],
                                        stk[:, g, 64 * j:64 * j + 64], start=True, stop=True)
                for j in range(8)])
            src = bk[:, :].rearrange("p (h n) -> p h n", h=8)
            hi, lo = (w[:, k, 8 * g:8 * g + 8, 0:64] for w in (wq_hi, wq_lo))
            a = put("S", "wn", [t], lambda e: e.activation(hi, src, ACT.Copy, scale=-SCALE))
            b = put("V", "wn", [t, a], lambda e: e.scalar_tensor_tensor(
                lo, src, -SCALE, hi.bitcast(F32), ALU.mult, ALU.subtract))
            wbank.free(i, a, b)
            free2[g] = [t]
            free_stk[g] = [t]
            k_w[("n", g, k)] = [a, b]

        d_wo = {}

        def load_o(g):
            d_wo[g] = [load(f"wo{g}", stage[g][:, :], wo[:, g * 2048:(g + 1) * 2048], free2[g]),
                       load(f"wv{g}", stk[:, g, :], wvbt[:, g * 512:(g + 1) * 512], free_stk[g])]

        def w_o(g, i2):
            i, bk, free = wbank.take()
            wv = stage[g][:, :].rearrange("p (h d) -> p h d", h=8)
            ms = []
            for j in range(2):
                for half in range(2):
                    h = 4 * half + 2 * i2 + j
                    ms.append(lambda e, j=j, half=half, h=h: e.matmul(
                        bk[64 * half:64 * half + 64, 256 * j:256 * j + 256],
                        stk[:, g, 64 * h:64 * h + 64], wv[:, h, :], start=True, stop=True))
            t = put("T", "wo", [*d_wo[g], *free], *ms)
            a = put("S", "wo", [t], lambda e: e.activation(
                woe[:, 4 * g + 2 * i2:4 * g + 2 * i2 + 2, :],
                bk[:, :].rearrange("p (j d) -> p j d", j=2), ACT.Copy))
            wbank.free(i, a)
            free2[g] = [t]
            free_stk[g] = [t]
            k_w[("o", g, i2)] = [a]

        d_wm = []

        def load_m():
            s = stage[2][:, 0:1040].rearrange("p (k n) -> p k n", k=2)
            w = free2[2]
            d_wm.append(load("wm0", s[:, :, 0:128], wkva, w))
            d_wm.append(load("wm1", s[:, :, 128:256], loraa, w))
            d_wm.append(load("wm2", s[:, :, 256:264], routert, w))
            d_wm.append(load("wm3", s[:, :, 264:520], baset, w))
            d_wm.append(load("wm4", LB[:, :], lorab))

        def w_m():
            s = stage[2][:, 0:1040].rearrange("p (k n) -> p k n", k=2)
            k_w["m"] = [*split(d_wm, s, wm_hi[:, :, :], wm_lo[:, :, :], "wm"), d_wm[-1]]

        def rope_tables():
            toks = []
            for q in range(2):
                for j in range(2):
                    toks.append(put("G", "rt", [d_const], lambda e, q=q, j=j: e.tensor_copy(
                        rope_c[:, q, j, :], cosT[q])))
                    toks.append(put("G", "rt", [], lambda e, q=q, j=j: e.tensor_scalar(
                        rope_s[:, q, j, :], sinT[q], 1.0 if j == 0 else -1.0, 1.0, ALU.mult, ALU.mult)))
            return toks[-1]

        k_rt = rope_tables()

        fill = {
            (1, 1): w_rope,
            (1, 3): lambda: (load_nope(0), load_nope(1), load_m()),
            (2, 4): lambda: w_nope(0, 0), (2, 6): lambda: w_nope(0, 1),
            (3, 1): lambda: w_nope(1, 0), (3, 3): lambda: w_nope(1, 1),
            (3, 4): w_m,
            (3, 5): lambda: (load_o(0), load_o(1)),
            (5, 1): lambda: w_o(0, 0), (5, 4): lambda: w_o(0, 1),
            (6, 1): lambda: w_o(1, 0), (6, 4): lambda: w_o(1, 1),
        }

        l0_norm(0)
        l0_turn(0, 0)
        l0_turn(0, 1)
        l0_scan(0)
        for c in range(NC):
            for hb in range(9):
                if hb < 8:
                    t = l0_up(c, hb)
                    if hb == 7:
                        last_up = t
                if hb == 0 and c + 1 < NC:
                    l0_norm(c + 1)
                if hb == 1:
                    l0_y(c, 0)
                if hb == 3:
                    l0_y(c, 1)
                if c + 1 < NC:
                    if hb == 4:
                        l0_turn(c + 1, 0)
                    if hb == 5:
                        l0_turn(c + 1, 1)
                    if hb == 7:
                        l0_scan(c + 1)
                if hb >= 1:
                    d = l0_down(c, hb - 1)
                if (c, hb) in fill:
                    fill[(c, hb)]()
            xt_r[c % 2] = [last_up]
            l0_out(c, d)
        end0 = [x1_k[NC - 1], ("f2_T", p.count["f2_T"]), ("hsl_V", p.count["hsl_V"]),
                ("hsh_S", p.count["hsh_S"]), ("th0_S", p.count["th0_S"]), ("dx_G", p.count["dx_G"]),
                ("y_T", p.count["y_T"]), ("wo_T", p.count["wo_T"]), ("wo_S", p.count["wo_S"]),
                ("wml_V", p.count["wml_V"]), ("wmh_S", p.count["wmh_S"])]
        pj = Ring([bank[1], bank[2]])
        tb = Ring([bank[0], bank[7]])
        sbk = Ring([bank[5], bank[6]])
        bsk, obk = bank[3], bank[4]
        for r_ in (pj, tb, sbk):
            for i in range(len(r_.buffers)):
                r_.free(i, *end0)
        bs_free, ob_free = [*end0], [*end0]
        qk = Ring(list(zip(QK, q1b, q2b)))
        sm, pp, pt = Ring(SM), Ring(PP), Ring(PT)
        for r_ in (qk, sm, pp, pt):
            for i in range(len(r_.buffers)):
                r_.free(i, *end0)
        B = {}

        def flip(n):
            return "S" if n % 2 == 0 else "V"

        def copy(eng, name, waits, dst, src):
            if eng == "S":
                return put("S", name, waits, lambda e: e.activation(dst, src, ACT.Copy))
            return put("V", name, waits, lambda e: e.tensor_copy(dst, src))

        r_yn, r_yx, r_qt, r_kt, r_z = (Turns(2, end0) for _ in range(5))
        r_kv = Turns(3, end0)
        r_mlt, r_mt, r_ln = (Turns(1, end0) for _ in range(3))
        r_ot, r_fo = [Turns(1, end0) for _ in range(2)], [Turns(1, end0) for _ in range(2)]

        def l1_norm(b):
            q = b % 2
            a = put("V", "bn1", [x1_k[b // 2], *end0, *r_ln.readers(b)],
                    *[lambda e, i=i: e.bn_stats(st1[:, i, :], X[:, 2 * b + i, :]) for i in range(2)])
            a = put("V", "bn1", [a], *[lambda e, i=i: e.bn_aggr(mv1[:, i, :], st1[:, i, :])
                                       for i in range(2)])
            a = rsqrt([a], mv1[:, :, 1], LN_EPS, 2, "ln1", rs1, ri1[:, :])
            k = put("V", "yn", [a, *r_yn.readers(b)], *[
                lambda e, i=i: e.tensor_scalar(yn[q][:, i, :], X[:, 2 * b + i, :], mv1[:, i, 0:1],
                                               rs1[:, 4, i:i + 1], ALU.subtract, ALU.mult)
                for i in range(2)])
            r_ln.free(b, k)
            B[b] = {"yn": k, "qt": {}, "rel": {}}

        def l1_turn(b):
            q = b % 2
            i, bk, free = tb.take()
            t = put("T", "ty", [B[b]["yn"], *free], *[
                lambda e, k=k, j=j: e.transpose(bk[:, 256 * k + 128 * j:256 * k + 128 * j + 128],
                                                yn[q][:, j, 128 * k:128 * k + 128], ident)
                for k in range(2) for j in range(2)])
            h, l = split([t, *r_yx.readers(b)], bk[:, :].rearrange("p (k n) -> p k n", k=2),
                         yh[q][:, :, :], yl[q][:, :, :], "yt")
            tb.free(i, h, l)
            r_yn.free(b, t)
            B[b]["yt"] = [h, l]

        def l1_misc(b, t):
            nonlocal bs_free
            q = b % 2
            sl = slice(128 * t, 128 * t + 128)
            i, bk, free = pj.take()
            m = []
            for k in range(2):
                m += three(bk[:, 0:264], yh[q][:, k, sl], yl[q][:, k, sl], wm_hi[:, k, 0:264],
                           wm_lo[:, k, 0:264], k == 0, k == 1)
            a = put("T", "mi", [*B[b]["yt"], *k_w["m"], *free], *m)
            c_ = put("S", "mi", [a, *r_mlt.readers(b)], lambda e: e.activation(
                ML[:, t, :], bk[:, 0:264], ACT.Copy))
            pj.free(i, c_)
            m = []
            for k in range(2):
                m += three(bsk[:, 256 * t:256 * t + 256], yh[q][:, k, sl], yl[q][:, k, sl],
                           wm_hi[:, k, 264:520], wm_lo[:, k, 264:520], t == 0 and k == 0, False,
                           skip=True)
            put("T", "ba", bs_free if t == 0 else [], *m)
            B[b][("mi", t)] = c_

        def vk(c, f, name="kv"):
            return put("V", name, c, f)

        def l1_kv(b):
            q = b % 2
            w = [B[b][("mi", 0)], B[b][("mi", 1)]]
            cl = ML[:, :, 0:64]
            a = vk(w, lambda e: e.tensor_tensor(sq[:, :, :], cl, cl, ALU.mult))
            a = vk([a], lambda e: e.tensor_reduce(lv[:, 0, :], sq[:, :, :], AX.X, ALU.add))
            a = vk([a], lambda e: e.tensor_scalar(lv[:, 1, :], lv[:, 0, :], 1.0 / 64, None, ALU.mult))
            a = rsqrt([a], lv[:, 1, :], RMS_EPS, 2, "rms", rs2, ri2[:, :])
            kw = VEC[:, OFF_KW:OFF_KW + 64]
            a = put("V", "kvw", [a, *r_kv.readers(b)], *[
                lambda e, t=t: e.scalar_tensor_tensor(KV[b % 3][:, t, 0:64], ML[:, t, 0:64],
                                                      rs2[:, 4, t:t + 1], kw, ALU.mult, ALU.mult)
                for t in range(2)])
            r = ML[:, :, 64:128].rearrange("p t (j n) -> p t j n", j=2)
            g = put("G", "kr", [*w, k_rt, *r_mlt.readers(b)], lambda e: e.tensor_tensor(
                kr[:, 0:2, 0, :, :], r, rope_c[:, :, :, :], ALU.mult))
            g = put("G", "kr", [g], lambda e: e.tensor_tensor(
                kr[:, 2:4, 0, :, :], r, rope_s[:, :, :, :], ALU.mult))
            gg = put("G", "kr", [g, *r_kv.readers(b)], *[
                lambda e, j=j: e.tensor_tensor(KV[b % 3][:, :, 64 + 32 * j:96 + 32 * j], kr[:, 0:2, 0, j, :],
                                               kr[:, 2:4, 0, 1 - j, :], ALU.add) for j in range(2)])
            i, bk, free = tb.take()
            t = put("T", "tk", [a, gg, *free], *[
                lambda e, j=j: e.transpose(bk[:, 128 * j:128 * j + 128], KV[b % 3][:, j, :], ident)
                for j in range(2)])
            k = put("S", "kt", [t, *r_kt.readers(b)], lambda e: e.activation(
                KT[q][:, :], bk[:, 0:256], ACT.Copy))
            tb.free(i, k)
            B[b]["kt"] = k
            B[b]["kv"] = [a, gg]
            B[b]["tk"] = t

        def l1_gate(b):
            w = [B[b][("mi", 0)], B[b][("mi", 1)], *r_mlt.readers(b)]
            L, E1, K1, L2, E2, SG, CT_ = (lg[:, i, :, :] for i in range(7))
            n = "gt"

            def bc(v):
                return v.unsqueeze(2).broadcast_to([128, 2, 8])

            def first_of(c, src, top, hot):
                c = vk(c, lambda e: e.tensor_reduce(top, src, AX.X, ALU.max), n)
                c = vk([c], lambda e: e.tensor_tensor(hot, src, bc(top), ALU.is_equal), n)
                c = vk([c], lambda e: e.tensor_tensor(hot, hot, ramp, ALU.mult), n)
                c = vk([c], lambda e: e.tensor_reduce(lv[:, 4, :], hot, AX.X, ALU.max), n)
                return vk([c], lambda e: e.tensor_tensor(hot, ramp, bc(lv[:, 4, :]), ALU.is_equal), n)

            rb = VEC[:, OFF_RB:OFF_RB + 8].unsqueeze(1).broadcast_to([128, 2, 8])
            c_ = vk(w, lambda e: e.tensor_tensor(L, ML[:, :, 256:264], rb, ALU.add), n)
            c_ = first_of([c_, k_ramp], L, lv[:, 2, :], E1)
            c_ = vk([c_], lambda e: e.scalar_tensor_tensor(L2, E1, -3e38, L, ALU.mult, ALU.add), n)
            c_ = first_of([c_], L2, lv[:, 3, :], E2)
            c_ = vk([c_], lambda e: e.tensor_tensor(E1, E1, E2, ALU.add), n)
            c_ = vk([c_], lambda e: e.tensor_tensor(L2, L, bc(lv[:, 2, :]), ALU.subtract), n)
            c_ = put("S", "gt", [c_], lambda e: e.activation(L2, L2, ACT.Exp))
            c_ = vk([c_], lambda e: e.tensor_tensor(E1, E1, L2, ALU.mult), n)
            c_ = vk([c_], lambda e: e.tensor_reduce(lv[:, 5, :], E1, AX.X, ALU.add), n)
            c_ = vk([c_], lambda e: e.reciprocal(lv[:, 6, :], lv[:, 5, :]), n)
            c_ = vk([c_], lambda e: e.scalar_tensor_tensor(E1, E1, 2.0, bc(lv[:, 6, :]), ALU.mult, ALU.mult), n)
            mids = ML[:, :, 128:256]
            c_ = vk([c_], lambda e, t=0: e.tensor_tensor(
                ML[:, t, 128:256].rearrange("p (x r) -> p x r", x=8),
                ML[:, t, 128:256].rearrange("p (x r) -> p x r", x=8),
                E1[:, t, :].unsqueeze(2).broadcast_to([128, 8, 16]), ALU.mult), n)
            c_ = vk([c_], lambda e: e.tensor_tensor(
                ML[:, 1, 128:256].rearrange("p (x r) -> p x r", x=8),
                ML[:, 1, 128:256].rearrange("p (x r) -> p x r", x=8),
                E1[:, 1, :].unsqueeze(2).broadcast_to([128, 8, 16]), ALU.mult), n)
            i, bk, free = tb.take()
            t = put("T", "tm", [c_, *free], *[
                lambda e, j=j: e.transpose(bk[:, 128 * j:128 * j + 128], ML[:, j, 128:256], ident)
                for j in range(2)])
            k = put("S", "mt", [t, *r_mt.readers(b)], lambda e: e.activation(
                MT[:, :, :], bk[:, 0:256].rearrange("p (t n) -> p t n", t=2), ACT.Copy))
            tb.free(i, k)
            B[b]["mt"] = k
            r_mlt.free(b, t, *B[b]["kv"])

        def l1_lora(b):
            nonlocal bs_free
            q = b % 2
            m = put("T", "lo", [B[b]["mt"], *k_w["m"]], *[
                lambda e, t=t: e.matmul(bsk[:, 256 * t:256 * t + 256], MT[:, t, :], LB[:, :],
                                        start=False, stop=True, skip_group_check=True)
                for t in range(2)])
            r_mt.free(b, m)
            bb = VEC[:, OFF_BB:OFF_BB + D].unsqueeze(1).broadcast_to([128, 2, D])
            z = put("V", "z1", [m, *r_z.readers(b)], lambda e: e.tensor_tensor(
                z1[q][:, :, :], bsk[:, :].rearrange("p (t d) -> p t d", t=2), bb, ALU.add))
            bs_free = [z]
            th = put("S", "th1", [z, *r_z.readers(b)], lambda e: e.activation(
                th1[q][:, :, :], z1[q][:, :, :], ACT.Tanh, scale=0.5))
            B[b]["w"] = put("V", "w1", [th, *r_z.readers(b)], lambda e: e.scalar_tensor_tensor(
                w1b[q][:, :, :], th1[q][:, :, :], 1.0, z1[q][:, :, :], ALU.add, ALU.mult))

        def l1_q(b, t, g):
            q = b % 2
            sl = slice(128 * t, 128 * t + 128)
            i, bk, free = pj.take()
            m = []
            for k in range(2):
                m += three(bk[:, :], yh[q][:, k, sl], yl[q][:, k, sl],
                           wq_hi[:, k, 4 * g:4 * g + 4, :], wq_lo[:, k, 4 * g:4 * g + 4, :],
                           k == 0, k == 1)
            wk = [*k_w["r"]]
            for kk in range(2):
                wk += k_w[("n", g // 2, kk)]
            a = put("T", "q", [*B[b]["yt"], *wk, *free], *m)
            if t == 1 and g == 3:
                r_yx.free(b, a)
            v = bk[:, :].rearrange("p (h n) -> p h n", h=4)
            ro = v[:, :, 64:128].rearrange("p h (j n) -> p h j n", j=2)
            n, (Q, t1, t2), fr = qk.take()
            c1 = put("S", "q", [a, *fr], lambda e: e.activation(Q[:, :, 0:64], v[:, :, 0:64], ACT.Copy))
            cb = rope_c[:, t, :, :].rearrange("p j n -> p (j n)").unsqueeze(1).broadcast_to([128, 4, 64])
            sb2 = rope_s[:, t, :, :].rearrange("p j n -> p (j n)").unsqueeze(1).broadcast_to([128, 4, 64])
            rf = v[:, :, 64:128]
            t1f = t1[:, :, :, :].rearrange("p h j n -> p h (j n)")
            t2f = t2[:, :, :, :].rearrange("p h j n -> p h (j n)")
            c2 = put("V", "q", [a, k_rt, c1, *fr],
                     lambda e: e.tensor_tensor(t1f, rf, cb, ALU.mult),
                     lambda e: e.tensor_tensor(t2f, rf, sb2, ALU.mult))
            pj.free(i, c1, c2)
            c3 = put("G", "q", [c2, *fr], *[
                lambda e, j=j: e.tensor_tensor(Q[:, :, 64 + 32 * j:96 + 32 * j], t1[:, :, j, :],
                                               t2[:, :, 1 - j, :], ALU.add) for j in range(2)])
            B[b][("q", t, g)] = (n, Q, c1, c3)

        def l1_qt(b, t, g):
            q = b % 2
            n, Q, c1, c3 = B[b][("q", t, g)]
            i, bk, free = tb.take()
            tr = put("T", "tq", [c1, c3, *free], *[
                lambda e, j=j: e.transpose(bk[:, 128 * j:128 * j + 128], Q[:, j, :], ident)
                for j in range(4)])
            qk.free(n, tr)
            e_ = copy(flip(g), "qt", [tr, *r_qt.readers(b)],
                      QT[q][:, t, 4 * g:4 * g + 4, :].rearrange("p h n -> p (h n)"), bk[:, :])
            tb.free(i, e_)
            B[b]["qt"][(t, g)] = e_

        def pair(pi):
            if pi < 2:
                return 0, [[8 * pi + i for i in range(4)], [8 * pi + 4 + i for i in range(4)]]
            hgrp, two = (pi - 2) // 2, (pi - 2) % 2
            return 1, [[8 * hgrp + 4 * hf + 2 * two + i for i in range(2)] for hf in range(2)]

        st_ring = Ring(st_b)
        for i in range(4):
            st_ring.free(i, *end0)

        def l1_s(b, pi, hf):
            q = b % 2
            qt, heads = pair(pi)
            hd = heads[hf]
            nk = 128 * (qt + 1)
            i, bk, free = sbk.take()
            w = [B[b]["qt"][(qt, h // 4)] for h in hd]
            s = put("T", "s", [B[b]["kt"], *w, *free], *[
                lambda e, j=j, h=h: e.matmul(bk[:, nk * j:nk * j + nk], QT[q][:, qt, h, :],
                                             KT[q][:, 0:nk], start=True, stop=True)
                for j, h in enumerate(hd)])
            if (pi, hf) == (5, 1):
                r_kt.free(b, s)
                r_qt.free(b, s)
            mi, M_, mf = sm.take()
            si, S_, sf = st_ring.take()
            mk = mask1 if qt else mask0
            a = put("V", "s", [s, *mf, *sf], *[
                lambda e, j=j: e.tensor_tensor_reduce(
                    M_[:, nk * j:nk * j + nk], bk[:, nk * j:nk * j + nk], mk, 1.0, 3e38,
                    ALU.add, ALU.min, S_[:, 0, j:j + 1]) for j in range(len(hd))])
            sbk.free(i, a)
            pi_, P_, pf = pp.take()
            x_ = put("S", "p", [a, *pf], *[
                lambda e, j=j: e.activation(P_[:, nk * j:nk * j + nk], M_[:, nk * j:nk * j + nk],
                                            ACT.Exp, bias=S_[:, 0, j:j + 1], scale=-1.0,
                                            accum_out=S_[:, 1, j:j + 1]) for j in range(len(hd))])
            sm.free(mi, x_)
            n = len(hd)
            r = put("V", "r", [x_], lambda e: e.reciprocal(S_[:, 2, 0:n], S_[:, 1, 0:n]))
            g = put("G", "n", [r], *[
                lambda e, j=j: e.tensor_scalar(P_[:, nk * j:nk * j + nk], P_[:, nk * j:nk * j + nk],
                                               S_[:, 2, j:j + 1], 1.0, ALU.mult, ALU.mult)
                for j in range(n)])
            st_ring.free(si, g)
            B[b][("s", pi, hf)] = (pi_, P_, g, s)

        nev = [0]

        def l1_pt(b, pi, hf):
            qt, heads = pair(pi)
            pi_, P_, g, _ = B[b][("s", pi, hf)]
            i, bk, free = tb.take()
            if qt == 0:
                spans = [(128 * j, 128 * j) for j in range(4)]
            else:
                spans = [(256 * kb + 128 * j, 256 * j + 128 * kb) for kb in range(2) for j in range(2)]
            t = put("T", "tp", [g, *free], *[
                lambda e, d=d, s=s: e.transpose(bk[:, d:d + 128], P_[:, s:s + 128], ident)
                for d, s in spans])
            pp.free(pi_, t)
            ti, T_, tf = pt.take()
            nev[0] += 1
            e_ = copy("V" if nev[0] % 3 == 0 else "S", "pt", [t, *tf], T_[:, :], bk[:, :])
            tb.free(i, e_)
            B[b][("t", pi, hf)] = (ti, T_, e_)

        def l1_pv(b, pi):
            nonlocal ob_free
            q = b % 2
            qt, heads = pair(pi)
            tk = [B[b][("t", pi, hf)] for hf in range(2)]
            first = pi < 2 or pi % 2 == 0
            ms = []
            for kb in range(qt + 1):
                for hf in range(2):
                    T_ = tk[hf][1]
                    if qt == 0:
                        dst, src = slice(0, 512), slice(0, 512)
                    else:
                        o = 128 * (heads[hf][0] % 4)
                        dst, src = slice(o, o + 256), slice(256 * kb, 256 * kb + 256)
                    ms.append(lambda e, kb=kb, hf=hf, T_=T_, dst=dst, src=src: e.matmul(
                        obk[64 * hf:64 * hf + 64, dst], KV[b % 3][:, kb, 0:64], T_[:, src],
                        start=(kb == 0), stop=(kb == qt), skip_group_check=True))
            m = put("T", "pv", [tk[0][2], tk[1][2], *B[b]["kv"], *(ob_free if first else [])], *ms)
            for hf in range(2):
                pt.free(tk[hf][0], m)
            if pi < 2 or pi % 2 == 1:
                H = heads[0][0] // 8
                e_ = copy("S" if H else "V", "ot", [m, *r_ot[qt].readers(b)], oT[qt][:, H, :], obk[:, :])
                ob_free = [e_]
                B[b][("o", qt, H)] = e_
            if pi == 5:
                r_kv.free(b, m, B[b]["tk"])

        d_out = []

        def l1_out(b, qt):
            q = b % 2
            i, bk, free = pj.take()
            wk = [t for g in range(2) for i2 in range(2) for t in k_w[("o", g, i2)]]
            m = put("T", "o", [B[b][("o", qt, 0)], B[b][("o", qt, 1)], *wk, *free], *[
                lambda e, c=c: e.matmul(bk[:, 0:256], oT[qt][:, c // 4, 128 * (c % 4):128 * (c % 4) + 128],
                                        woe[:, c, :], start=(c == 0), stop=(c == 7)) for c in range(8)])
            r_ot[qt].free(b, m)
            a = put("V", "o", [m, B[b]["w"], *r_fo[qt].readers(b)], lambda e: e.tensor_tensor(
                pr[qt][:, :], bk[:, 0:256], w1b[q][:, qt, :], ALU.mult))
            pj.free(i, a)
            f = put("V", "o", [a], lambda e: e.scalar_tensor_tensor(
                fo[qt][:, :], pr[qt][:, :], 0.5, X[:, 2 * b + qt, :], ALU.mult, ALU.add))
            if qt == 1:
                r_z.free(b, f)
            n = 2 * b + qt
            d = put("D", f"out{qt}", [f], lambda e: e.dma_start(out[:, n * D:(n + 1) * D], fo[qt][:, :]))
            r_fo[qt].free(b, d)
            d_out.append(d)

        def ramp_make():
            c_ = []
            for j in range(8):
                c_.append(put("G", "ra", end0, lambda e, j=j: e.memset(lg[:, 11, :, j:j + 1], 8.0 - j)))
            return c_[-1]

        k_ramp = ramp_make()
        ramp = lg[:, 11, :, :]

        def prep(b):
            yield lambda: l1_norm(b)
            yield lambda: l1_turn(b)
            yield lambda: l1_misc(b, 0)
            yield lambda: l1_misc(b, 1)
            yield lambda: l1_kv(b)
            for t in range(2):
                for g in range(4):
                    yield lambda t=t, g=g: l1_q(b, t, g)
                    if (t, g) == (0, 0):
                        yield lambda: l1_gate(b)
                    if (t, g) == (0, 3):
                        yield lambda: l1_lora(b)
                    if (t, g) != (0, 0):
                        u = 4 * t + g - 1
                        yield lambda u=u: l1_qt(b, u // 4, u % 4)
            yield lambda: l1_qt(b, 1, 3)

        for f in prep(0):
            f()
        units = [(b, pi, hf) for b in range(NB) for pi in range(6) for hf in range(2)]
        LAG_T, LAG_V = 2, 4
        steps = {}
        for n in range(len(units) + LAG_V + 2):
            if n < len(units):
                b, pi, hf = units[n]
                if pi == 0 and hf == 0 and b + 1 < NB:
                    steps = iter(list(prep(b + 1)))
                l1_s(b, pi, hf)
            work = 2 if n < len(units) else 0
            for _ in range(work):
                f = next(steps, None) if n // 12 + 1 < NB + 1 and n // 12 < NB - 1 else None
                if f:
                    f()
            if 0 <= n - LAG_T < len(units):
                l1_pt(*units[n - LAG_T])
            if 0 <= n - LAG_V < len(units) and units[n - LAG_V][2] == 1:
                b, pi, hf = units[n - LAG_V]
                l1_pv(b, pi)
            k = n - LAG_V - 2
            if 0 <= k < len(units):
                b, pi, hf = units[k]
                if pi == 1 and hf == 1:
                    l1_out(b, 0)
                if pi == 5 and hf == 1:
                    l1_out(b, 1)

        block = ctx.enter_context(nc.Block())

        @block.sync
        def _(e):
            p.run("D", e)
            for k in ("out0_D", "out1_D"):
                e.wait_ge(p.sems[k], p.count[k])

        @block.tensor
        def _(e):
            p.run("T", e)

        @block.vector
        def _(e):
            p.run("V", e)

        @block.scalar
        def _(e):
            p.run("S", e)

        @block.gpsimd
        def _(e):
            p.run("G", e)


def shape_constants():
    c = np.zeros((128, 514), np.float32)
    c[:, 0:128] = np.eye(128)
    i = np.arange(128)
    c[:, 256:384] = np.where(i[None, :] > i[:, None], BIG, 0.0)
    freqs = (np.float32(1.0) / np.power(np.float32(10000.0), np.arange(0, 64, 2, dtype=np.float32)
                                        / np.float32(64))).astype(np.float32)
    t = (np.arange(T, dtype=np.float32)[:, None] * freqs[None, :]).astype(np.float32)
    for q in range(2):
        a = t[128 * q:128 * q + 128].astype(np.float64)
        c[:, 384 + 32 * q:416 + 32 * q] = np.cos(a)
        c[:, 448 + 32 * q:480 + 32 * q] = np.sin(a)
    quad = i // 32
    c[:, 512] = np.where(quad % 2 == 0, 1.0, -1.0)
    c[:, 513] = np.where(quad == 0, 1.0, -1.0)
    return c


def kernel(**inputs):
    import concourse.bacc as bacc
    from concourse.bass_utils import run_bass_kernel_spmd

    a = {k: np.asarray(v) for k, v in inputs.items()}

    def chunks(w):
        k = w.shape[0] // 128
        return w.reshape(k, 128, -1).transpose(1, 0, 2).reshape(128, -1)

    wq = a["L1_attn_Wq"].reshape(D, NH, 192)
    kvb = a["L1_attn_Wkv_b"].reshape(64, NH, 256)
    rope = wq[:, :, 128:]
    wkva = a["L1_attn_Wkv_a"]
    bre, bim = a["L0_attn_B_re"].T, a["L0_attn_B_im"].T
    cre, cim = a["L0_attn_C_re"].T, a["L0_attn_C_im"].T
    vecs = np.concatenate([a["L0_attn_D"], a["L0_ffn_proj2_bias"], a["L1_ffn_base_b"],
                           a["L1_ffn_router_b"], a["L1_attn_kv_norm_w"]])
    nuth = np.stack([a["L0_attn_nu_log"], a["L0_attn_theta_log"]], axis=1)
    arrays = {
        "x": a["L0_attn_x"].reshape(NT, 128, D).transpose(1, 0, 2).reshape(128, -1),
        "consts": shape_constants(),
        "vecs": np.tile(vecs[None, :], (128, 1)),
        "w1t": chunks(a["L0_ffn_proj1"].T),
        "w2t": chunks(a["L0_ffn_proj2"].T),
        "b1c": a["L0_ffn_proj1_bias"].reshape(8, 128).T,
        "bt": chunks(np.concatenate([bre, bim, bim, bre], axis=1)),
        "ct": np.concatenate([cre, cim, cim, cre], axis=0),
        "nuth": np.tile(nuth, (4, 1)),
        "wqn": wq[:, :, :128].transpose(2, 1, 0).reshape(128, -1),
        "wkbt": kvb[:, :, :128].transpose(2, 1, 0).reshape(128, -1),
        "wqr": chunks(np.concatenate([rope[:, :, 0::2], rope[:, :, 1::2]], axis=2).reshape(D, -1)),
        "wkva": chunks(np.concatenate([wkva[:, :64], wkva[:, 64::2], wkva[:, 65::2]], axis=1)
                       ).reshape(128, 2, 128),
        "wvbt": kvb[:, :, 128:].transpose(2, 1, 0).reshape(128, -1),
        "wo": a["L1_attn_Wo"].reshape(NH, 128, D).transpose(1, 0, 2).reshape(128, -1),
        "baset": chunks(a["L1_ffn_base_w"].T).reshape(128, 2, 256),
        "lorab": a["L1_ffn_lora_B"].reshape(128, D),
        "loraa": chunks(a["L1_ffn_lora_A"].transpose(1, 0, 2).reshape(D, 128)).reshape(128, 2, 128),
        "routert": chunks(a["L1_ffn_router_w"].T).reshape(128, 2, 8),
    }
    nc = bacc.Bacc("TRN2", target_bir_lowering=False, num_devices=1)
    feeds, args = {}, []
    for name, v in arrays.items():
        v = np.ascontiguousarray(v)
        feeds[f"in_{name}"] = v
        args.append(nc.dram_tensor(f"in_{name}", v.shape, mybir.dt.from_np(v.dtype),
                                   kind="ExternalInput").ap())
    args.append(nc.dram_tensor("out_0", (128, NT * D), F32, kind="ExternalOutput").ap())
    build(nc, *args)
    r = run_bass_kernel_spmd(nc, [feeds], core_ids=[0])
    y = r.results[0]["out_0"]
    return y.reshape(128, NT, D).transpose(1, 0, 2).reshape(NB, T, D)
```

```python
from contextlib import ExitStack

import numpy as np

import concourse.bass as bass
from concourse import mybir

F32 = mybir.dt.float32
F32R = mybir.dt.float32r
I32 = mybir.dt.int32
ALU = mybir.AluOpType
ACT = mybir.ActivationFunctionType
AX = mybir.AxisListType

NB = 16
T = 256
D = 256
NH = 16
NT = NB * T // 128
NC = NB // 2
LN_EPS = 1e-5
RMS_EPS = 1.1920928955078125e-07
SCALE = 1.0 / float(np.sqrt(192))
BIG = 1e30
OFF_D, OFF_B2, OFF_BB, OFF_RB, OFF_KW, OFF_END = 0, 256, 512, 768, 776, 840


class Program:

    def __init__(self, nc, ctx):
        self.nc = nc
        self.ctx = ctx
        self.queue = {k: [] for k in "TVSGD"}
        self.count = {}
        self.sems = {}

    def put(self, engine, name, waits, *instructions):
        step = 16 if engine == "D" else 1
        key = f"{name}_{engine}"
        if key not in self.sems:
            self.sems[key] = self.ctx.enter_context(self.nc.semaphore(key))
            self.count[key] = 0
        self.count[key] += step
        self.queue[engine].append((list(waits), instructions, key, step))
        return key, self.count[key]

    def run(self, engine, e):
        seen = {}
        for waits, instructions, key, step in self.queue[engine]:
            for k, v in waits:
                if seen.get(k, 0) < v:
                    e.wait_ge(self.sems[k], v)
                    seen[k] = v
            for make in instructions:
                last = make(e)
            last.then_inc(self.sems[key], step)


class Ring:

    def __init__(self, buffers):
        self.buffers = buffers
        self.readers = [[] for _ in buffers]
        self.n = 0

    def take(self):
        i = self.n % len(self.buffers)
        self.n += 1
        assert self.readers[i] is not None, "taken again before its readers were named"
        r, self.readers[i] = self.readers[i], None
        return i, self.buffers[i], r

    def free(self, i, *readers):
        self.readers[i] = list(readers)


class Turns:

    def __init__(self, count, first):
        self.count = count
        self.first = first
        self.named = {}

    def readers(self, n):
        return self.first if n < self.count else self.named[n - self.count]

    def free(self, n, *readers):
        self.named[n] = list(readers)


def build(nc, x, consts, vecs, w1t, w2t, b1c, bt, ct, nuth, wqn, wkbt, wqr, wkva, wvbt, wo,
          baset, lorab, loraa, routert, out):
    ctx = ExitStack()
    with ctx:
        p = Program(nc, ctx)
        put = p.put

        def sb(name, shape, dt=F32, where=ctx):
            return where.enter_context(nc.sbuf_tensor(name, shape, dt))

        X = sb("X", [128, NT, D])
        CONST = sb("CONST", [128, 128 + 256 + 128 + 2])
        ident = CONST[:, 0:128]
        mask0 = CONST[:, 256:384]
        mask1 = CONST[:, 128:384]
        cosT = [CONST[:, 384 + 32 * q:384 + 32 * q + 32] for q in range(2)]
        sinT = [CONST[:, 448 + 32 * q:448 + 32 * q + 32] for q in range(2)]
        sgn = CONST[:, 512:513]
        sgnc = CONST[:, 513:514]
        VEC = sb("VEC", [128, OFF_END])
        rope_c = sb("rope_c", [128, 2, 2, 32])
        rope_s = sb("rope_s", [128, 2, 2, 32])
        wq_hi = sb("wq_hi", [128, 2, NH, 128], F32R)
        wq_lo = sb("wq_lo", [128, 2, NH, 128], F32R)
        wm_hi = sb("wm_hi", [128, 2, 520], F32R)
        wm_lo = sb("wm_lo", [128, 2, 520], F32R)
        woe = sb("woe", [128, 8, D])
        LB = sb("LB", [128, D])

        l0 = ExitStack()
        stage = [sb(f"stage{i}", [128, 2048], F32, l0) for i in range(3)]
        stk = sb("stk", [128, 2, 512], F32, l0)
        w1h = sb("w1h", [128, 2, 1024], F32R, l0)
        w1l = sb("w1l", [128, 2, 1024], F32R, l0)
        w2h = sb("w2h", [128, 8, D], F32R, l0)
        w2l = sb("w2l", [128, 8, D], F32R, l0)
        bh = sb("bh", [128, 2, 128], F32R, l0)
        bl = sb("bl", [128, 2, 128], F32R, l0)
        B1 = sb("B1", [128, 8], F32, l0)
        RR = sb("RR", [128, D], F32, l0)
        xn = [sb(f"xn{i}", [128, 4, D], F32, l0) for i in range(2)]
        xh = [sb(f"xh{i}", [128, 2, 512], F32R, l0) for i in range(2)]
        xl = [sb(f"xl{i}", [128, 2, 512], F32R, l0) for i in range(2)]
        hs = [sb(f"hs{i}", [128, 512], F32, l0) for i in range(2)]
        hh = [sb(f"hh{i}", [128, 512], F32R, l0) for i in range(3)]
        hl = [sb(f"hl{i}", [128, 512], F32R, l0) for i in range(3)]
        tc = sb("tc", [128, T], F32, l0)
        tsn = sb("tsn", [128, T], F32, l0)
        tci = sb("tci", [128, T], F32, l0)
        tsi = sb("tsi", [128, T], F32, l0)
        g1 = sb("g1", [128, T], F32, l0)
        g2 = sb("g2", [128, T], F32, l0)
        gs = sb("gs", [128, T], F32, l0)
        Z = [sb(f"Z{i}", [128, T], F32, l0) for i in range(2)]
        z0 = sb("z0", [128, 4, D], F32, l0)
        th0 = sb("th0", [128, 2, D], F32, l0)
        par = sb("par", [128, 64], F32, l0)
        pari = sb("pari", [128, 4], I32, l0)
        st0 = sb("st0", [128, 4, 6], F32, l0)
        mv0 = sb("mv0", [128, 4, 2], F32, l0)
        rs0 = sb("rs0", [128, 5, 4], F32, l0)
        ri0 = sb("ri0", [128, 4], I32, l0)
        l0.close()

        l1 = ExitStack()
        QT = [sb(f"QT{i}", [128, 2, NH, 128], F32, l1) for i in range(2)]
        QK = [sb(f"QK{i}", [128, 4, 128], F32, l1) for i in range(3)]
        q1b = [sb(f"q1b{i}", [128, 4, 2, 32], F32, l1) for i in range(3)]
        q2b = [sb(f"q2b{i}", [128, 4, 2, 32], F32, l1) for i in range(3)]
        SM = [sb(f"SM{i}", [128, 512], F32, l1) for i in range(3)]
        PP = [sb(f"PP{i}", [128, 512], F32, l1) for i in range(4)]
        PT = [sb(f"PT{i}", [128, 512], F32, l1) for i in range(4)]
        st_b = [sb(f"stb{i}", [128, 3, 4], F32, l1) for i in range(4)]
        oT = [sb(f"oT{i}", [128, 2, 512], F32, l1) for i in range(2)]
        yn = [sb(f"yn{i}", [128, 2, D], F32, l1) for i in range(2)]
        yh = [sb(f"yh{i}", [128, 2, T], F32R, l1) for i in range(3)]
        yl = [sb(f"yl{i}", [128, 2, T], F32R, l1) for i in range(3)]
        KV = [sb(f"KV{i}", [128, 2, 128], F32, l1) for i in range(4)]
        KT = [sb(f"KT{i}", [128, T], F32, l1) for i in range(3)]
        ML = sb("ML", [128, 2, 264], F32, l1)
        MT = sb("MT", [128, 2, 128], F32, l1)
        kr = sb("kr", [128, 4, 2, 2, 32], F32, l1)
        sq = sb("sq", [128, 2, 64], F32, l1)
        lg = sb("lg", [128, 12, 2, 8], F32, l1)
        lv = sb("lv", [128, 10, 2], F32, l1)
        st1 = sb("st1", [128, 2, 6], F32, l1)
        mv1 = sb("mv1", [128, 2, 2], F32, l1)
        rs1 = sb("rs1", [128, 5, 2], F32, l1)
        rs2 = sb("rs2", [128, 5, 2], F32, l1)
        ri1 = sb("ri1", [128, 2], I32, l1)
        ri2 = sb("ri2", [128, 2], I32, l1)
        z1 = [sb(f"z1{i}", [128, 2, D], F32, l1) for i in range(2)]
        w1b = [sb(f"w1b{i}", [128, 2, D], F32, l1) for i in range(3)]
        fo = [sb(f"fo{i}", [128, D], F32, l1) for i in range(2)]
        pr = [sb(f"pr{i}", [128, D], F32, l1) for i in range(2)]
        l1.close()

        bank = [ctx.enter_context(nc.psum_tensor(f"bank{i}", [128, 512], F32)) for i in range(8)]

        def load(name, dst, src, waits=()):
            return put("D", name, waits, lambda e: e.dma_start(dst, src))

        d_x = [None] * NC

        def load_x(c):
            d_x[c] = load(f"x{c}", X[:, 4 * c:4 * c + 4, :].rearrange("p a b -> p (a b)"),
                          x[:, 4 * c * D:(4 * c + 4) * D])

        load_x(0)
        d_const = load("const", CONST[:, :], consts)
        d_nuth = load("nuth", par[:, 0:2], nuth)
        d_w1 = load("w1", stage[0][:, :], w1t)
        d_bt = load("bt", stk[:, 0, 0:256], bt)
        d_b1 = load("b1", B1[:, :], b1c)
        d_vec = load("vec", VEC[:, :], vecs)
        d_ct = load("ct", RR[:, :], ct)
        d_w2 = load("w2", stage[1][:, :], w2t)
        load_x(1)
        d_wqr = load("wqr", stage[2][:, :], wqr)
        for c in range(2, NC):
            load_x(c)

        def split(waits, src, hi, lo, name):
            a = put("S", name + "h", waits, lambda e: e.activation(hi, src, ACT.Copy))
            b = put("V", name + "l", [*waits, a],
                    lambda e: e.tensor_tensor(lo, src, hi.bitcast(F32), ALU.subtract))
            return a, b

        def drain(steps):
            for _ in steps:
                pass

        def rsqrt(waits, v, eps, name, t, ti):
            half, y, a = t[:, 0, :], t[:, 4, :], t[:, 1, :]
            c = put("V", name, waits, lambda e: e.tensor_scalar(half, v, eps, None, ALU.add))
            c = put("V", name, [c], lambda e: e.tensor_scalar(
                ti, half.bitcast(I32), -0.5, 1597463007.0, ALU.mult, ALU.add))
            src = ti.bitcast(F32)
            yield
            for n in range(4):
                dst = y if n == 3 else t[:, 2 + n % 2, :]
                c = put("V", name, [c], lambda e, s=src: e.tensor_tensor(a, s, s, ALU.mult))
                c = put("V", name, [c], lambda e: e.tensor_tensor(a, a, half, ALU.mult))
                yield
                c = put("V", name, [c], lambda e: e.tensor_scalar(a, a, -0.5, 1.5, ALU.mult, ALU.add))
                c = put("V", name, [c], lambda e, s=src, d=dst: e.tensor_tensor(d, s, a, ALU.mult))
                src = dst
                yield
            return c

        def col(i, n=1):
            return par[:, i:i + n]

        def vp(c, f):
            return put("V", "par", c, f)

        def ts(dst, src, a, b, o1, o2=ALU.bypass):
            return lambda e: e.tensor_scalar(dst, src, a, b, o1, o2)

        def tt(dst, a, b, o):
            return lambda e: e.tensor_tensor(dst, a, b, o)

        MAGIC = 12582912.0
        LN2_HI, LN2_LO = 0.693145751953125, 1.42860682030941723212e-6
        INV_LN2 = 1.4426950408889634

        def exact_exp(c, src, dst, n, base):
            k, r, q, w = (col(base + n * i, n) for i in range(4))
            c = vp([*c], ts(r, src, -87.0, 88.0, ALU.max, ALU.min))
            c = vp([c], ts(k, r, INV_LN2, MAGIC, ALU.mult, ALU.add))
            c = vp([c], ts(k, k, MAGIC, None, ALU.subtract))
            c = vp([c], ts(w, k, LN2_HI, None, ALU.mult))
            c = vp([c], tt(r, r, w, ALU.subtract))
            c = vp([c], ts(w, k, LN2_LO, None, ALU.mult))
            c = vp([c], tt(r, r, w, ALU.subtract))
            c = vp([c], ts(q, r, 1.0 / 5040, 1.0 / 720, ALU.mult, ALU.add))
            for f in (1.0 / 120, 1.0 / 24, 1.0 / 6, 0.5, 1.0, 1.0):
                c = vp([c], tt(q, q, r, ALU.mult))
                c = vp([c], ts(q, q, f, None, ALU.add))
            c = vp([c], ts(pari[:, 0:n], k, 8388608.0, 1065353216.0, ALU.mult, ALU.add))
            return vp([c], tt(dst, q, pari[:, 0:n].bitcast(F32), ALU.mult))

        nu, en, theta = col(0), col(2), col(3)
        c = exact_exp([d_nuth], col(0, 2), col(2, 2), 2, 8)
        c = vp([c], ts(col(4), en, 1.0, -1.0, ALU.add, ALU.mult))
        c = exact_exp([c], col(4), col(5), 1, 8)
        mag = col(5)
        c = vp([c], ts(col(7), col(4), -87.0, None, ALU.is_gt))
        c = vp([c], tt(mag, mag, col(7), ALU.mult))
        c = vp([c], tt(col(6), mag, mag, ALU.mult))
        c = vp([c], ts(col(6), col(6), -1.0, 1.0, ALU.mult, ALU.add))
        gt = par[:, 16:21].unsqueeze(2)
        got = []

        def keep(steps):
            got.append((yield from steps))

        drain(keep(rsqrt([c], col(6), 0.0, "par", gt, pari[:, 0:1])))
        c = got.pop()
        c = vp([c], tt(col(6), col(6), par[:, 20:21], ALU.mult))
        gamma = col(6)
        c = vp([c], ts(col(24), theta, 0.15915494309189535, MAGIC, ALU.mult, ALU.add))
        c = vp([c], ts(col(24), col(24), MAGIC, None, ALU.subtract))
        c = vp([c], ts(col(25), theta, 0.0, None, ALU.add))
        for part in (6.28125, 0.0019340515136718750, 1.2556659146932927e-06):
            c = vp([c], ts(col(26), col(24), part, None, ALU.mult))
            c = vp([c], tt(col(25), col(25), col(26), ALU.subtract))
        PI = 3.1415925
        c = vp([c], ts(col(25), col(25), PI, -PI, ALU.min, ALU.max))
        c = vp([c], ts(col(26), col(25), -1.0, None, ALU.mult))
        c = vp([c], tt(col(26), col(25), col(26), ALU.max))
        c = vp([c], ts(col(26), col(26), -1.0, 1.5707963267948966, ALU.mult, ALU.add))
        c = put("S", "sin", [c], lambda e: e.activation(col(27, 2), col(25, 2), ACT.Sin))
        ps, pc = col(27), col(28)

        def unit(c, s, co):
            c = vp([c], tt(col(30), s, s, ALU.mult))
            c = vp([c], tt(col(31), co, co, ALU.mult))
            c = vp([c], tt(col(30), col(30), col(31), ALU.add))
            c = vp([c], ts(col(30), col(30), -0.5, 1.5, ALU.mult, ALU.add))
            c = vp([c], tt(s, s, col(30), ALU.mult))
            return vp([c], tt(co, co, col(30), ALU.mult))

        c = unit(c, ps, pc)
        c = vp([c], lambda e: e.memset(tc[:, 0:1], 1.0))
        c = vp([c], lambda e: e.memset(tsn[:, 0:1], 0.0))
        n = 1
        while n < T:
            def grow(c, n=n, ps=ps, pc=pc):
                c = vp([c], lambda e: e.tensor_scalar(g1[:, 0:n], tsn[:, 0:n], ps, None, ALU.mult))
                c = vp([c], lambda e: e.scalar_tensor_tensor(tc[:, n:2 * n], tc[:, 0:n], pc, g1[:, 0:n],
                                                             ALU.mult, ALU.subtract))
                c = vp([c], lambda e: e.tensor_scalar(g1[:, 0:n], tc[:, 0:n], ps, None, ALU.mult))
                return vp([c], lambda e: e.scalar_tensor_tensor(tsn[:, n:2 * n], tsn[:, 0:n], pc,
                                                                g1[:, 0:n], ALU.mult, ALU.add))
            c = grow(c)
            n *= 2
            if n < T:
                i = 32 + 2 * (n.bit_length() % 8)
                ns, nc_ = col(i), col(i + 1)
                c = vp([c], tt(ns, ps, pc, ALU.mult))
                c = vp([c], ts(ns, ns, 2.0, None, ALU.mult))
                c = vp([c], tt(nc_, ps, ps, ALU.mult))
                c = vp([c], ts(nc_, nc_, -2.0, 1.0, ALU.mult, ALU.add))
                c = unit(c, ns, nc_)
                ps, pc = ns, nc_
        c = vp([c], lambda e: e.tensor_scalar(tci[:, :], tc[:, :], gamma, None, ALU.mult))
        c = vp([c, d_const], lambda e: e.tensor_scalar(tsi[:, :], tsn[:, :], gamma, sgn, ALU.mult, ALU.mult))
        c = vp([c, d_ct], lambda e: e.tensor_scalar(RR[:, :], RR[:, :], sgnc, None, ALU.mult))
        k_tab = c

        st3 = stage[0][:, :].rearrange("p (k n) -> p k n", k=2)
        k_w1 = split([d_w1], st3, w1h[:, :, :], w1l[:, :, :], "w1s")
        k_b = split([d_bt], stk[:, 0, 0:256].rearrange("p (k n) -> p k n", k=2), bh[:, :, :], bl[:, :, :], "bs")
        st8 = stage[1][:, :].rearrange("p (k n) -> p k n", k=8)
        k_w2 = split([d_w2], st8, w2h[:, :, :], w2l[:, :, :], "w2s")

        tbank = Ring([bank[0]])
        fbank = Ring([bank[1], bank[2]])
        obank = [bank[3], bank[4]]
        ubank = Ring([bank[5]])
        ybank = Ring([bank[6]])
        wbank = Ring([bank[7]])
        xn_r = [[], []]
        xt_r = [[], []]
        k_xn = [None] * NC
        k_xt = [None] * NC
        turned = [None] * NC

        def l0_norm(c):
            q = c % 2
            w = [d_x[c]]
            a = put("V", "bn", w + ([k_xn[c - 1]] if c else []),
                    *[lambda e, i=i: e.bn_stats(st0[:, i, :], X[:, 4 * c + i, :]) for i in range(4)])
            a = put("V", "bn", [a], *[lambda e, i=i: e.bn_aggr(mv0[:, i, :], st0[:, i, :]) for i in range(4)])
            yield
            a = yield from rsqrt([a], mv0[:, :, 1], LN_EPS, "ln0", rs0, ri0[:, :])
            k_xn[c] = put("V", "xn", [a, *xn_r[q]], *[
                lambda e, i=i: e.tensor_scalar(xn[q][:, i, :], X[:, 4 * c + i, :], mv0[:, i, 0:1],
                                               rs0[:, 4, i:i + 1], ALU.subtract, ALU.mult)
                for i in range(4)])

        def l0_turn(c, k):
            q = c % 2
            i, bk, free = tbank.take()
            t = put("T", "tx", [k_xn[c], d_const, *free], *[
                lambda e, j=j: e.transpose(bk[:, 128 * j:128 * j + 128],
                                           xn[q][:, j, 128 * k:128 * k + 128], ident) for j in range(4)])
            h, l = split([t, *xt_r[q]], bk[:, :], xh[q][:, k, :], xl[q][:, k, :], "xt")
            tbank.free(i, h, l)
            k_xt[c] = [h, l]
            turned[c] = [t]

        def three(dst, wh, wl, mh, ml, first, last, skip=False):
            out_ = []
            for j, (a, b) in enumerate(((wl, mh), (wh, ml), (wh, mh))):
                out_.append(lambda e, a=a, b=b, j=j: e.matmul(
                    dst, a, b, start=(first and j == 0), stop=(last and j == 2), skip_group_check=skip))
            return out_

        z_k = [None] * NC
        z_r = [[], []]
        g_prev = []

        def l0_scan(c):
            nonlocal g_prev
            q = c % 2
            i, bk, free = ubank.take()
            m = []
            for k in range(2):
                m += three(bk[:, :], bh[:, k, :], bl[:, k, :], xh[q][:, k, :], xl[q][:, k, :], k == 0, k == 1)
            u = put("T", "bu", [*k_b, *k_xt[c], *free], *m)
            ks = []
            for b in range(2):
                r = slice(64 * b, 64 * b + 64)
                s = slice(256 * b, 256 * b + 256)
                ks.append(put("V", "rot", [u, k_tab, *g_prev], lambda e, r=r, s=s: e.tensor_tensor(
                    g1[r, :], bk[0:64, s], tci[r, :], ALU.mult)))
                ks.append(put("V", "rot", [], lambda e, r=r, s=s: e.tensor_tensor(
                    g2[r, :], bk[64:128, s], tsi[r, :], ALU.mult)))
            ubank.free(i, ks[-1])
            a = put("V", "rot", [ks[-1]], lambda e: e.tensor_tensor(g1[:, :], g1[:, :], g2[:, :], ALU.add))
            a = put("V", "rot", [a], lambda e: e.tensor_tensor_scan(gs[:, :], mag.broadcast_to([128, T]), g1[:, :], 0.0,
                                                                    ALU.mult, ALU.add))
            zs = []
            for b in range(2):
                r = slice(64 * b, 64 * b + 64)
                w = [a, *z_r[b]]
                put("V", "rot", w, lambda e, r=r, b=b: e.tensor_tensor(
                    Z[b][0:64, :], gs[r, :], tc[r, :], ALU.mult))
                zs.append(put("V", "rot", [], lambda e, r=r, b=b: e.tensor_tensor(
                    Z[b][64:128, :], gs[r, :], tsn[r, :], ALU.mult)))
            g_prev = [zs[-1]]
            z_k[c] = zs

        z_prev = [[], []]
        th_prev = []
        s_tok = {}

        def l0_y(c, b):
            q = c % 2
            i, bk, free = ybank.take()
            y = put("T", "y", [z_k[c][b], *free], *[
                lambda e, j=j: e.matmul(bk[:, 256 * j:256 * j + 256], Z[b][:, 128 * j:128 * j + 128],
                                        RR[:, :], start=True, stop=True) for j in range(2)])
            z_r[b] = [y]
            db = VEC[:, OFF_D:OFF_D + D].unsqueeze(1).broadcast_to([128, 2, D])
            s0 = xn[q]
            g = put("G", "dx", [k_xn[c], d_vec, *turned[c]], lambda e: e.tensor_tensor(
                s0[:, 2 * b:2 * b + 2, :], s0[:, 2 * b:2 * b + 2, :], db, ALU.mult))
            v = put("V", "sy", [y, g], lambda e: e.tensor_tensor(
                s0[:, 2 * b:2 * b + 2, :], bk[:, :].rearrange("p (a d) -> p a d", a=2),
                s0[:, 2 * b:2 * b + 2, :], ALU.add))
            ybank.free(i, v)
            s_tok[b] = v
            return g

        h_r = [[], [], []]
        hs_r = [[], []]
        k_h = {}
        hn = [0]

        def l0_up(c, hb):
            q = c % 2
            i, bk, free = fbank.take()
            m = []
            sl = slice(128 * hb, 128 * hb + 128)
            for k in range(2):
                m += three(bk[:, :], w1h[:, k, sl], w1l[:, k, sl], xh[q][:, k, :], xl[q][:, k, :],
                           k == 0, k == 1)
            t = put("T", "f1", [*k_w1, *k_xt[c], *free], *m)
            r, v = hn[0] % 3, hn[0] % 2
            hn[0] += 1
            g = put("S", "gelu", [t, d_b1, *hs_r[v]], lambda e: e.activation(
                hs[v][:, :], bk[:, :], ACT.Gelu, bias=B1[:, hb:hb + 1]))
            fbank.free(i, g)
            a, b = split([g, *h_r[r]], hs[v][:, :], hh[r][:, :], hl[r][:, :], "hs")
            hs_r[v] = [a, b]
            k_h[(c, hb)] = (r, a, b)
            return t

        z_free = []

        def l0_down(c, hb):
            nonlocal z_free
            r, a, b = k_h[(c, hb)]
            m = []
            for t in range(4):
                dst = obank[t // 2][:, 256 * (t % 2):256 * (t % 2) + 256]
                sl = slice(128 * t, 128 * t + 128)
                first = hb == 0 and t % 2 == 0
                m += three(dst, hh[r][:, sl], hl[r][:, sl], w2h[:, hb, :], w2l[:, hb, :],
                           first, hb == 7, skip=True)
            t = put("T", "f2", [a, b, *k_w2, *(z_free if hb == 0 else [])], *m)
            h_r[r] = [t]
            return t

        x1_k = [None] * NC

        def l0_out(c, t):
            nonlocal z_free, th_prev
            z_free = []
            s0 = xn[c % 2]
            for b in range(2):
                sl = slice(2 * b, 2 * b + 2)
                bb = VEC[:, OFF_B2:OFF_B2 + D].unsqueeze(1).broadcast_to([128, 2, D])
                z = put("V", "z0", [t, d_vec, *z_prev[b]], lambda e, b=b, sl=sl: e.tensor_tensor(
                    z0[:, sl, :], obank[b][:, :].rearrange("p (a d) -> p a d", a=2), bb, ALU.add))
                z_free.append(z)
            for b in range(2):
                sl = slice(2 * b, 2 * b + 2)
                xs = slice(4 * c + 2 * b, 4 * c + 2 * b + 2)
                th = put("S", "th0", [z_free[b], *th_prev], lambda e, sl=sl: e.activation(
                    th0[:, :, :], z0[:, sl, :], ACT.Tanh, scale=0.5))
                a = put("V", "x1", [th], lambda e, sl=sl: e.scalar_tensor_tensor(
                    z0[:, sl, :], th0[:, :, :], 1.0, z0[:, sl, :], ALU.add, ALU.mult))
                th_prev = [a]
                a = put("V", "x1", [a, s_tok[b]], lambda e, sl=sl: e.tensor_tensor(
                    s0[:, sl, :], s0[:, sl, :], z0[:, sl, :], ALU.mult))
                a = put("V", "x1", [a], lambda e, sl=sl, xs=xs: e.scalar_tensor_tensor(
                    X[:, xs, :], s0[:, sl, :], 0.5, X[:, xs, :], ALU.mult, ALU.add))
                z_prev[b] = [a]
            x1_k[c] = a
            xn_r[c % 2] = [a]

        free2 = {i: [] for i in range(3)}
        free2[0] = list(k_w1)
        free2[1] = list(k_w2)
        free_stk = {0: list(k_b), 1: []}
        k_w = {}

        def w_rope():
            src = stage[2][:, :].rearrange("p (k h n) -> p k h n", k=2, h=NH)
            a = put("S", "wr", [d_wqr], lambda e: e.activation(
                wq_hi[:, :, :, 64:128], src, ACT.Copy, scale=-SCALE))
            b = put("V", "wr", [a], lambda e: e.scalar_tensor_tensor(
                wq_lo[:, :, :, 64:128], src, -SCALE, wq_hi[:, :, :, 64:128].bitcast(F32),
                ALU.mult, ALU.subtract))
            free2[2] = [a, b]
            k_w["r"] = [a, b]

        d_wn = {}

        def load_nope(g):
            s = g
            d_wn[g] = [load(f"wn{g}", stage[s][:, :], wqn[:, g * 2048:(g + 1) * 2048], free2[s]),
                       load(f"wk{g}", stk[:, g, :], wkbt[:, g * 512:(g + 1) * 512], free_stk[g])]

        def w_nope(g, k):
            i, bk, free = wbank.take()
            wn = stage[g][:, :].rearrange("p (h d) -> p h d", h=8)
            t = put("T", "wn", [*d_wn[g], *free], *[
                lambda e, j=j: e.matmul(bk[:, 64 * j:64 * j + 64], wn[:, j, 128 * k:128 * k + 128],
                                        stk[:, g, 64 * j:64 * j + 64], start=True, stop=True)
                for j in range(8)])
            src = bk[:, :].rearrange("p (h n) -> p h n", h=8)
            hi, lo = (w[:, k, 8 * g:8 * g + 8, 0:64] for w in (wq_hi, wq_lo))
            a = put("S", "wn", [t], lambda e: e.activation(hi, src, ACT.Copy, scale=-SCALE))
            b = put("V", "wn", [t, a], lambda e: e.scalar_tensor_tensor(
                lo, src, -SCALE, hi.bitcast(F32), ALU.mult, ALU.subtract))
            wbank.free(i, a, b)
            free2[g] = [t]
            free_stk[g] = [t]
            k_w[("n", g, k)] = [a, b]

        d_wo = {}

        def load_o(g):
            d_wo[g] = [load(f"wo{g}", stage[g][:, :], wo[:, g * 2048:(g + 1) * 2048], free2[g]),
                       load(f"wv{g}", stk[:, g, :], wvbt[:, g * 512:(g + 1) * 512], free_stk[g])]

        def w_o(g, i2):
            i, bk, free = wbank.take()
            wv = stage[g][:, :].rearrange("p (h d) -> p h d", h=8)
            ms = []
            for j in range(2):
                for half in range(2):
                    h = 4 * half + 2 * i2 + j
                    ms.append(lambda e, j=j, half=half, h=h: e.matmul(
                        bk[64 * half:64 * half + 64, 256 * j:256 * j + 256],
                        stk[:, g, 64 * h:64 * h + 64], wv[:, h, :], start=True, stop=True))
            t = put("T", "wo", [*d_wo[g], *free], *ms)
            a = put("S", "wo", [t], lambda e: e.activation(
                woe[:, 4 * g + 2 * i2:4 * g + 2 * i2 + 2, :],
                bk[:, :].rearrange("p (j d) -> p j d", j=2), ACT.Copy))
            wbank.free(i, a)
            free2[g] = [t]
            free_stk[g] = [t]
            k_w[("o", g, i2)] = [a]

        d_wm = []

        def load_m():
            s = stage[2][:, 0:1040].rearrange("p (k n) -> p k n", k=2)
            w = free2[2]
            d_wm.append(load("wm0", s[:, :, 0:128], wkva, w))
            d_wm.append(load("wm1", s[:, :, 128:256], loraa, w))
            d_wm.append(load("wm2", s[:, :, 256:264], routert, w))
            d_wm.append(load("wm3", s[:, :, 264:520], baset, w))
            d_wm.append(load("wm4", LB[:, :], lorab))

        def w_m():
            s = stage[2][:, 0:1040].rearrange("p (k n) -> p k n", k=2)
            k_w["m"] = [*split(d_wm, s, wm_hi[:, :, :], wm_lo[:, :, :], "wm"), d_wm[-1]]

        def rope_tables():
            toks = []
            for q in range(2):
                for j in range(2):
                    toks.append(put("G", "rt", [d_const], lambda e, q=q, j=j: e.tensor_copy(
                        rope_c[:, q, j, :], cosT[q])))
                    toks.append(put("G", "rt", [], lambda e, q=q, j=j: e.tensor_scalar(
                        rope_s[:, q, j, :], sinT[q], 1.0 if j == 0 else -1.0, 1.0, ALU.mult, ALU.mult)))
            return toks[-1]

        k_rt = rope_tables()

        fill = {
            (1, 1): w_rope,
            (1, 3): lambda: (load_nope(0), load_nope(1), load_m()),
            (2, 4): lambda: w_nope(0, 0), (2, 6): lambda: w_nope(0, 1),
            (3, 1): lambda: w_nope(1, 0), (3, 3): lambda: w_nope(1, 1),
            (3, 4): w_m,
            (3, 5): lambda: (load_o(0), load_o(1)),
            (5, 1): lambda: w_o(0, 0), (5, 4): lambda: w_o(0, 1),
            (6, 1): lambda: w_o(1, 0), (6, 4): lambda: w_o(1, 1),
        }

        drain(l0_norm(0))
        l0_turn(0, 0)
        l0_turn(0, 1)
        l0_scan(0)
        for c in range(NC):
            for hb in range(9):
                if hb < 8:
                    t = l0_up(c, hb)
                    if hb == 7:
                        last_up = t
                if hb == 0:
                    norm = l0_norm(c + 1) if c + 1 < NC else iter(())
                for _ in range(4 if hb < 4 else 0):
                    next(norm, None)
                if hb == 1:
                    l0_y(c, 0)
                if hb == 3:
                    l0_y(c, 1)
                if c + 1 < NC:
                    if hb == 4:
                        l0_turn(c + 1, 0)
                    if hb == 5:
                        l0_turn(c + 1, 1)
                    if hb == 7:
                        l0_scan(c + 1)
                if hb >= 1:
                    d = l0_down(c, hb - 1)
                if (c, hb) in fill:
                    fill[(c, hb)]()
            xt_r[c % 2] = [last_up]
            l0_out(c, d)
        end0 = [x1_k[NC - 1], ("f2_T", p.count["f2_T"]), ("hsl_V", p.count["hsl_V"]),
                ("hsh_S", p.count["hsh_S"]), ("th0_S", p.count["th0_S"]), ("dx_G", p.count["dx_G"]),
                ("y_T", p.count["y_T"]), ("wo_T", p.count["wo_T"]), ("wo_S", p.count["wo_S"]),
                ("wml_V", p.count["wml_V"]), ("wmh_S", p.count["wmh_S"])]
        pj = Ring([bank[1], bank[2]])
        tb = Ring([bank[0], bank[7]])
        sbk = Ring([bank[5], bank[6]])
        bsk, obk = bank[3], bank[4]
        for r_ in (pj, tb, sbk):
            for i in range(len(r_.buffers)):
                r_.free(i, *end0)
        bs_free, ob_free = [*end0], [*end0]
        qk = Ring(list(zip(QK, q1b, q2b)))
        sm, pp, pt = Ring(SM), Ring(PP), Ring(PT)
        for r_ in (qk, sm, pp, pt):
            for i in range(len(r_.buffers)):
                r_.free(i, *end0)
        B = {}

        def flip(n):
            return "S" if n % 2 == 0 else "V"

        def copy(eng, name, waits, dst, src):
            if eng == "S":
                return put("S", name, waits, lambda e: e.activation(dst, src, ACT.Copy))
            return put("V", name, waits, lambda e: e.tensor_copy(dst, src))

        r_yn, r_qt, r_z = (Turns(2, end0) for _ in range(3))
        r_kt, r_yx, r_w = (Turns(3, end0) for _ in range(3))
        r_kv = Turns(4, end0)
        r_mlt, r_mt, r_ln = (Turns(1, end0) for _ in range(3))
        r_ot, r_fo = [Turns(1, end0) for _ in range(2)], [Turns(1, end0) for _ in range(2)]

        def l1_norm(b):
            q = b % 2
            a = put("V", "bn1", [x1_k[b // 2], *end0, *r_ln.readers(b)],
                    *[lambda e, i=i: e.bn_stats(st1[:, i, :], X[:, 2 * b + i, :]) for i in range(2)])
            yield
            a = put("V", "bn1", [a], *[lambda e, i=i: e.bn_aggr(mv1[:, i, :], st1[:, i, :])
                                       for i in range(2)])
            yield
            a = yield from rsqrt([a], mv1[:, :, 1], LN_EPS, "ln1", rs1, ri1[:, :])
            k = put("V", "yn", [a, *r_yn.readers(b)], *[
                lambda e, i=i: e.tensor_scalar(yn[q][:, i, :], X[:, 2 * b + i, :], mv1[:, i, 0:1],
                                               rs1[:, 4, i:i + 1], ALU.subtract, ALU.mult)
                for i in range(2)])
            r_ln.free(b, k)
            B[b] = {"yn": k, "qt": {}}

        def l1_turn(b):
            q = b % 2
            i, bk, free = tb.take()
            t = put("T", "ty", [B[b]["yn"], *free], *[
                lambda e, k=k, j=j: e.transpose(bk[:, 256 * k + 128 * j:256 * k + 128 * j + 128],
                                                yn[q][:, j, 128 * k:128 * k + 128], ident)
                for k in range(2) for j in range(2)])
            src = bk[:, :].rearrange("p (k n) -> p k n", k=2)
            hi, lo = yh[b % 3][:, :, :], yl[b % 3][:, :, :]
            h = put("S", "yth", [t, *r_yx.readers(b)], lambda e: e.activation(hi, src, ACT.Copy))
            r_yn.free(b, t)

            def low():
                l = put("V", "ytl", [t, h, *r_yx.readers(b)],
                        lambda e: e.tensor_tensor(lo, src, hi.bitcast(F32), ALU.subtract))
                tb.free(i, h, l)
                B[b]["yt"] = [h, l]
            later(low)

        def l1_misc(b, t):
            nonlocal bs_free
            q = b % 2
            sl = slice(128 * t, 128 * t + 128)
            i, bk, free = pj.take()
            m = []
            for k in range(2):
                m += three(bk[:, 0:264], yh[b % 3][:, k, sl], yl[b % 3][:, k, sl], wm_hi[:, k, 0:264],
                           wm_lo[:, k, 0:264], k == 0, k == 1)
            a = put("T", "mi", [*B[b]["yt"], *k_w["m"], *free], *m)
            c_ = put("S", "mi", [a, *r_mlt.readers(b)], lambda e: e.activation(
                ML[:, t, :], bk[:, 0:264], ACT.Copy))
            pj.free(i, c_)
            m = []
            for k in range(2):
                m += three(bsk[:, 256 * t:256 * t + 256], yh[b % 3][:, k, sl], yl[b % 3][:, k, sl],
                           wm_hi[:, k, 264:520], wm_lo[:, k, 264:520], t == 0 and k == 0, False,
                           skip=True)
            put("T", "ba", bs_free if t == 0 else [], *m)
            B[b][("mi", t)] = c_

        def vk(c, f, name="kv"):
            return put("V", name, c, f)

        def l1_kv(b):
            q = b % 2
            w = [B[b][("mi", 0)], B[b][("mi", 1)]]
            r = ML[:, :, 64:128].rearrange("p t (j n) -> p t j n", j=2)
            g = put("G", "kr", [*w, k_rt, *r_mlt.readers(b)], lambda e: e.tensor_tensor(
                kr[:, 0:2, 0, :, :], r, rope_c[:, :, :, :], ALU.mult))
            g = put("G", "kr", [g], lambda e: e.tensor_tensor(
                kr[:, 2:4, 0, :, :], r, rope_s[:, :, :, :], ALU.mult))
            gg = put("G", "kr", [g, *r_kv.readers(b)], *[
                lambda e, j=j: e.tensor_tensor(KV[b % 4][:, :, 64 + 32 * j:96 + 32 * j], kr[:, 0:2, 0, j, :],
                                               kr[:, 2:4, 0, 1 - j, :], ALU.add) for j in range(2)])
            cl = ML[:, :, 0:64]
            a = vk(w, lambda e: e.tensor_tensor(sq[:, :, :], cl, cl, ALU.mult))
            yield
            a = vk([a], lambda e: e.tensor_reduce(lv[:, 0, :], sq[:, :, :], AX.X, ALU.add))
            a = vk([a], lambda e: e.tensor_scalar(lv[:, 1, :], lv[:, 0, :], 1.0 / 64, None, ALU.mult))
            yield
            a = yield from rsqrt([a], lv[:, 1, :], RMS_EPS, "rms", rs2, ri2[:, :])
            kw = VEC[:, OFF_KW:OFF_KW + 64]
            a = put("V", "kvw", [a, *r_kv.readers(b)], *[
                lambda e, t=t: e.scalar_tensor_tensor(KV[b % 4][:, t, 0:64], ML[:, t, 0:64],
                                                      rs2[:, 4, t:t + 1], kw, ALU.mult, ALU.mult)
                for t in range(2)])
            yield
            i, bk, free = tb.take()
            t = put("T", "tk", [a, gg, *free], *[
                lambda e, j=j: e.transpose(bk[:, 128 * j:128 * j + 128], KV[b % 4][:, j, :], ident)
                for j in range(2)])
            k = put("S", "kt", [t, *r_kt.readers(b)], lambda e: e.activation(
                KT[b % 3][:, :], bk[:, 0:256], ACT.Copy))
            tb.free(i, k)
            B[b]["kt"] = k
            B[b]["kv"] = [a, gg]
            B[b]["tk"] = t

        def l1_gate(b):
            w = [B[b][("mi", 0)], B[b][("mi", 1)], *r_mlt.readers(b)]
            L, E1, K1, L2, E2, SG, CT_ = (lg[:, i, :, :] for i in range(7))
            n = "gt"

            def bc(v):
                return v.unsqueeze(2).broadcast_to([128, 2, 8])

            def first_of(c, src, top, hot):
                c = vk(c, lambda e: e.tensor_reduce(top, src, AX.X, ALU.max), n)
                c = vk([c], lambda e: e.tensor_tensor(hot, src, bc(top), ALU.is_equal), n)
                yield
                c = vk([c], lambda e: e.tensor_tensor(hot, hot, ramp, ALU.mult), n)
                c = vk([c], lambda e: e.tensor_reduce(lv[:, 4, :], hot, AX.X, ALU.max), n)
                yield
                return vk([c], lambda e: e.tensor_tensor(hot, ramp, bc(lv[:, 4, :]), ALU.is_equal), n)

            rb = VEC[:, OFF_RB:OFF_RB + 8].unsqueeze(1).broadcast_to([128, 2, 8])
            c_ = vk(w, lambda e: e.tensor_tensor(L, ML[:, :, 256:264], rb, ALU.add), n)
            c_ = yield from first_of([c_, k_ramp], L, lv[:, 2, :], E1)
            c_ = vk([c_], lambda e: e.scalar_tensor_tensor(L2, E1, -3e38, L, ALU.mult, ALU.add), n)
            yield
            c_ = yield from first_of([c_], L2, lv[:, 3, :], E2)
            c_ = vk([c_], lambda e: e.tensor_tensor(E1, E1, E2, ALU.add), n)
            c_ = vk([c_], lambda e: e.tensor_tensor(L2, L, bc(lv[:, 2, :]), ALU.subtract), n)
            yield
            yield
            c_ = put("S", "gt", [c_], lambda e: e.activation(L2, L2, ACT.Exp))
            for _ in range(6):
                yield
            c_ = vk([c_], lambda e: e.tensor_tensor(E1, E1, L2, ALU.mult), n)
            c_ = vk([c_], lambda e: e.tensor_reduce(lv[:, 5, :], E1, AX.X, ALU.add), n)
            yield
            c_ = vk([c_], lambda e: e.reciprocal(lv[:, 6, :], lv[:, 5, :]), n)
            c_ = vk([c_], lambda e: e.scalar_tensor_tensor(E1, E1, 2.0, bc(lv[:, 6, :]), ALU.mult, ALU.mult), n)
            yield
            c_ = vk([c_], lambda e, t=0: e.tensor_tensor(
                ML[:, t, 128:256].rearrange("p (x r) -> p x r", x=8),
                ML[:, t, 128:256].rearrange("p (x r) -> p x r", x=8),
                E1[:, t, :].unsqueeze(2).broadcast_to([128, 8, 16]), ALU.mult), n)
            c_ = vk([c_], lambda e: e.tensor_tensor(
                ML[:, 1, 128:256].rearrange("p (x r) -> p x r", x=8),
                ML[:, 1, 128:256].rearrange("p (x r) -> p x r", x=8),
                E1[:, 1, :].unsqueeze(2).broadcast_to([128, 8, 16]), ALU.mult), n)
            for _ in range(4):
                yield
            i, bk, free = tb.take()
            t = put("T", "tm", [c_, *free], *[
                lambda e, j=j: e.transpose(bk[:, 128 * j:128 * j + 128], ML[:, j, 128:256], ident)
                for j in range(2)])
            k = put("S", "mt", [t, *r_mt.readers(b)], lambda e: e.activation(
                MT[:, :, :], bk[:, 0:256].rearrange("p (t n) -> p t n", t=2), ACT.Copy))
            tb.free(i, k)
            B[b]["mt"] = k
            r_mlt.free(b, t, *B[b]["kv"])

        def l1_lora(b):
            nonlocal bs_free
            q = b % 2
            m = put("T", "lo", [B[b]["mt"], *k_w["m"]], *[
                lambda e, t=t: e.matmul(bsk[:, 256 * t:256 * t + 256], MT[:, t, :], LB[:, :],
                                        start=False, stop=True, skip_group_check=True)
                for t in range(2)])
            r_mt.free(b, m)
            bb = VEC[:, OFF_BB:OFF_BB + D].unsqueeze(1).broadcast_to([128, 2, D])
            z = put("V", "z1", [m, *r_z.readers(b)], lambda e: e.tensor_tensor(
                z1[q][:, :, :], bsk[:, :].rearrange("p (t d) -> p t d", t=2), bb, ALU.add))
            bs_free = [z]
            th = put("S", "th1", [z, *r_w.readers(b)], lambda e: e.activation(
                w1b[b % 3][:, :, :], z1[q][:, :, :], ACT.Tanh, scale=0.5))

            def weigh():
                B[b]["w"] = put("V", "w1", [th], lambda e: e.scalar_tensor_tensor(
                    w1b[b % 3][:, :, :], w1b[b % 3][:, :, :], 1.0, z1[q][:, :, :], ALU.add, ALU.mult))
                r_z.free(b, B[b]["w"])
            later(weigh)

        def l1_q(b, t, g):
            q = b % 2
            sl = slice(128 * t, 128 * t + 128)
            i, bk, free = pj.take()
            m = []
            for k in range(2):
                m += three(bk[:, :], yh[b % 3][:, k, sl], yl[b % 3][:, k, sl],
                           wq_hi[:, k, 4 * g:4 * g + 4, :], wq_lo[:, k, 4 * g:4 * g + 4, :],
                           k == 0, k == 1)
            wk = [*k_w["r"]]
            for kk in range(2):
                wk += k_w[("n", g // 2, kk)]
            a = put("T", "q", [*B[b]["yt"], *wk, *free], *m)
            if t == 1 and g == 3:
                r_yx.free(b, a)
            v = bk[:, :].rearrange("p (h n) -> p h n", h=4)
            ro = v[:, :, 64:128].rearrange("p h (j n) -> p h j n", j=2)
            n, (Q, t1, t2), fr = qk.take()
            c1 = put("S", "q", [a, *fr], lambda e: e.activation(Q[:, :, 0:64], v[:, :, 0:64], ACT.Copy))
            cb = rope_c[:, t, :, :].rearrange("p j n -> p (j n)").unsqueeze(1).broadcast_to([128, 4, 64])
            sb2 = rope_s[:, t, :, :].rearrange("p j n -> p (j n)").unsqueeze(1).broadcast_to([128, 4, 64])
            rf = v[:, :, 64:128]
            t1f = t1[:, :, :, :].rearrange("p h j n -> p h (j n)")
            t2f = t2[:, :, :, :].rearrange("p h j n -> p h (j n)")
            c2 = put("V", "q", [a, k_rt, c1, *fr],
                     lambda e: e.tensor_tensor(t1f, rf, cb, ALU.mult),
                     lambda e: e.tensor_tensor(t2f, rf, sb2, ALU.mult))
            pj.free(i, c1, c2)
            c3 = put("G", "q", [c2, *fr], *[
                lambda e, j=j: e.tensor_tensor(Q[:, :, 64 + 32 * j:96 + 32 * j], t1[:, :, j, :],
                                               t2[:, :, 1 - j, :], ALU.add) for j in range(2)])
            B[b][("q", t, g)] = (n, Q, c1, c3)

        def l1_qt(b, t, g):
            q = b % 2
            n, Q, c1, c3 = B[b][("q", t, g)]
            i, bk, free = tb.take()
            tr = put("T", "tq", [c1, c3, *free], *[
                lambda e, j=j: e.transpose(bk[:, 128 * j:128 * j + 128], Q[:, j, :], ident)
                for j in range(4)])
            qk.free(n, tr)
            e_ = copy(flip(g), "qt", [tr, *r_qt.readers(b)],
                      QT[q][:, t, 4 * g:4 * g + 4, :].rearrange("p h n -> p (h n)"), bk[:, :])
            tb.free(i, e_)
            B[b]["qt"][(t, g)] = e_

        def pair(pi):
            if pi < 2:
                return 0, [[8 * pi + i for i in range(4)], [8 * pi + 4 + i for i in range(4)]]
            hgrp, two = (pi - 2) // 2, (pi - 2) % 2
            return 1, [[8 * hgrp + 4 * hf + 2 * two + i for i in range(2)] for hf in range(2)]

        st_ring = Ring(st_b)
        for i in range(4):
            st_ring.free(i, *end0)

        def l1_s(b, pi, hf):
            q = b % 2
            qt, heads = pair(pi)
            hd = heads[hf]
            nk = 128 * (qt + 1)
            i, bk, free = sbk.take()
            w = [B[b]["qt"][(qt, h // 4)] for h in hd]
            s = put("T", "s", [B[b]["kt"], *w, *free], *[
                lambda e, j=j, h=h: e.matmul(bk[:, nk * j:nk * j + nk], QT[q][:, qt, h, :],
                                             KT[b % 3][:, 0:nk], start=True, stop=True)
                for j, h in enumerate(hd)])
            if (pi, hf) == (5, 1):
                r_kt.free(b, s)
                r_qt.free(b, s)
            mi, M_, mf = sm.take()
            si, S_, sf = st_ring.take()
            mk = mask1 if qt else mask0
            a = put("V", "s", [s, *mf, *sf], *[
                lambda e, j=j: e.tensor_tensor_reduce(
                    M_[:, nk * j:nk * j + nk], bk[:, nk * j:nk * j + nk], mk, 1.0, 3e38,
                    ALU.add, ALU.min, S_[:, 0, j:j + 1]) for j in range(len(hd))])
            sbk.free(i, a)
            B[b][("s", pi, hf)] = s
            n = len(hd)

            def exps():
                pi_, P_, pf = pp.take()
                x_ = put("S", "p", [a, *pf], *[
                    lambda e, j=j: e.activation(P_[:, nk * j:nk * j + nk], M_[:, nk * j:nk * j + nk],
                                                ACT.Exp, bias=S_[:, 0, j:j + 1], scale=-1.0,
                                                accum_out=S_[:, 1, j:j + 1]) for j in range(n)])
                sm.free(mi, x_)

                def norms():
                    r = put("V", "r", [x_], lambda e: e.reciprocal(S_[:, 2, 0:n], S_[:, 1, 0:n]))
                    g = put("G", "n", [r], *[
                        lambda e, j=j: e.tensor_scalar(P_[:, nk * j:nk * j + nk], P_[:, nk * j:nk * j + nk],
                                                       S_[:, 2, j:j + 1], 1.0, ALU.mult, ALU.mult)
                        for j in range(n)])
                    st_ring.free(si, g)
                    B[b][("p", pi, hf)] = (pi_, P_, g)
                later(norms)
            later(exps)

        nev = [0]

        def l1_pt(b, pi, hf):
            qt, heads = pair(pi)
            pi_, P_, g = B[b][("p", pi, hf)]
            i, bk, free = tb.take()
            if qt == 0:
                spans = [(128 * j, 128 * j) for j in range(4)]
            else:
                spans = [(256 * kb + 128 * j, 256 * j + 128 * kb) for kb in range(2) for j in range(2)]
            t = put("T", "tp", [g, *free], *[
                lambda e, d=d, s=s: e.transpose(bk[:, d:d + 128], P_[:, s:s + 128], ident)
                for d, s in spans])
            pp.free(pi_, t)
            ti, T_, tf = pt.take()
            nev[0] += 1
            e_ = copy("V" if nev[0] % 3 == 0 else "S", "pt", [t, *tf], T_[:, :], bk[:, :])
            tb.free(i, e_)
            B[b][("t", pi, hf)] = (ti, T_, e_)

        def l1_pv(b, pi):
            nonlocal ob_free
            q = b % 2
            qt, heads = pair(pi)
            tk = [B[b][("t", pi, hf)] for hf in range(2)]
            first = pi < 2 or pi % 2 == 0
            ms = []
            for kb in range(qt + 1):
                for hf in range(2):
                    T_ = tk[hf][1]
                    if qt == 0:
                        dst, src = slice(0, 512), slice(0, 512)
                    else:
                        o = 128 * (heads[hf][0] % 4)
                        dst, src = slice(o, o + 256), slice(256 * kb, 256 * kb + 256)
                    ms.append(lambda e, kb=kb, hf=hf, T_=T_, dst=dst, src=src: e.matmul(
                        obk[64 * hf:64 * hf + 64, dst], KV[b % 4][:, kb, 0:64], T_[:, src],
                        start=(kb == 0), stop=(kb == qt), skip_group_check=True))
            m = put("T", "pv", [tk[0][2], tk[1][2], *B[b]["kv"], *(ob_free if first else [])], *ms)
            for hf in range(2):
                pt.free(tk[hf][0], m)
            if pi < 2 or pi % 2 == 1:
                H = heads[0][0] // 8
                e_ = copy("S" if H else "V", "ot", [m, *r_ot[qt].readers(b)], oT[qt][:, H, :], obk[:, :])
                ob_free = [e_]
                B[b][("o", qt, H)] = e_
            if pi == 5:
                r_kv.free(b, m, B[b]["tk"])

        d_out = []

        def l1_out(b, qt):
            q = b % 2
            i, bk, free = pj.take()
            wk = [t for g in range(2) for i2 in range(2) for t in k_w[("o", g, i2)]]
            m = put("T", "o", [B[b][("o", qt, 0)], B[b][("o", qt, 1)], *wk, *free], *[
                lambda e, c=c: e.matmul(bk[:, 0:256], oT[qt][:, c // 4, 128 * (c % 4):128 * (c % 4) + 128],
                                        woe[:, c, :], start=(c == 0), stop=(c == 7)) for c in range(8)])
            r_ot[qt].free(b, m)
            a = put("V", "o", [m, B[b]["w"], *r_fo[qt].readers(b)], lambda e: e.tensor_tensor(
                pr[qt][:, :], bk[:, 0:256], w1b[b % 3][:, qt, :], ALU.mult))
            pj.free(i, a)
            f = put("V", "o", [a], lambda e: e.scalar_tensor_tensor(
                fo[qt][:, :], pr[qt][:, :], 0.5, X[:, 2 * b + qt, :], ALU.mult, ALU.add))
            if qt == 1:
                r_w.free(b, f)
            n = 2 * b + qt
            d = put("D", f"out{qt}", [f], lambda e: e.dma_start(out[:, n * D:(n + 1) * D], fo[qt][:, :]))
            r_fo[qt].free(b, d)
            d_out.append(d)

        def ramp_make():
            c_ = []
            for j in range(8):
                c_.append(put("G", "ra", end0, lambda e, j=j: e.memset(lg[:, 11, :, j:j + 1], 8.0 - j)))
            return c_[-1]

        k_ramp = ramp_make()
        ramp = lg[:, 11, :, :]

        waiting = []

        def later(f):
            waiting.append(f)

        def start_step():
            now, waiting[:] = list(waiting), []
            for f in now:
                f()

        def at_once(*fs):
            for f in fs:
                f()
                start_step()

        drain(l1_norm(0))
        at_once(lambda: l1_turn(0), lambda: l1_misc(0, 0), lambda: l1_misc(0, 1))
        drain(l1_norm(1))
        at_once(lambda: l1_q(0, 0, 0), lambda: l1_turn(1))
        drain(l1_kv(0))
        for u in range(1, 8):
            l1_q(0, u // 4, u % 4)
            l1_qt(0, (u - 1) // 4, (u - 1) % 4)
        l1_qt(0, 1, 3)
        drain(l1_gate(0))
        at_once(lambda: l1_lora(0), lambda: l1_misc(1, 0), lambda: l1_misc(1, 1))
        drain(l1_kv(1))

        Q_AT = {0: 0, 1: 1, 2: 2, 3: 3, 4: 4, 7: 5, 8: 6, 9: 7}
        QT_AT = {1: 0, 2: 1, 3: 2, 4: 3, 5: 4, 8: 5, 9: 6, 10: 7}
        units = [(b, pi, hf) for b in range(NB) for pi in range(6) for hf in range(2)]
        LAG_T, LAG_V, LAG_O = 3, 5, 7
        total = len(units)
        threads = []
        for n in range(total + LAG_O + 1):
            now, m = n // 12, n % 12
            nxt, far = now + 1, now + 2
            start_step()
            if n < total:
                if m == 0 and nxt < NB:
                    threads.append((l1_gate(nxt), 6))
                if m == 1 and far < NB:
                    threads.append((l1_norm(far), 4))
                if m == 9 and far < NB:
                    threads.append((l1_kv(far), 6))
            for g, per in threads:
                for _ in range(per):
                    next(g, None)
            if n < total:
                l1_s(*units[n])
                if nxt < NB:
                    if m in Q_AT:
                        l1_q(nxt, Q_AT[m] // 4, Q_AT[m] % 4)
                    if m in QT_AT:
                        l1_qt(nxt, QT_AT[m] // 4, QT_AT[m] % 4)
                    if m == 6:
                        l1_lora(nxt)
                if far < NB:
                    if m == 6:
                        l1_turn(far)
                    if m == 7:
                        l1_misc(far, 0)
                    if m == 8:
                        l1_misc(far, 1)
            if 0 <= n - LAG_T < total:
                l1_pt(*units[n - LAG_T])
            if 0 <= n - LAG_V < total and units[n - LAG_V][2] == 1:
                b, pi, hf = units[n - LAG_V]
                l1_pv(b, pi)
            if 0 <= n - LAG_O < total:
                b, pi, hf = units[n - LAG_O]
                if (pi, hf) == (1, 1):
                    l1_out(b, 0)
                if (pi, hf) == (5, 1):
                    l1_out(b, 1)

        block = ctx.enter_context(nc.Block())

        @block.sync
        def _(e):
            p.run("D", e)
            for k in ("out0_D", "out1_D"):
                e.wait_ge(p.sems[k], p.count[k])

        @block.tensor
        def _(e):
            p.run("T", e)

        @block.vector
        def _(e):
            p.run("V", e)

        @block.scalar
        def _(e):
            p.run("S", e)

        @block.gpsimd
        def _(e):
            p.run("G", e)


def shape_constants():
    c = np.zeros((128, 514), np.float32)
    c[:, 0:128] = np.eye(128)
    i = np.arange(128)
    c[:, 256:384] = np.where(i[None, :] > i[:, None], BIG, 0.0)
    freqs = (np.float32(1.0) / np.power(np.float32(10000.0), np.arange(0, 64, 2, dtype=np.float32)
                                        / np.float32(64))).astype(np.float32)
    t = (np.arange(T, dtype=np.float32)[:, None] * freqs[None, :]).astype(np.float32)
    for q in range(2):
        a = t[128 * q:128 * q + 128].astype(np.float64)
        c[:, 384 + 32 * q:416 + 32 * q] = np.cos(a)
        c[:, 448 + 32 * q:480 + 32 * q] = np.sin(a)
    quad = i // 32
    c[:, 512] = np.where(quad % 2 == 0, 1.0, -1.0)
    c[:, 513] = np.where(quad == 0, 1.0, -1.0)
    return c


def kernel(**inputs):
    import concourse.bacc as bacc
    from concourse.bass_utils import run_bass_kernel_spmd

    a = {k: np.asarray(v) for k, v in inputs.items()}

    def chunks(w):
        k = w.shape[0] // 128
        return w.reshape(k, 128, -1).transpose(1, 0, 2).reshape(128, -1)

    wq = a["L1_attn_Wq"].reshape(D, NH, 192)
    kvb = a["L1_attn_Wkv_b"].reshape(64, NH, 256)
    rope = wq[:, :, 128:]
    wkva = a["L1_attn_Wkv_a"]
    bre, bim = a["L0_attn_B_re"].T, a["L0_attn_B_im"].T
    cre, cim = a["L0_attn_C_re"].T, a["L0_attn_C_im"].T
    vecs = np.concatenate([a["L0_attn_D"], a["L0_ffn_proj2_bias"], a["L1_ffn_base_b"],
                           a["L1_ffn_router_b"], a["L1_attn_kv_norm_w"]])
    nuth = np.stack([a["L0_attn_nu_log"], a["L0_attn_theta_log"]], axis=1)
    arrays = {
        "x": a["L0_attn_x"].reshape(NT, 128, D).transpose(1, 0, 2).reshape(128, -1),
        "consts": shape_constants(),
        "vecs": np.tile(vecs[None, :], (128, 1)),
        "w1t": chunks(a["L0_ffn_proj1"].T),
        "w2t": chunks(a["L0_ffn_proj2"].T),
        "b1c": a["L0_ffn_proj1_bias"].reshape(8, 128).T,
        "bt": chunks(np.concatenate([bre, bim, bim, bre], axis=1)),
        "ct": np.concatenate([cre, cim, cim, cre], axis=0),
        "nuth": np.tile(nuth, (4, 1)),
        "wqn": wq[:, :, :128].transpose(2, 1, 0).reshape(128, -1),
        "wkbt": kvb[:, :, :128].transpose(2, 1, 0).reshape(128, -1),
        "wqr": chunks(np.concatenate([rope[:, :, 0::2], rope[:, :, 1::2]], axis=2).reshape(D, -1)),
        "wkva": chunks(np.concatenate([wkva[:, :64], wkva[:, 64::2], wkva[:, 65::2]], axis=1)
                       ).reshape(128, 2, 128),
        "wvbt": kvb[:, :, 128:].transpose(2, 1, 0).reshape(128, -1),
        "wo": a["L1_attn_Wo"].reshape(NH, 128, D).transpose(1, 0, 2).reshape(128, -1),
        "baset": chunks(a["L1_ffn_base_w"].T).reshape(128, 2, 256),
        "lorab": a["L1_ffn_lora_B"].reshape(128, D),
        "loraa": chunks(a["L1_ffn_lora_A"].transpose(1, 0, 2).reshape(D, 128)).reshape(128, 2, 128),
        "routert": chunks(a["L1_ffn_router_w"].T).reshape(128, 2, 8),
    }
    nc = bacc.Bacc("TRN2", target_bir_lowering=False, num_devices=1)
    feeds, args = {}, []
    for name, v in arrays.items():
        v = np.ascontiguousarray(v)
        feeds[f"in_{name}"] = v
        args.append(nc.dram_tensor(f"in_{name}", v.shape, mybir.dt.from_np(v.dtype),
                                   kind="ExternalInput").ap())
    args.append(nc.dram_tensor("out_0", (128, NT * D), F32, kind="ExternalOutput").ap())
    build(nc, *args)
    r = run_bass_kernel_spmd(nc, [feeds], core_ids=[0])
    y = r.results[0]["out_0"]
    return y.reshape(128, NT, D).transpose(1, 0, 2).reshape(NB, T, D)
```

```python
from contextlib import ExitStack

import numpy as np

import concourse.bass as bass
from concourse import mybir

F32 = mybir.dt.float32
F32R = mybir.dt.float32r
I32 = mybir.dt.int32
ALU = mybir.AluOpType
ACT = mybir.ActivationFunctionType
AX = mybir.AxisListType

NB = 16
T = 256
D = 256
NH = 16
NT = NB * T // 128
NC = NB // 2
LN_EPS = 1e-5
RMS_EPS = 1.1920928955078125e-07
SCALE = 1.0 / float(np.sqrt(192))
BIG = 1e30
OFF_D, OFF_B2, OFF_BB, OFF_RB, OFF_KW, OFF_END = 0, 256, 512, 768, 776, 840


PLAN = {"order": (0, 2, 3, 1, 4, 5), "lags": (4, 6, 8), "q": (0, 1, 3, 4, 6, 7, 9, 11), "lora": 8,
        "gate": 1, "norm": 1, "turn": 6, "misc": (8, 9), "kv": 10, "rates": (1, 2, 2),
        "exp": 6, "tk": 14, "tm": 16, "l0": (5, 6), "tables": 4, "sine": 2, "first": 4}


class Program:

    def __init__(self, nc, ctx):
        self.nc = nc
        self.ctx = ctx
        self.queue = {k: [] for k in "TVSGD"}
        self.count = {}
        self.sems = {}

    def put(self, engine, name, waits, *instructions):
        step = 16 if engine == "D" else 1
        key = f"{name}_{engine}"
        if key not in self.sems:
            self.sems[key] = self.ctx.enter_context(self.nc.semaphore(key))
            self.count[key] = 0
        self.count[key] += step
        self.queue[engine].append((list(waits), instructions, key, step))
        return key, self.count[key]

    def run(self, engine, e):
        seen = {}
        for waits, instructions, key, step in self.queue[engine]:
            for k, v in waits:
                if seen.get(k, 0) < v:
                    e.wait_ge(self.sems[k], v)
                    seen[k] = v
            for make in instructions:
                last = make(e)
            last.then_inc(self.sems[key], step)


class Ring:

    def __init__(self, buffers):
        self.buffers = buffers
        self.readers = [[] for _ in buffers]
        self.n = 0

    def take(self):
        i = self.n % len(self.buffers)
        self.n += 1
        assert self.readers[i] is not None, "taken again before its readers were named"
        r, self.readers[i] = self.readers[i], None
        return i, self.buffers[i], r

    def free(self, i, *readers):
        self.readers[i] = list(readers)


class Turns:

    def __init__(self, count, first):
        self.count = count
        self.first = first
        self.named = {}

    def readers(self, n):
        return self.first(n) if n < self.count else self.named[n - self.count]

    def free(self, n, *readers):
        self.named[n] = list(readers)


def build(nc, x, consts, rows, vecs, w1t, w2t, b1c, bt, ct, nuth, wqn, wkbt, wqr, wkva, wvbt, wo,
          baset, lorab, loraa, routert, out):
    ctx = ExitStack()
    with ctx:
        p = Program(nc, ctx)
        put = p.put

        def sb(name, shape, dt=F32, where=ctx):
            return where.enter_context(nc.sbuf_tensor(name, shape, dt))

        X = sb("X", [128, NT, D])
        CONST = sb("CONST", [128, 128 + 256 + 128 + 2])
        ident = CONST[:, 0:128]
        mask0 = CONST[:, 256:384]
        mask1 = CONST[:, 128:384]
        cosT = [CONST[:, 384 + 32 * q:384 + 32 * q + 32] for q in range(2)]
        sinT = [CONST[:, 448 + 32 * q:448 + 32 * q + 32] for q in range(2)]
        sgn = CONST[:, 512:513]
        sgnc = CONST[:, 513:514]
        VEC = sb("VEC", [128, OFF_END])
        rope_c = sb("rope_c", [128, 2, 2, 32])
        rope_s = sb("rope_s", [128, 2, 2, 32])
        wq_hi = sb("wq_hi", [128, 2, NH // 2, 256], F32R)
        wq_lo = sb("wq_lo", [128, 2, NH // 2, 256], F32R)
        wm_hi = sb("wm_hi", [128, 2, 520], F32R)
        wm_lo = sb("wm_lo", [128, 2, 520], F32R)
        woe_hi = sb("woe_hi", [128, 8, D], F32R)
        LB = sb("LB", [128, D])

        l0 = ExitStack()
        stage = [sb(f"stage{i}", [128, 2048], F32, l0) for i in range(3)]
        stk = sb("stk", [128, 2, 512], F32, l0)
        w1h = sb("w1h", [128, 2, 1024], F32R, l0)
        w1l = sb("w1l", [128, 2, 1024], F32R, l0)
        w2h = sb("w2h", [128, 8, D], F32R, l0)
        w2l = sb("w2l", [128, 8, D], F32R, l0)
        bh = sb("bh", [128, 2, 128], F32R, l0)
        bl = sb("bl", [128, 2, 128], F32R, l0)
        B1 = sb("B1", [128, 8], F32, l0)
        RR = sb("RR", [128, D], F32, l0)
        xn = [sb(f"xn{i}", [128, 4, D], F32, l0) for i in range(2)]
        xh = [sb(f"xh{i}", [128, 2, 512], F32R, l0) for i in range(2)]
        xl = [sb(f"xl{i}", [128, 2, 512], F32R, l0) for i in range(2)]
        hs = [sb(f"hs{i}", [128, 512], F32, l0) for i in range(2)]
        hh = [sb(f"hh{i}", [128, 512], F32R, l0) for i in range(3)]
        hl = [sb(f"hl{i}", [128, 512], F32R, l0) for i in range(3)]
        tc = sb("tc", [128, T], F32, l0)
        tsn = sb("tsn", [128, T], F32, l0)
        tci = sb("tci", [128, T], F32, l0)
        tsi = sb("tsi", [128, T], F32, l0)
        g1 = sb("g1", [128, T], F32, l0)
        g2 = sb("g2", [128, T], F32, l0)
        gs = sb("gs", [128, T], F32, l0)
        Z = [sb(f"Z{i}", [128, T], F32, l0) for i in range(2)]
        z0 = sb("z0", [128, 4, D], F32, l0)
        th0 = sb("th0", [128, 2, D], F32, l0)
        par = sb("par", [128, 64], F32, l0)
        pari = sb("pari", [128, 4], I32, l0)
        st0 = sb("st0", [128, 4, 6], F32, l0)
        mv0 = sb("mv0", [128, 4, 2], F32, l0)
        rs0 = sb("rs0", [128, 5, 4], F32, l0)
        ri0 = sb("ri0", [128, 4], I32, l0)
        l0.close()

        l1 = ExitStack()
        yh = [sb(f"yh{i}", [128, 2, T], F32R, l1) for i in range(2)]
        yl = [sb(f"yl{i}", [128, 2, T], F32R, l1) for i in range(2)]
        yn = [sb(f"yn{i}", [128, 2, D], F32, l1) for i in range(2)]
        ML = sb("ML", [128, 2, 264], F32, l1)
        MT = sb("MT", [128, 2, 128], F32, l1)
        sq = sb("sq", [128, 2, 64], F32, l1)
        sb("gap", [128, 112], F32, l1)
        woe_lo = sb("woe_lo", [128, 8, D], F32R, l1)
        kr = sb("kr", [128, 4, 2, 32], F32, l1)
        lg = sb("lg", [128, 12, 2, 8], F32, l1)
        lv = sb("lv", [128, 10, 2], F32, l1)
        st1 = sb("st1", [128, 2, 6], F32, l1)
        mv1 = sb("mv1", [128, 2, 2], F32, l1)
        rs1 = sb("rs1", [128, 5, 2], F32, l1)
        rs2 = sb("rs2", [128, 5, 2], F32, l1)
        ri1 = sb("ri1", [128, 2], I32, l1)
        ri2 = sb("ri2", [128, 2], I32, l1)
        sb("gap2", [128, 448], F32, l1)
        KV = [sb(f"KV{i}", [128, 2, 128], F32, l1) for i in range(2)]
        KT = [sb(f"KT{i}", [128, 2, T], F32, l1) for i in range(2)]
        TR = sb("TR", [128, 2, T], F32, l1)
        QT = [sb(f"QT{i}", [128, 8, T], F32, l1) for i in range(3)]
        yh.append(sb("yh2", [128, 2, T], F32R, l1))
        yl.append(sb("yl2", [128, 2, T], F32R, l1))
        KV += [sb(f"KV{i}", [128, 2, 128], F32, l1) for i in range(2, 4)]
        KT.append(sb("KT2", [128, 2, T], F32, l1))
        SM = [sb(f"SM{i}", [128, 512], F32, l1) for i in range(3)]
        PP = [sb(f"PP{i}", [128, 512], F32, l1) for i in range(4)]
        PT = [sb(f"PT{i}", [128, 512], F32, l1) for i in range(4)]
        qa = [sb(f"qa{i}", [128, 2, T], F32, l1) for i in range(3)]
        qs = [sb(f"qs{i}", [128, 2, T], F32, l1) for i in range(3)]
        st_b = [sb(f"stb{i}", [128, 3, 4], F32, l1) for i in range(4)]
        oh = [sb(f"oh{i}", [128, 512], F32R, l1) for i in range(2)]
        ol = [sb(f"ol{i}", [128, 512], F32R, l1) for i in range(2)]
        fo = [sb(f"fo{i}", [128, D], F32, l1) for i in range(2)]
        z1 = sb("z1", [128, 2, D], F32, l1)
        w1b = [sb(f"w1b{i}", [128, 2, D], F32, l1) for i in range(3)]
        l1.close()

        bank = [ctx.enter_context(nc.psum_tensor(f"bank{i}", [128, 512], F32)) for i in range(8)]

        def load(name, dst, src, waits=()):
            return put("D", name, waits, lambda e: e.dma_start(dst, src))

        d_x = [None] * NC

        def load_x(c):
            d_x[c] = load(f"x{c}", X[:, 4 * c:4 * c + 4, :].rearrange("p a b -> p (a b)"),
                          x[:, 4 * c * D:(4 * c + 4) * D])

        load_x(0)
        d_const = load("const", CONST[:, :], consts)
        d_nuth = load("nuth", par[:, 0:2], nuth)
        st3 = stage[0][:, :].rearrange("p (k n) -> p k n", k=2)
        d_w1 = [load(f"w1{n}", st3[:, :, 512 * n:512 * n + 512], w1t[:, :, 512 * n:512 * n + 512])
                for n in range(2)]
        d_b1 = load("b1", B1[:, :], b1c)
        d_w2 = load("w2", stage[1][:, :], w2t)
        d_bt = load("bt", stk[:, 0, 0:256], bt)
        d_ct = load("ct", RR[:, :], ct)
        d_vec = load("vec", VEC[:, :], vecs)
        load_x(1)
        d_wqr = load("wqr", stage[2][:, :], wqr)
        for c in range(2, NC):
            load_x(c)

        def split(waits, src, hi, lo, name):
            a = put("S", name + "h", waits, lambda e: e.activation(hi, src, ACT.Copy))
            b = put("V", name + "l", [*waits, a],
                    lambda e: e.tensor_tensor(lo, src, hi.bitcast(F32), ALU.subtract))
            return a, b

        def drain(steps):
            for _ in steps:
                pass

        def rsqrt(waits, v, eps, name, t, ti, eng="V"):
            full, y, a, half = t[:, 0, :], t[:, 4, :], t[:, 1, :], t[:, 3, :]
            put(eng, name, waits, lambda e: e.tensor_scalar(half, v, eps, -0.5, ALU.add, ALU.mult))
            c = put(eng, name, [], lambda e: e.tensor_scalar(full, v, eps, None, ALU.add))
            c = put(eng, name, [c], lambda e: e.tensor_scalar(
                ti, full.bitcast(I32), -0.5, 1597463007.0, ALU.mult, ALU.add))
            src = ti.bitcast(F32)
            yield
            for n in range(3):
                dst = t[:, 2, :] if n == 0 else full if n == 1 else y
                c = put(eng, name, [c], lambda e, s=src: e.tensor_tensor(a, s, s, ALU.mult))
                c = put(eng, name, [c], lambda e: e.tensor_tensor(a, a, half, ALU.mult))
                yield
                if eng == "V":
                    c = put(eng, name, [c], lambda e, s=src, d=dst: e.scalar_tensor_tensor(
                        d, a, 1.5, s, ALU.add, ALU.mult))
                else:
                    c = put(eng, name, [c], lambda e: e.tensor_scalar(a, a, 1.5, None, ALU.add))
                    c = put(eng, name, [c], lambda e, s=src, d=dst: e.tensor_tensor(d, s, a, ALU.mult))
                src = dst
                yield
            return c

        def col(i, n=1):
            return par[:, i:i + n]

        def vp(c, f):
            return put("V", "par", c, f)

        def gp(c, f):
            return put("G", "par", c, f)

        def ts(dst, src, a, b, o1, o2=ALU.bypass):
            return lambda e: e.tensor_scalar(dst, src, a, b, o1, o2)

        def tt(dst, a, b, o):
            return lambda e: e.tensor_tensor(dst, a, b, o)

        MAGIC = 12582912.0
        LN2_HI, LN2_LO = 0.693145751953125, 1.42860682030941723212e-6
        INV_LN2 = 1.4426950408889634

        def exact_exp(c, src, dst, base, i):
            k, r, q, w = (col(base + j) for j in range(4))
            c = gp([*c], ts(r, src, -87.0, 88.0, ALU.max, ALU.min))
            c = gp([c], ts(k, r, INV_LN2, MAGIC, ALU.mult, ALU.add))
            c = gp([c], ts(k, k, MAGIC, None, ALU.subtract))
            c = gp([c], ts(w, k, LN2_HI, None, ALU.mult))
            c = gp([c], tt(r, r, w, ALU.subtract))
            c = gp([c], ts(w, k, LN2_LO, None, ALU.mult))
            c = gp([c], tt(r, r, w, ALU.subtract))
            c = gp([c], ts(q, r, 1.0 / 5040, 1.0 / 720, ALU.mult, ALU.add))
            for f in (1.0 / 120, 1.0 / 24, 1.0 / 6, 0.5, 1.0, 1.0):
                c = gp([c], tt(q, q, r, ALU.mult))
                c = gp([c], ts(q, q, f, None, ALU.add))
            c = gp([c], ts(pari[:, i:i + 1], k, 8388608.0, 1065353216.0, ALU.mult, ALU.add))
            return gp([c], tt(dst, q, pari[:, i:i + 1].bitcast(F32), ALU.mult))

        def reduce(c, k, r, w):
            c = gp([c], ts(k, r, 0.15915494309189535, MAGIC, ALU.mult, ALU.add))
            c = gp([c], ts(k, k, MAGIC, None, ALU.subtract))
            for part in (6.28125, 0.0019340515136718750, 1.2556659146932927e-06):
                c = gp([c], ts(w, k, part, None, ALU.mult))
                c = gp([c], tt(r, r, w, ALU.subtract))
            return c

        def angles():
            c = exact_exp([d_nuth], col(1), col(3), 12, 2)
            c = reduce(c, col(24), col(3), col(25))
            r, ab = col(32, 8), col(40, 8)
            c = put("G", "par", [c], *[ts(col(32 + i), col(3), float(2 ** i), None, ALU.mult)
                                       for i in range(8)])
            c = reduce(c, ab, r, col(48, 8))
            PI = 3.1415925
            c = gp([c], ts(r, r, PI, -PI, ALU.min, ALU.max))
            return gp([c], ts(ab, r, 0.5, None, ALU.mult))

        def magnitudes():
            mag, gamma = col(5), col(6)
            c = exact_exp([d_nuth], col(0), col(2), 8, 0)
            c = gp([c], ts(col(4), col(2), 1.0, -1.0, ALU.add, ALU.mult))
            c = exact_exp([c], col(4), mag, 8, 0)
            c = gp([c], ts(col(7), col(4), -87.0, None, ALU.is_gt))
            c = gp([c], tt(mag, mag, col(7), ALU.mult))
            c = gp([c], tt(gamma, mag, mag, ALU.mult))
            c = gp([c], ts(gamma, gamma, -1.0, 1.0, ALU.mult, ALU.add))
            steps = rsqrt([c], gamma, 0.0, "par", par[:, 16:21].unsqueeze(2), pari[:, 1:2], "G")
            drain(steps)
            return gp([("par_G", p.count["par_G"])], tt(gamma, gamma, par[:, 20:21], ALU.mult))

        k_angles = angles()
        k_mag = magnitudes()
        k_tab = []

        def sines():
            return put("S", "sin", [k_angles], lambda e: e.activation(col(48, 16), col(32, 16), ACT.Sin))

        def tables(c):
            s8, c8, w8, v8 = col(48, 8), col(56, 8), col(32, 8), col(40, 8)
            c = vp([c, k_angles], tt(c8, c8, c8, ALU.mult))
            c = vp([c], ts(c8, c8, -2.0, 1.0, ALU.mult, ALU.add))
            c = vp([c], tt(w8, s8, s8, ALU.mult))
            c = vp([c], tt(v8, c8, c8, ALU.mult))
            c = vp([c], tt(w8, w8, v8, ALU.add))
            c = vp([c], ts(w8, w8, -0.5, 1.5, ALU.mult, ALU.add))
            c = vp([c], tt(s8, s8, w8, ALU.mult))
            c = vp([c], tt(c8, c8, w8, ALU.mult))
            c = vp([c], lambda e: e.memset(tc[:, 0:1], 1.0))
            c = vp([c], lambda e: e.memset(tsn[:, 0:1], 0.0))
            yield
            for i in range(8):
                n, ps, pc = 2 ** i, col(48 + i), col(56 + i)

                put("V", "par", [c], lambda e, n=n, ps=ps: e.tensor_scalar(
                    g1[:, 0:n], tsn[:, 0:n], ps, None, ALU.mult))
                a = put("V", "par", [], lambda e, n=n, ps=ps: e.tensor_scalar(
                    g2[:, 0:n], tc[:, 0:n], ps, None, ALU.mult))
                put("V", "par", [a], lambda e, n=n, pc=pc: e.scalar_tensor_tensor(
                    tc[:, n:2 * n], tc[:, 0:n], pc, g1[:, 0:n], ALU.mult, ALU.subtract))
                c = put("V", "par", [], lambda e, n=n, pc=pc: e.scalar_tensor_tensor(
                    tsn[:, n:2 * n], tsn[:, 0:n], pc, g2[:, 0:n], ALU.mult, ALU.add))
                yield
            c = vp([c, k_mag], lambda e: e.tensor_scalar(tci[:, :], tc[:, :], col(6), None, ALU.mult))
            c = vp([c, d_const], lambda e: e.tensor_scalar(tsi[:, :], tsn[:, :], col(6), sgn, ALU.mult, ALU.mult))
            c = vp([c, d_ct], lambda e: e.tensor_scalar(RR[:, :], RR[:, :], sgnc, None, ALU.mult))
            k_tab.append(c)

        st8 = stage[1][:, :].rearrange("p (k n) -> p k n", k=8)
        k_w1, k_w2, k_b = [], [], []
        free2 = {i: [] for i in range(3)}
        free_stk = {0: [], 1: []}

        def weights_1(n):
            sl = slice(512 * n, 512 * n + 512)
            k_w1.append(split([d_w1[n]], st3[:, :, sl], w1h[:, :, sl], w1l[:, :, sl], "w1s"))
            free2[0] = list(k_w1[-1])

        def weights_2(n):
            sl = slice(4 * n, 4 * n + 4)
            k_w2.append(split([d_w2], st8[:, sl, :], w2h[:, sl, :], w2l[:, sl, :], "w2s"))
            free2[1] = list(k_w2[-1])

        def weights_b():
            k_b.extend(split([d_bt], stk[:, 0, 0:256].rearrange("p (k n) -> p k n", k=2),
                             bh[:, :, :], bl[:, :, :], "bs"))
            free_stk[0] = list(k_b)

        tbank = Ring([bank[0]])
        fbank = Ring([bank[1], bank[2]])
        obank = [bank[3], bank[4], bank[6]]
        ubank = ybank = Ring([bank[5]])
        wbank = Ring([bank[7]])
        xn_r = [[], []]
        xt_r = [[], []]
        k_xn = [None] * NC
        k_xt = [None] * NC
        turned = [None] * NC

        def l0_norm(c):
            q = c % 2
            w = [d_x[c]]
            a = put("V", "bn", w + ([k_xn[c - 1]] if c else []),
                    *[lambda e, i=i: e.bn_stats(st0[:, i, :], X[:, 4 * c + i, :]) for i in range(4)])
            a = put("V", "bn", [a], *[lambda e, i=i: e.bn_aggr(mv0[:, i, :], st0[:, i, :]) for i in range(4)])
            yield
            a = yield from rsqrt([a], mv0[:, :, 1], LN_EPS, "ln0", rs0, ri0[:, :])
            k_xn[c] = put("V", "xn", [a, *xn_r[q]], *[
                lambda e, i=i: e.tensor_scalar(xn[q][:, i, :], X[:, 4 * c + i, :], mv0[:, i, 0:1],
                                               rs0[:, 4, i:i + 1], ALU.subtract, ALU.mult)
                for i in range(4)])

        def l0_turn(c, k):
            q = c % 2
            i, bk, free = tbank.take()
            t = put("T", "tx", [k_xn[c], d_const, *free], *[
                lambda e, j=j: e.transpose(bk[:, 128 * j:128 * j + 128],
                                           xn[q][:, j, 128 * k:128 * k + 128], ident) for j in range(4)])
            h, l = split([t, *xt_r[q]], bk[:, :], xh[q][:, k, :], xl[q][:, k, :], "xt")
            tbank.free(i, h, l)
            k_xt[c] = [h, l]
            turned[c] = [t]

        def three(dst, wh, wl, mh, ml, first, last, skip=False):
            out_ = []
            for j, (a, b) in enumerate(((wl, mh), (wh, ml), (wh, mh))):
                out_.append(lambda e, a=a, b=b, j=j: e.matmul(
                    dst, a, b, start=(first and j == 0), stop=(last and j == 2), skip_group_check=skip))
            return out_

        z_k = [None] * NC
        z_r = [[], []]
        g_prev = []

        def l0_scan(c):
            nonlocal g_prev
            q = c % 2
            i, bk, free = ubank.take()
            m = []
            for k in range(2):
                m += three(bk[:, :], bh[:, k, :], bl[:, k, :], xh[q][:, k, :], xl[q][:, k, :], k == 0, k == 1)
            u = put("T", "bu", [*k_b, *k_xt[c], *free], *m)
            ks = []
            for b in range(2):
                r = slice(64 * b, 64 * b + 64)
                s = slice(256 * b, 256 * b + 256)
                ks.append(put("V", "rot", [u, *k_tab, *g_prev], lambda e, r=r, s=s: e.tensor_tensor(
                    g1[r, :], bk[0:64, s], tci[r, :], ALU.mult)))
                ks.append(put("V", "rot", [], lambda e, r=r, s=s: e.tensor_tensor(
                    g2[r, :], bk[64:128, s], tsi[r, :], ALU.mult)))
            ubank.free(i, ks[-1])
            a = put("V", "rot", [ks[-1]], lambda e: e.tensor_tensor(g1[:, :], g1[:, :], g2[:, :], ALU.add))
            a = put("V", "rot", [a], lambda e: e.tensor_tensor_scan(gs[:, :], par[:, 5:6].broadcast_to([128, T]), g1[:, :], 0.0,
                                                                    ALU.mult, ALU.add))
            zs = []
            for b in range(2):
                r = slice(64 * b, 64 * b + 64)
                w = [a, *z_r[b]]
                put("V", "rot", w, lambda e, r=r, b=b: e.tensor_tensor(
                    Z[b][0:64, :], gs[r, :], tc[r, :], ALU.mult))
                zs.append(put("V", "rot", [], lambda e, r=r, b=b: e.tensor_tensor(
                    Z[b][64:128, :], gs[r, :], tsn[r, :], ALU.mult)))
            g_prev = [zs[-1]]
            z_k[c] = zs
            return u

        z_prev = [[], []]
        th_prev = []
        s_tok = {}

        def l0_y(c, b):
            q = c % 2
            i, bk, free = ybank.take()
            y = put("T", "y", [z_k[c][b], *free], *[
                lambda e, j=j: e.matmul(bk[:, 256 * j:256 * j + 256], Z[b][:, 128 * j:128 * j + 128],
                                        RR[:, :], start=True, stop=True) for j in range(2)])
            z_r[b] = [y]
            db = VEC[:, OFF_D:OFF_D + D].unsqueeze(1).broadcast_to([128, 2, D])
            s0 = xn[q]
            g = put("G", "dx", [k_xn[c], d_vec, *turned[c]], lambda e: e.tensor_tensor(
                s0[:, 2 * b:2 * b + 2, :], s0[:, 2 * b:2 * b + 2, :], db, ALU.mult))
            v = put("V", "sy", [y, g], lambda e: e.tensor_tensor(
                s0[:, 2 * b:2 * b + 2, :], bk[:, :].rearrange("p (a d) -> p a d", a=2),
                s0[:, 2 * b:2 * b + 2, :], ALU.add))
            ybank.free(i, v)
            s_tok[b] = v
            return g

        h_r = [[], [], []]
        hs_r = [[], []]
        k_h = {}
        hn = [0]

        def l0_up(c, hb):
            q = c % 2
            i, bk, free = fbank.take()
            m = []
            sl = slice(128 * hb, 128 * hb + 128)
            for k in range(2):
                m += three(bk[:, :], w1h[:, k, sl], w1l[:, k, sl], xh[q][:, k, :], xl[q][:, k, :],
                           k == 0, k == 1)
            t = put("T", "f1", [*k_w1[hb // 4], *k_xt[c], *free], *m)
            r, v = hn[0] % 3, hn[0] % 2
            hn[0] += 1
            g = put("S", "gelu", [t, d_b1, *hs_r[v]], lambda e: e.activation(
                hs[v][:, :], bk[:, :], ACT.Gelu, bias=B1[:, hb:hb + 1]))
            fbank.free(i, g)
            a, b = split([g, *h_r[r]], hs[v][:, :], hh[r][:, :], hl[r][:, :], "hs")
            hs_r[v] = [a, b]
            k_h[(c, hb)] = (r, a, b)
            return t

        z_free = Turns(3, lambda n: [])

        def l0_down(c, hb):
            r, a, b = k_h[(c, hb)]
            for half in range(2):
                n = 2 * c + half
                m = []
                for t in range(2):
                    dst = obank[n % 3][:, 256 * t:256 * t + 256]
                    sl = slice(256 * half + 128 * t, 256 * half + 128 * t + 128)
                    m += three(dst, hh[r][:, sl], hl[r][:, sl], w2h[:, hb, :], w2l[:, hb, :],
                               hb == 0 and t == 0, hb == 7, skip=True)
                w = z_free.readers(n) if hb == 0 else []
                t = put("T", "f2", [a, b, *k_w2[hb // 4], *w], *m)
            h_r[r] = [t]
            return t

        x1_k = [None] * NC

        def l0_out(c, t):
            nonlocal th_prev
            zs = []
            s0 = xn[c % 2]
            for b in range(2):
                sl = slice(2 * b, 2 * b + 2)
                bb = VEC[:, OFF_B2:OFF_B2 + D].unsqueeze(1).broadcast_to([128, 2, D])
                z = put("V", "z0", [t, d_vec, *z_prev[b]], lambda e, b=b, sl=sl: e.tensor_tensor(
                    z0[:, sl, :], obank[(2 * c + b) % 3][:, :].rearrange("p (a d) -> p a d", a=2), bb, ALU.add))
                zs.append(z)
                z_free.free(2 * c + b, z)
            for b in range(2):
                sl = slice(2 * b, 2 * b + 2)
                xs = slice(4 * c + 2 * b, 4 * c + 2 * b + 2)
                th = put("S", "th0", [zs[b], *th_prev], lambda e, sl=sl: e.activation(
                    th0[:, :, :], z0[:, sl, :], ACT.Tanh, scale=0.5))
                a = put("V", "x1", [th], lambda e, sl=sl: e.scalar_tensor_tensor(
                    z0[:, sl, :], th0[:, :, :], 1.0, z0[:, sl, :], ALU.add, ALU.mult))
                th_prev = [a]
                a = put("V", "x1", [a, s_tok[b]], lambda e, sl=sl: e.tensor_tensor(
                    s0[:, sl, :], s0[:, sl, :], z0[:, sl, :], ALU.mult))
                a = put("V", "x1", [a], lambda e, sl=sl, xs=xs: e.scalar_tensor_tensor(
                    X[:, xs, :], s0[:, sl, :], 0.5, X[:, xs, :], ALU.mult, ALU.add))
                z_prev[b] = [a]
            x1_k[c] = a
            xn_r[c % 2] = [a]

        k_w = {}

        def w_rope():
            src = stage[2][:, :].rearrange("p (k q j n) -> p k q j n", k=2, q=NH // 2, j=2)
            a, b = [], []
            for j in range(2):
                cols = slice(128 + 64 * (1 - j), 192 + 64 * (1 - j))
                a.append(put("S", "wr", [d_wqr], lambda e, j=j, cols=cols: e.activation(
                    wq_hi[:, :, :, cols], src[:, :, :, j, :], ACT.Copy, scale=-SCALE)))
                b.append(put("V", "wr", [a[-1]], lambda e, j=j, cols=cols: e.scalar_tensor_tensor(
                    wq_lo[:, :, :, cols], src[:, :, :, j, :], -SCALE, wq_hi[:, :, :, cols].bitcast(F32),
                    ALU.mult, ALU.subtract)))
            free2[2] = a + b
            k_w["r"] = a + b

        d_wn = {}

        def load_nope(g):
            s = g
            d_wn[g] = [load(f"wn{g}", stage[s][:, :], wqn[:, g * 2048:(g + 1) * 2048], free2[s]),
                       load(f"wk{g}", stk[:, g, :], wkbt[:, g * 512:(g + 1) * 512], free_stk[g])]

        def w_nope(g, k):
            i, bk, free = wbank.take()
            wn = stage[g][:, :].rearrange("p (h d) -> p h d", h=8)
            t = put("T", "wn", [*d_wn[g], *free], *[
                lambda e, j=j: e.matmul(bk[:, 64 * j:64 * j + 64], wn[:, j, 128 * k:128 * k + 128],
                                        stk[:, g, 64 * j:64 * j + 64], start=True, stop=True)
                for j in range(8)])
            src = bk[:, :].rearrange("p (q n) -> p q n", q=4)
            hi, lo = (w[:, k, 4 * g:4 * g + 4, 0:128] for w in (wq_hi, wq_lo))
            a = put("S", "wn", [t], lambda e: e.activation(hi, src, ACT.Copy, scale=-SCALE))
            b = put("V", "wn", [t, a], lambda e: e.scalar_tensor_tensor(
                lo, src, -SCALE, hi.bitcast(F32), ALU.mult, ALU.subtract))
            wbank.free(i, a, b)
            free2[g] = [t]
            free_stk[g] = [t]
            k_w[("n", g, k)] = [a, b]

        d_wo = {}

        def load_o(g):
            d_wo[g] = [load(f"wo{g}", stage[g][:, :], wo[:, g * 2048:(g + 1) * 2048], free2[g]),
                       load(f"wv{g}", stk[:, g, :], wvbt[:, g * 512:(g + 1) * 512], free_stk[g])]

        def w_o(g, i2):
            i, bk, free = wbank.take()
            wv = stage[g][:, :].rearrange("p (h d) -> p h d", h=8)
            ms = []
            for j in range(2):
                for half in range(2):
                    h = 4 * half + 2 * i2 + j
                    ms.append(lambda e, j=j, half=half, h=h: e.matmul(
                        bk[64 * half:64 * half + 64, 256 * j:256 * j + 256],
                        stk[:, g, 64 * h:64 * h + 64], wv[:, h, :], start=True, stop=True))
            t = put("T", "wo", [*d_wo[g], *free], *ms)
            rows = slice(4 * g + 2 * i2, 4 * g + 2 * i2 + 2)
            a = split([t, *k_w["m"]], bk[:, :].rearrange("p (j d) -> p j d", j=2),
                      woe_hi[:, rows, :], woe_lo[:, rows, :], "woe")
            wbank.free(i, *a)
            free2[g] = [t]
            free_stk[g] = [t]
            k_w[("o", g, i2)] = [*a]

        d_wm = []

        def load_m():
            s = stage[2][:, 0:1040].rearrange("p (k n) -> p k n", k=2)
            w = free2[2]
            d_wm.append(load("wm0", s[:, :, 0:128], wkva, w))
            d_wm.append(load("wm1", s[:, :, 128:256], loraa, w))
            d_wm.append(load("wm2", s[:, :, 256:264], routert, w))
            d_wm.append(load("wm3", s[:, :, 264:520], baset, w))
            d_wm.append(load("wm4", LB[:, :], lorab))

        def w_m():
            s = stage[2][:, 0:1040].rearrange("p (k n) -> p k n", k=2)
            k_w["m"] = [*split(d_wm, s, wm_hi[:, :, :], wm_lo[:, :, :], "wm"), d_wm[-1]]

        def rope_tables():
            toks = []
            for q in range(2):
                for j in range(2):
                    toks.append(put("G", "rt", [d_const], lambda e, q=q, j=j: e.tensor_copy(
                        rope_c[:, q, j, :], cosT[q])))
                    toks.append(put("G", "rt", [], lambda e, q=q, j=j: e.tensor_scalar(
                        rope_s[:, q, j, :], sinT[q], 1.0 if j == 0 else -1.0, 1.0, ALU.mult, ALU.mult)))
            return toks[-1]

        k_rt = rope_tables()

        fill = {
            (1, 1): w_rope,
            (1, 3): lambda: (load_nope(0), load_nope(1), load_m()),
            (2, 4): lambda: w_nope(0, 0), (2, 6): lambda: w_nope(0, 1),
            (3, 1): lambda: w_nope(1, 0), (3, 3): lambda: w_nope(1, 1),
            (3, 4): w_m,
            (3, 5): lambda: (load_o(0), load_o(1)),
            (5, 1): lambda: w_o(0, 0), (5, 4): lambda: w_o(0, 1),
            (6, 1): lambda: w_o(1, 0), (6, 4): lambda: w_o(1, 1),
        }

        end0, endm, endf, endw = [], [], [], []
        tb = pj = wbank
        sbk = Ring([bank[3], bank[5]])
        obk = Ring([bank[4]])
        ob = None
        qk = Ring(list(zip(qa, qs)))
        sm, pp, pt, ot = Ring(SM), Ring(PP), Ring(PT), Ring(list(zip(oh, ol)))
        st_ring = Ring(st_b)
        for r_ in (sbk, obk, qk, sm, pp, pt, ot, st_ring):
            for i in range(len(r_.buffers)):
                r_.readers[i] = endm if r_ is qk else end0
        B = {}
        k_ramp, k_tr = [], []
        ramp = lg[:, 11, :, :]

        r_qt, r_z = Turns(3, lambda n: endm if n == 0 else end0), Turns(1, lambda n: end0)
        r_w = Turns(3, lambda n: end0)
        r_kt = Turns(3, lambda n: endf if n < 2 else end0)
        r_yx = Turns(3, lambda n: endw if n < 2 else end0)
        r_kv = Turns(4, lambda n: endf if n < 2 else end0)
        r_yn = Turns(2, lambda n: endw)
        r_mlt, r_mt, r_ln = (Turns(1, lambda n: endw) for _ in range(3))
        r_fo = [Turns(1, lambda n: end0) for _ in range(2)]

        pool_last, pool_half = [], []

        def pool(name, waits, *fs):
            t = put("G", name, [*waits, *pool_half], *fs)
            pool_last[:] = [t]
            return t

        def l1_norm(b):
            q = b % 2
            a = put("V", "bn1", [x1_k[b // 2], *r_ln.readers(b)],
                    *[lambda e, i=i: e.bn_stats(st1[:, i, :], X[:, 2 * b + i, :]) for i in range(2)])
            yield
            a = put("V", "bn1", [a], *[lambda e, i=i: e.bn_aggr(mv1[:, i, :], st1[:, i, :])
                                       for i in range(2)])
            yield
            a = yield from rsqrt([a], mv1[:, :, 1], LN_EPS, "ln1", rs1, ri1[:, :])
            k = put("V", "yn", [a, *r_yn.readers(b)], *[
                lambda e, i=i: e.tensor_scalar(yn[q][:, i, :], X[:, 2 * b + i, :], mv1[:, i, 0:1],
                                               rs1[:, 4, i:i + 1], ALU.subtract, ALU.mult)
                for i in range(2)])
            r_ln.free(b, k)
            B[b] = {"yn": k, "qt": {}}

        def l1_turn(b):
            q = b % 2
            i, bk, free = tb.take()
            t = put("T", "ty", [B[b]["yn"], *free], *[
                lambda e, k=k, j=j: e.transpose(bk[:, 256 * k + 128 * j:256 * k + 128 * j + 128],
                                                yn[q][:, j, 128 * k:128 * k + 128], ident)
                for k in range(2) for j in range(2)])
            src = bk[:, :].rearrange("p (k n) -> p k n", k=2)
            hi, lo = yh[b % 3][:, :, :], yl[b % 3][:, :, :]
            h = put("S", "yth", [t, *r_yx.readers(b)], lambda e: e.activation(hi, src, ACT.Copy))
            r_yn.free(b, t)

            def low():
                l = put("V", "ytl", [t, h, *r_yx.readers(b)],
                        lambda e: e.tensor_tensor(lo, src, hi.bitcast(F32), ALU.subtract))
                tb.free(i, h, l)
                B[b]["yt"] = [h, l]
            later(low)

        def l1_misc(b, t):
            q = b % 2
            sl = slice(128 * t, 128 * t + 128)
            i, bk, free = pj.take()
            m = []
            for k in range(2):
                m += three(bk[:, 0:264], yh[b % 3][:, k, sl], yl[b % 3][:, k, sl], wm_hi[:, k, 0:264],
                           wm_lo[:, k, 0:264], k == 0, k == 1)
            a = put("T", "mi", [*B[b]["yt"], *k_w["m"], *free], *m)
            c_ = put("S", "mi", [a, *r_mlt.readers(b)], lambda e: e.activation(
                ML[:, t, :], bk[:, 0:264], ACT.Copy))
            pj.free(i, c_)
            B[b][("mi", t)] = c_

        def vk(c, f, name="kv"):
            return put("V", name, c, f)

        def l1_kv(b):
            q = b % 2
            w = [B[b][("mi", 0)], B[b][("mi", 1)]]
            r = ML[:, :, 64:128].rearrange("p t (j n) -> p t j n", j=2)
            g = pool("kr", [*w, k_rt, *r_mlt.readers(b)], lambda e: e.tensor_tensor(
                kr[:, 0:2, :, :], r, rope_c[:, :, :, :], ALU.mult))
            g = pool("kr", [g], lambda e: e.tensor_tensor(
                kr[:, 2:4, :, :], r, rope_s[:, :, :, :], ALU.mult))
            gg = pool("kr", [g, *r_kv.readers(b)], *[
                lambda e, j=j: e.tensor_tensor(KV[b % 4][:, :, 64 + 32 * j:96 + 32 * j], kr[:, 0:2, j, :],
                                               kr[:, 2:4, 1 - j, :], ALU.add) for j in range(2)])
            cl = ML[:, :, 0:64]
            a = vk(w, lambda e: e.tensor_tensor(sq[:, :, :], cl, cl, ALU.mult))
            yield
            a = vk([a], lambda e: e.tensor_reduce(lv[:, 0, :], sq[:, :, :], AX.X, ALU.add))
            a = vk([a], lambda e: e.tensor_scalar(lv[:, 1, :], lv[:, 0, :], 1.0 / 64, None, ALU.mult))
            yield
            a = yield from rsqrt([a], lv[:, 1, :], RMS_EPS, "rms", rs2, ri2[:, :])
            kw = VEC[:, OFF_KW:OFF_KW + 64]
            a = put("V", "kvw", [a, *r_kv.readers(b)], *[
                lambda e, t=t: e.scalar_tensor_tensor(KV[b % 4][:, t, 0:64], ML[:, t, 0:64],
                                                      rs2[:, 4, t:t + 1], kw, ALU.mult, ALU.mult)
                for t in range(2)])
            yield
            for _ in range(PLAN["tk"]):
                yield
            i, bk, free = tb.take()
            t = put("T", "tk", [a, gg, *free], *[
                lambda e, j=j: e.transpose(bk[:, 128 * j:128 * j + 128], KV[b % 4][:, j, :], ident)
                for j in range(2)])
            def keys():
                k = put("S", "kt", [t, *r_kt.readers(b)],
                        lambda e: e.activation(KT[b % 3][:, 0, :], bk[:, 0:256], ACT.Copy),
                        lambda e: e.activation(KT[b % 3][0:64, 1, :], bk[64:128, 0:256], ACT.Copy),
                        lambda e: e.activation(KT[b % 3][64:128, 1, :], bk[0:64, 0:256], ACT.Copy))
                tb.free(i, k)
                B[b]["kt"] = k
            later(keys)
            B[b]["kv"] = [a, gg]
            B[b]["tk"] = t

        def l1_gate(b):
            w = [B[b][("mi", 0)], B[b][("mi", 1)], *r_mlt.readers(b)]
            L, E1, K1, L2, E2, SG, CT_ = (lg[:, i, :, :] for i in range(7))
            n = "gt"

            def bc(v):
                return v.unsqueeze(2).broadcast_to([128, 2, 8])

            def first_of(c, src, top, hot):
                c = vk(c, lambda e: e.tensor_reduce(top, src, AX.X, ALU.max), n)
                c = vk([c], lambda e: e.tensor_tensor(hot, src, bc(top), ALU.is_equal), n)
                yield
                c = vk([c], lambda e: e.tensor_tensor(hot, hot, ramp, ALU.mult), n)
                c = vk([c], lambda e: e.tensor_reduce(lv[:, 4, :], hot, AX.X, ALU.max), n)
                yield
                return vk([c], lambda e: e.tensor_tensor(hot, ramp, bc(lv[:, 4, :]), ALU.is_equal), n)

            rb = VEC[:, OFF_RB:OFF_RB + 8].unsqueeze(1).broadcast_to([128, 2, 8])
            c_ = vk(w, lambda e: e.tensor_tensor(L, ML[:, :, 256:264], rb, ALU.add), n)
            c_ = yield from first_of([c_, *k_ramp], L, lv[:, 2, :], E1)
            c_ = vk([c_], lambda e: e.scalar_tensor_tensor(L2, E1, -3e38, L, ALU.mult, ALU.add), n)
            yield
            c_ = yield from first_of([c_], L2, lv[:, 3, :], E2)
            c_ = vk([c_], lambda e: e.tensor_tensor(E1, E1, E2, ALU.add), n)
            c_ = vk([c_], lambda e: e.tensor_tensor(L2, L, bc(lv[:, 2, :]), ALU.subtract), n)
            for _ in range(PLAN["exp"]):
                yield
            c_ = put("S", "gt", [c_], lambda e: e.activation(L2, L2, ACT.Exp))
            for _ in range(6):
                yield
            c_ = vk([c_], lambda e: e.tensor_tensor(E1, E1, L2, ALU.mult), n)
            c_ = vk([c_], lambda e: e.tensor_reduce(lv[:, 5, :], E1, AX.X, ALU.add), n)
            yield
            c_ = vk([c_], lambda e: e.reciprocal(lv[:, 6, :], lv[:, 5, :]), n)
            c_ = vk([c_], lambda e: e.scalar_tensor_tensor(E1, E1, 2.0, bc(lv[:, 6, :]), ALU.mult, ALU.mult), n)
            yield
            c_ = vk([c_], lambda e, t=0: e.tensor_tensor(
                ML[:, t, 128:256].rearrange("p (x r) -> p x r", x=8),
                ML[:, t, 128:256].rearrange("p (x r) -> p x r", x=8),
                E1[:, t, :].unsqueeze(2).broadcast_to([128, 8, 16]), ALU.mult), n)
            c_ = vk([c_], lambda e: e.tensor_tensor(
                ML[:, 1, 128:256].rearrange("p (x r) -> p x r", x=8),
                ML[:, 1, 128:256].rearrange("p (x r) -> p x r", x=8),
                E1[:, 1, :].unsqueeze(2).broadcast_to([128, 8, 16]), ALU.mult), n)
            for _ in range(PLAN["tm"]):
                yield
            i, bk, free = tb.take()
            t = put("T", "tm", [c_, *free], *[
                lambda e, j=j: e.transpose(bk[:, 128 * j:128 * j + 128], ML[:, j, 128:256], ident)
                for j in range(2)])
            def mids():
                k = put("S", "mt", [t, *r_mt.readers(b)], lambda e: e.activation(
                    MT[:, :, :], bk[:, 0:256].rearrange("p (t n) -> p t n", t=2), ACT.Copy))
                tb.free(i, k)
                B[b]["mt"] = k
            later(mids)
            r_mlt.free(b, t, *B[b]["kv"])

        def l1_lora(b):
            q = b % 2
            i, bk, free = pj.take()
            m = []
            for t in range(2):
                dst, sl = bk[:, 256 * t:256 * t + 256], slice(128 * t, 128 * t + 128)
                for k in range(2):
                    m += three(dst, yh[b % 3][:, k, sl], yl[b % 3][:, k, sl], wm_hi[:, k, 264:520],
                               wm_lo[:, k, 264:520], k == 0, False, skip=True)
                m.append(lambda e, t=t, dst=dst: e.matmul(dst, MT[:, t, :], LB[:, :], start=False,
                                                          stop=True, skip_group_check=True))
            m = put("T", "lo", [B[b]["mt"], *k_w["m"], *free], *m)
            r_mt.free(b, m)
            done_yx(b, m)
            bb = VEC[:, OFF_BB:OFF_BB + D].unsqueeze(1).broadcast_to([128, 2, D])
            z = put("V", "z1", [m, *r_z.readers(b)], lambda e: e.tensor_tensor(
                z1[:, :, :], bk[:, :].rearrange("p (t d) -> p t d", t=2), bb, ALU.add))
            pj.free(i, z)

            def gate_tanh():
                th = put("S", "th1", [z, *r_w.readers(b)], lambda e: e.activation(
                    w1b[b % 3][:, :, :], z1[:, :, :], ACT.Tanh, scale=0.5))

                def weigh():
                    B[b]["w"] = put("V", "w1", [th], lambda e: e.scalar_tensor_tensor(
                        w1b[b % 3][:, :, :], w1b[b % 3][:, :, :], 1.0, z1[:, :, :], ALU.add, ALU.mult))
                    r_z.free(b, B[b]["w"])
                later(weigh)
            later(gate_tanh)

        def done_yx(b, token):
            both = B[b].setdefault("yx", [])
            both.append(token)
            if len(both) == 2:
                r_yx.free(b, *both)

        def l1_q(b, u):
            g, rot = u // 2, u % 2
            i, bk, free = pj.take()
            m = []
            for j in range(2):
                cols = slice(128 * rot, 128 * rot + 128)
                for k in range(2):
                    m += three(bk[:, 256 * j:256 * j + 256], wq_hi[:, k, 2 * g + j, cols],
                               wq_lo[:, k, 2 * g + j, cols], yh[b % 3][:, k, :], yl[b % 3][:, k, :],
                               k == 0, k == 1)
            wk = [*k_w["r"]] if rot else [x for kk in range(2) for x in k_w[("n", g // 2, kk)]]
            a = put("T", "q", [*B[b]["yt"], *wk, *free], *m)
            if u == 7:
                done_yx(b, a)
            src = bk[:, :].rearrange("p (j t) -> p j t", j=2)
            even, odd = slice(0, 64), slice(64, 128)
            Q_, h0 = QT[(2 * b + g // 2) % 3], 4 * (g % 2)
            if not rot:
                c = put("S", "qn", [a, *r_qt.readers(2 * b + g // 2)], *[
                    lambda e, r=r, o=o: e.activation(Q_[r, h0 + o:h0 + 4:2, :], src[r, :, :], ACT.Copy)
                    for o, r in enumerate((even, odd))])
                pj.free(i, c)
                B[b]["qt"][g] = [c]
                return
            n, (A_, S_), fr = qk.take()
            c1 = put("S", "qs", [a, *fr], *[
                lambda e, d=d: e.activation(S_[32 * d:32 * d + 32, :, :], src[32 * (d ^ 1):32 * (d ^ 1) + 32, :, :],
                                            ACT.Copy) for d in range(4)])
            cb, sn = (TR[:, x, :].unsqueeze(1).broadcast_to([128, 2, T]) for x in range(2))
            c2 = put("V", "qa", [c1, *k_tr, *fr], lambda e: e.tensor_tensor(A_[:, :, :], src, cb, ALU.mult))
            c3 = put("V", "qa", [c1], lambda e: e.tensor_tensor(S_[:, :, :], S_[:, :, :], sn, ALU.mult))
            pj.free(i, c1, c2)
            c4 = c3
            for o, r in enumerate((odd, even)):
                c4 = pool("q", [c4, *pool_last, *r_qt.readers(2 * b + g // 2)], lambda e, r=r, o=o: e.tensor_tensor(
                    Q_[r, h0 + o:h0 + 4:2, :], A_[r, :, :], S_[r, :, :], ALU.add))
            pool_half[:] = [c4]
            qk.free(n, c4)
            B[b]["qt"][g].append(c4)

        def pair(pi):
            if pi < 2:
                return 0, [[8 * pi + i for i in range(4)], [8 * pi + 4 + i for i in range(4)]]
            hgrp, two = (pi - 2) // 2, (pi - 2) % 2
            return 1, [[8 * hgrp + 4 * hf + 2 * two + i for i in range(2)] for hf in range(2)]

        def l1_s(b, pi, hf):
            q = b % 2
            qt, heads = pair(pi)
            hd = heads[hf]
            nk = 128 * (qt + 1)
            i, bk, free = sbk.take()
            w = B[b]["qt"][hd[0] // 4]
            n = 2 * b + hd[0] // 8
            Q_ = QT[n % 3]
            s = put("T", "s", [B[b]["kt"], *w, *free], *[
                lambda e, j=j, h=h: e.matmul(bk[:, nk * j:nk * j + nk], Q_[:, h % 8, 128 * qt:128 * qt + 128],
                                             KT[b % 3][:, h % 2, 0:nk], start=True, stop=True)
                for j, h in enumerate(hd)])
            if (pi, hf) == (5, 1):
                r_kt.free(b, s)
            if hf == 1 and pi in (3, 5):
                r_qt.free(n, s)
            mi, M_, mf = sm.take()
            si, S_, sf = st_ring.take()
            mk = mask1 if qt else mask0
            a = put("V", "s", [s, *mf, *sf], *[
                lambda e, j=j: e.tensor_tensor_reduce(
                    M_[:, nk * j:nk * j + nk], bk[:, nk * j:nk * j + nk], mk, 1.0, 3e38,
                    ALU.add, ALU.min, S_[:, 0, j:j + 1]) for j in range(len(hd))])
            sbk.free(i, a)
            B[b][("s", pi, hf)] = s
            n = len(hd)

            def exps():
                pi_, P_, pf = pp.take()
                x_ = put("S", "p", [a, *pf], *[
                    lambda e, j=j: e.activation(P_[:, nk * j:nk * j + nk], M_[:, nk * j:nk * j + nk],
                                                ACT.Exp, bias=S_[:, 0, j:j + 1], scale=-1.0,
                                                accum_out=S_[:, 1, j:j + 1]) for j in range(n)])
                sm.free(mi, x_)

                def norms():
                    r = put("V", "r", [x_], lambda e: e.reciprocal(S_[:, 2, 0:n], S_[:, 1, 0:n]))
                    g = pool("n", [r], *[
                        lambda e, j=j: e.tensor_scalar(P_[:, nk * j:nk * j + nk], P_[:, nk * j:nk * j + nk],
                                                       S_[:, 2, j:j + 1], 1.0, ALU.mult, ALU.mult)
                        for j in range(n)])
                    st_ring.free(si, g)
                    B[b][("p", pi, hf)] = (pi_, P_, g)
                later(norms)
            later(exps)

        def l1_pt(b, pi, hf):
            qt, heads = pair(pi)
            pi_, P_, g = B[b][("p", pi, hf)]
            i, bk, free = tb.take()
            if qt == 0:
                spans = [(128 * j, 128 * j) for j in range(4)]
            else:
                spans = [(256 * kb + 128 * j, 256 * j + 128 * kb) for kb in range(2) for j in range(2)]
            t = put("T", "tp", [g, *free], *[
                lambda e, d=d, s=s: e.transpose(bk[:, d:d + 128], P_[:, s:s + 128], ident)
                for d, s in spans])
            pp.free(pi_, t)
            ti, T_, tf = pt.take()
            e_ = put("S", "pt", [t, *tf], lambda e: e.activation(T_[:, :], bk[:, :], ACT.Copy))
            tb.free(i, e_)
            B[b][("t", pi, hf)] = (ti, T_, e_)

        def l1_pv(b, pi):
            nonlocal ob
            q = b % 2
            qt, heads = pair(pi)
            tk = [B[b][("t", pi, hf)] for hf in range(2)]
            free = []
            if pi < 2 or pi % 2 == 0:
                ob = obk.take()
                free = ob[2]
            oi, ok = ob[:2]
            ms = []
            for kb in range(qt + 1):
                for hf in range(2):
                    T_ = tk[hf][1]
                    if qt == 0:
                        dst, src = slice(0, 512), slice(0, 512)
                    else:
                        o = 128 * (heads[hf][0] % 4)
                        dst, src = slice(o, o + 256), slice(256 * kb, 256 * kb + 256)
                    ms.append(lambda e, kb=kb, hf=hf, T_=T_, dst=dst, src=src: e.matmul(
                        ok[64 * hf:64 * hf + 64, dst], KV[b % 4][:, kb, 0:64], T_[:, src],
                        start=(kb == 0), stop=(kb == qt), skip_group_check=True))
            m = put("T", "pv", [tk[0][2], tk[1][2], *B[b]["kv"], *free], *ms)
            for hf in range(2):
                pt.free(tk[hf][0], m)
            if pi < 2 or pi % 2 == 1:
                H = heads[0][0] // 8
                i, (hi, lo), fr = ot.take()
                e_ = split([m, *fr], ok[:, :], hi[:, :], lo[:, :], "ot")
                obk.free(oi, *e_)
                B[b][("o", qt, H)] = (i, hi, lo, e_)
            if pi == 5:
                r_kv.free(b, m, B[b]["tk"])

        d_out = []

        def l1_out(b, qt, H):
            i, bk, free = pj.take()
            wk = [t for i2 in range(2) for t in k_w[("o", H, i2)]]
            oi, hi, lo, tk = B[b][("o", qt, H)]
            m = []
            for c in range(4):
                sl = slice(128 * c, 128 * c + 128)
                m += three(bk[:, 0:256], hi[:, sl], lo[:, sl], woe_hi[:, 4 * H + c, :],
                           woe_lo[:, 4 * H + c, :], c == 0, c == 3)
            m = put("T", "o", [*tk, *wk, *free], *m)
            ot.free(oi, m)
            if H == 0:
                B[b][("f", qt)] = put("S", "of", [m, *r_fo[qt].readers(b)], lambda e: e.activation(
                    fo[qt][:, :], bk[:, 0:256], ACT.Copy))
                pj.free(i, B[b][("f", qt)])
                return
            a = put("V", "o", [m, B[b][("f", qt)]], lambda e: e.tensor_tensor(
                fo[qt][:, :], bk[:, 0:256], fo[qt][:, :], ALU.add))
            pj.free(i, a)
            a = put("V", "o", [a, B[b]["w"]], lambda e: e.tensor_tensor(
                fo[qt][:, :], fo[qt][:, :], w1b[b % 3][:, qt, :], ALU.mult))
            f = put("V", "o", [a], lambda e: e.scalar_tensor_tensor(
                fo[qt][:, :], fo[qt][:, :], 0.5, X[:, 2 * b + qt, :], ALU.mult, ALU.add))
            if qt == 1:
                r_w.free(b, f)
            n = 2 * b + qt
            d = put("D", f"out{qt}", [f], lambda e: e.dma_start(out[:, n * D:(n + 1) * D], fo[qt][:, :]))
            r_fo[qt].free(b, d)
            d_out.append(d)

        waiting = []

        def later(f):
            waiting.append(f)

        def start_step():
            now, waiting[:] = list(waiting), []
            for f in now:
                f()

        norm = l0_norm(0)
        drain(norm)
        weights_1(0)
        l0_turn(0, 0)
        l0_turn(0, 1)
        make = iter(())
        threads = []
        for g in range(8 * NC + 2):
            c, hb = g // 8, g % 8
            start_step()
            for th, per in threads:
                for _ in range(per):
                    next(th, None)
            if g == 1:
                weights_2(0)
            if g == 3:
                weights_1(1)
            if g == 4:
                weights_b()
            if g == 5:
                weights_2(1)
            if g < 8 * NC:
                last_up = l0_up(c, hb)
                if g == PLAN["sine"]:
                    make = tables(sines())
                if g == 8:
                    l0_y(0, 1)
                if hb == 0:
                    norm = l0_norm(c + 1) if c + 1 < NC else iter(())
                for _ in range(3 if hb < 5 else 0):
                    next(norm, None)
                if c == 0 and hb <= 5:
                    for _ in range(PLAN["tables"]):
                        next(make, None)
                if hb == (6 if c == 0 else 4):
                    drain(make)
                    k_scan = l0_scan(c)
                if hb == (7 if c == 0 else 6):
                    l0_y(c, 0)
                if hb == 7:
                    xt_r[c % 2] = [last_up, k_scan]
                if hb == 7 and c:
                    l0_y(c, 1)
                if c + 1 < NC:
                    if hb == PLAN["l0"][0]:
                        l0_turn(c + 1, 0)
                    if hb == PLAN["l0"][1]:
                        l0_turn(c + 1, 1)
            if g >= 2:
                d = l0_down((g - 2) // 8, (g - 2) % 8)
                if (g - 2) % 8 == 7:
                    l0_out((g - 2) // 8, d)
            if (c, hb) in fill:
                fill[(c, hb)]()
            e = g - 8 * (NC - 1)
            if e == 0:
                endw += [("wo_T", p.count["wo_T"]), ("wml_V", p.count["wml_V"]),
                         ("wmh_S", p.count["wmh_S"])]
                k_ramp += [put("G", "ra", endw, lambda e, j=j: e.memset(lg[:, 11, :, j:j + 1], 8.0 - j))
                           for j in range(8)]
                threads = [(l1_norm(0), 6)]
            if e == 3:
                l1_turn(0)
                threads = [(l1_norm(1), 4)]
            if e == 5:
                l1_misc(0, 0)
            if e == 6:
                l1_misc(0, 1)
            if e == 7:
                endf.append(("f1_T", p.count["f1_T"]))
                k_tr.append(load("tr", TR[:, :, :].rearrange("p a t -> p (a t)"), rows, endf))
                threads.append((l1_kv(0), 6))
            if e == 8:
                l1_turn(1)
        endm += [(k, p.count[k]) for k in ("f1_T", "f2_T", "hsl_V", "hsh_S")]
        end0 += [x1_k[NC - 1], ("f2_T", p.count["f2_T"]), ("hsl_V", p.count["hsl_V"]),
                 ("hsh_S", p.count["hsh_S"]), ("th0_S", p.count["th0_S"]), ("dx_G", p.count["dx_G"])]
        for th, per in threads:
            drain(th)
        start_step()
        pj = tb = Ring([bank[1], bank[2], bank[7], bank[0], bank[6]])
        tb.readers = [endm, endm, wbank.readers[0], tbank.readers[0], end0]
        gate = l1_gate(0)
        for u in range(PLAN["first"]):
            start_step()
            l1_q(0, u)
            for _ in range(28 // PLAN["first"]):
                next(gate, None)
            if u == PLAN["first"] - 2:
                drain(gate)
        l1_lora(0)
        start_step()
        l1_misc(1, 0)
        l1_misc(1, 1)
        threads = [(l1_kv(1), 3)]

        q_at = {m: u for u, m in enumerate(PLAN["q"])}
        units = [(b, pi, hf) for b in range(NB) for pi in PLAN["order"] for hf in range(2)]
        LAG_T, LAG_V, LAG_O = PLAN["lags"]
        total = len(units)

        def tick():
            for g, per in threads:
                for _ in range(per):
                    next(g, None)

        for n in range(total + LAG_O + 1):
            now, m = n // 12, n % 12
            nxt, far = now + 1, now + 2
            start_step()
            if n < total:
                if m == PLAN["gate"] and nxt < NB:
                    threads.append((l1_gate(nxt), PLAN["rates"][1]))
                if m == PLAN["norm"] and far < NB:
                    threads.append((l1_norm(far), PLAN["rates"][0]))
                if m == PLAN["kv"] and far < NB:
                    threads.append((l1_kv(far), PLAN["rates"][2]))
            tick()
            if n < total:
                l1_s(*units[n])
                tick()
                if n + PLAN["first"] < 8:
                    l1_q(0, n + PLAN["first"])
                if nxt < NB:
                    if m in q_at:
                        l1_q(nxt, q_at[m])
                    if m == PLAN["lora"]:
                        l1_lora(nxt)
                if far < NB:
                    if m == PLAN["turn"]:
                        l1_turn(far)
                    if m == PLAN["misc"][0]:
                        l1_misc(far, 0)
                    if m == PLAN["misc"][1]:
                        l1_misc(far, 1)
            tick()
            if 0 <= n - LAG_T < total:
                l1_pt(*units[n - LAG_T])
            tick()
            if 0 <= n - LAG_V < total and units[n - LAG_V][2] == 1:
                b, pi, hf = units[n - LAG_V]
                l1_pv(b, pi)
            if 0 <= n - LAG_O < total:
                b, pi, hf = units[n - LAG_O]
                if hf == 1 and pi in (0, 1, 3, 5):
                    l1_out(b, int(pi > 1), int(pi in (1, 5)))

        block = ctx.enter_context(nc.Block())

        @block.sync
        def _(e):
            p.run("D", e)
            for k in ("out0_D", "out1_D"):
                e.wait_ge(p.sems[k], p.count[k])

        @block.tensor
        def _(e):
            p.run("T", e)

        @block.vector
        def _(e):
            p.run("V", e)

        @block.scalar
        def _(e):
            p.run("S", e)

        @block.gpsimd
        def _(e):
            p.run("G", e)


def shape_constants():
    c = np.zeros((128, 514), np.float32)
    c[:, 0:128] = np.eye(128)
    i = np.arange(128)
    c[:, 256:384] = np.where(i[None, :] > i[:, None], BIG, 0.0)
    freqs = (np.float32(1.0) / np.power(np.float32(10000.0), np.arange(0, 64, 2, dtype=np.float32)
                                        / np.float32(64))).astype(np.float32)
    t = (np.arange(T, dtype=np.float32)[:, None] * freqs[None, :]).astype(np.float32)
    for q in range(2):
        a = t[128 * q:128 * q + 128].astype(np.float64)
        c[:, 384 + 32 * q:416 + 32 * q] = np.cos(a)
        c[:, 448 + 32 * q:480 + 32 * q] = np.sin(a)
    quad = i // 32
    c[:, 512] = np.where(quad % 2 == 0, 1.0, -1.0)
    c[:, 513] = np.where(quad == 0, 1.0, -1.0)
    return c


def rotation_by_rows():
    i = np.arange(128)
    freqs = (np.float32(1.0) / np.power(np.float32(10000.0), np.arange(0, 64, 2, dtype=np.float32)
                                        / np.float32(64))).astype(np.float32)
    t = (np.arange(T, dtype=np.float32)[:, None] * freqs[None, :]).astype(np.float32)
    a = t.astype(np.float64)[:, i % 32].T
    s = np.where((i // 32) % 2 == 0, -1.0, 1.0)[:, None]
    return np.concatenate([np.cos(a), s * np.sin(a)], axis=1).astype(np.float32)


def kernel(**inputs):
    import concourse.bacc as bacc
    from concourse.bass_utils import run_bass_kernel_spmd

    a = {k: np.asarray(v) for k, v in inputs.items()}

    def chunks(w):
        k = w.shape[0] // 128
        return w.reshape(k, 128, -1).transpose(1, 0, 2).reshape(128, -1)

    wq = a["L1_attn_Wq"].reshape(D, NH, 192)
    kvb = a["L1_attn_Wkv_b"].reshape(64, NH, 256)
    rope = wq[:, :, 128:]
    wkva = a["L1_attn_Wkv_a"]
    bre, bim = a["L0_attn_B_re"].T, a["L0_attn_B_im"].T
    cre, cim = a["L0_attn_C_re"].T, a["L0_attn_C_im"].T
    vecs = np.concatenate([a["L0_attn_D"], a["L0_ffn_proj2_bias"], a["L1_ffn_base_b"],
                           a["L1_ffn_router_b"], a["L1_attn_kv_norm_w"]])
    nuth = np.stack([a["L0_attn_nu_log"], a["L0_attn_theta_log"]], axis=1)
    arrays = {
        "x": a["L0_attn_x"].reshape(NT, 128, D).transpose(1, 0, 2).reshape(128, -1),
        "consts": shape_constants(),
        "rows": rotation_by_rows(),
        "vecs": np.tile(vecs[None, :], (128, 1)),
        "w1t": chunks(a["L0_ffn_proj1"].T).reshape(128, 2, 1024),
        "w2t": chunks(a["L0_ffn_proj2"].T),
        "b1c": a["L0_ffn_proj1_bias"].reshape(8, 128).T,
        "bt": chunks(np.concatenate([bre, bim, bim, bre], axis=1)),
        "ct": np.concatenate([cre, cim, cim, cre], axis=0),
        "nuth": np.tile(nuth, (4, 1)),
        "wqn": wq[:, :, :128].transpose(2, 1, 0).reshape(128, -1),
        "wkbt": kvb[:, :, :128].transpose(2, 1, 0).reshape(128, -1),
        "wqr": chunks(np.concatenate([rope[:, :, 0::2], rope[:, :, 1::2]], axis=2).reshape(D, -1)),
        "wkva": chunks(np.concatenate([wkva[:, :64], wkva[:, 64::2], wkva[:, 65::2]], axis=1)
                       ).reshape(128, 2, 128),
        "wvbt": kvb[:, :, 128:].transpose(2, 1, 0).reshape(128, -1),
        "wo": a["L1_attn_Wo"].reshape(NH, 128, D).transpose(1, 0, 2).reshape(128, -1),
        "baset": chunks(a["L1_ffn_base_w"].T).reshape(128, 2, 256),
        "lorab": a["L1_ffn_lora_B"].reshape(128, D),
        "loraa": chunks(a["L1_ffn_lora_A"].transpose(1, 0, 2).reshape(D, 128)).reshape(128, 2, 128),
        "routert": chunks(a["L1_ffn_router_w"].T).reshape(128, 2, 8),
    }
    nc = bacc.Bacc("TRN2", target_bir_lowering=False, num_devices=1)
    feeds, args = {}, []
    for name, v in arrays.items():
        v = np.ascontiguousarray(v)
        feeds[f"in_{name}"] = v
        args.append(nc.dram_tensor(f"in_{name}", v.shape, mybir.dt.from_np(v.dtype),
                                   kind="ExternalInput").ap())
    args.append(nc.dram_tensor("out_0", (128, NT * D), F32, kind="ExternalOutput").ap())
    build(nc, *args)
    r = run_bass_kernel_spmd(nc, [feeds], core_ids=[0])
    y = r.results[0]["out_0"]
    return y.reshape(128, NT, D).transpose(1, 0, 2).reshape(NB, T, D)
```
